# Optimizing a Trainium2 kernel written in Bass

```python
import numpy as np
import jax
import jax.numpy as jnp

def _softmax(x, axis=-1):
    return jax.nn.softmax(x, axis=axis)

def _gelu(x):
    return jax.nn.gelu(x, approximate=True)

def _silu(x):
    return jax.nn.silu(x)

def _sigmoid(x):
    return jax.nn.sigmoid(x)

def _layernorm(x, axis=-1, eps=1e-05):
    m = jnp.mean(x, axis=axis, keepdims=True)
    v = jnp.var(x, axis=axis, keepdims=True)
    return (x - m) / jnp.sqrt(v + eps)

def _scatter_add(tgt, idx, src, axis=0):
    return tgt.at[idx].add(src)

def _segment_sum(src, seg, n):
    return jax.ops.segment_sum(src, seg, n)
kernel_name = 'mk_flamingo_gated_d1_seqx_r4_bc7f53'

def setup_inputs(seed: int=0):
    np.random.seed(seed)
    _w = jnp.asarray

    def _rec_inputs():
        import jax
        import jax.numpy as jnp
        _rk = jax.random.key(seed)
        x = 7.22e-05 + 1 * jax.random.normal(jax.random.fold_in(_rk, 1), (64, 128, 256), jnp.float32)
        _lenS = 128 - jax.random.randint(jax.random.fold_in(_rk, 7), (64,), 0, max(1, 128 // 4) + 1, jnp.int32)
        _lenS2 = 128 - jax.random.randint(jax.random.fold_in(_rk, 8), (64,), 0, max(1, 128 // 4) + 1, jnp.int32)
        _ctx_1024P = jax.random.normal(jax.random.fold_in(_rk, 11), (64, 16, 256), jnp.float32)
        _ctx_1024c = jax.random.dirichlet(jax.random.fold_in(_rk, 511), 0.3 * jnp.ones((16,), jnp.float32), (64, 128))
        _ctx_1024t = jnp.einsum('bsk,bkd->bsd', _ctx_1024c, _ctx_1024P)
        _ctx_1024t = _ctx_1024t * jax.lax.rsqrt(jnp.mean(jnp.square(_ctx_1024t)) + 1e-12) * 0.953939
        ctx_1024 = 4.13588e-05 + 0.999923 * (_ctx_1024t + 0.3 * jax.random.normal(jax.random.fold_in(_rk, 611), (64, 128, 256), jnp.float32))
        _g = jax.random.normal(jax.random.fold_in(_rk, 9001), (2, 1), jnp.float32)
        _g = jnp.sign(_g) * jnp.maximum(jnp.abs(_g), 1.0) + (_g == 0) * 1.0
        g_xattn = _g[0]
        g_ffn = _g[1]
        return (x, ctx_1024, g_xattn, g_ffn)
    x, ctx_1024, g_xattn, g_ffn = _rec_inputs()

    def _L0_xattn_setup():
        import jax, jax.numpy as jnp
        import numpy as np
        B, S, D, H, W = (2, 1024, 256, 16, 16)
        HD = D // H
        key = jax.random.key(seed)
        ks = jax.random.split(key, 10)
        std = 0.02
        mk_w = lambda k: jax.random.normal(k, (D, D), jnp.float32) * std
        mk_b = lambda k: jax.random.normal(k, (D,), jnp.float32) * std
        return {'query': jax.random.normal(ks[0], (B, S, D), jnp.float32), 'kv': jax.random.normal(ks[1], (B, S, D), jnp.float32), 'Wq': mk_w(ks[2]), 'bq': mk_b(ks[3]), 'Wk': mk_w(ks[4]), 'bk': mk_b(ks[5]), 'Wv': mk_w(ks[6]), 'bv': mk_b(ks[7]), 'Wo': mk_w(ks[8]), 'bo': mk_b(ks[9]), 'is_causal': 1}
    _L0_xattn_all = _L0_xattn_setup()
    _L0_xattn_in = {k: v for k, v in _L0_xattn_all.items() if k in ('Wq', 'bq', 'Wk', 'bk', 'Wv', 'bv', 'Wo', 'bo')}
    del _L0_xattn_all

    def _L0_ffn_setup():
        import jax, jax.numpy as jnp
        import numpy as np
        TOP_K = 2
        CAP_FACTOR = 1.25
        MIN_CAPACITY = 4
        key = jax.random.key(seed)
        k1, k2, k3, k4 = jax.random.split(key, 4)
        B, T, C, E = (8, 512, 256, 8)
        x = jax.random.normal(k1, (B, T, C), dtype=jnp.float32)
        w_g = jax.random.normal(k2, (E, C), dtype=jnp.float32) * 0.02
        c_fc = jax.random.normal(k3, (E, C, 4 * C), dtype=jnp.float32) * 0.02
        c_proj = jax.random.normal(k4, (E, 4 * C, C), dtype=jnp.float32) * 0.02
        return {'x': x, 'w_g': w_g, 'c_fc': c_fc, 'c_proj': c_proj}
    _L0_ffn_all = _L0_ffn_setup()
    _L0_ffn_in = {k: v for k, v in _L0_ffn_all.items() if k in ('w_g', 'c_fc', 'c_proj')}
    del _L0_ffn_all
    return {'x': x, 'ctx_1024': ctx_1024, 'g_xattn': g_xattn, 'g_ffn': g_ffn, 'L0_xattn_Wq': _L0_xattn_in['Wq'], 'L0_xattn_bq': _L0_xattn_in['bq'], 'L0_xattn_Wk': _L0_xattn_in['Wk'], 'L0_xattn_bk': _L0_xattn_in['bk'], 'L0_xattn_Wv': _L0_xattn_in['Wv'], 'L0_xattn_bv': _L0_xattn_in['bv'], 'L0_xattn_Wo': _L0_xattn_in['Wo'], 'L0_xattn_bo': _L0_xattn_in['bo'], 'L0_ffn_w_g': _L0_ffn_in['w_g'], 'L0_ffn_c_fc': _L0_ffn_in['c_fc'], 'L0_ffn_c_proj': _L0_ffn_in['c_proj']}

def reference(x, ctx_1024, g_xattn, g_ffn, L0_xattn_Wq, L0_xattn_bq, L0_xattn_Wk, L0_xattn_bk, L0_xattn_Wv, L0_xattn_bv, L0_xattn_Wo, L0_xattn_bo, L0_ffn_w_g, L0_ffn_c_fc, L0_ffn_c_proj):
    import jax
    import jax.numpy as jnp

    def _L0_xattn_ref(query, kv, Wq, bq, Wk, bk, Wv, bv, Wo, bo, is_causal):
        import jax, jax.numpy as jnp
        import numpy as np
        B, S, D, H, W = (2, 1024, 256, 16, 16)
        HD = D // H
        b, s, d = query.shape

        def split_heads(x):
            return x.reshape(b, s, H, HD).transpose(0, 2, 1, 3)
        Q = split_heads(query @ Wq.T + bq)
        K = split_heads(kv @ Wk.T + bk)
        V = split_heads(kv @ Wv.T + bv)
        pad = W - 1
        Kp = jnp.pad(K, ((0, 0), (0, 0), (pad, 0), (0, 0)))
        Vp = jnp.pad(V, ((0, 0), (0, 0), (pad, 0), (0, 0)))
        idx = jnp.arange(s)[:, None] + jnp.arange(W)[None, :]
        Kw = Kp[:, :, idx]
        Vw = Vp[:, :, idx]
        scores = jnp.einsum('bhsd,bhswd->bhsw', Q, Kw) / np.sqrt(HD).astype(np.float32)
        if is_causal:
            mask = jnp.arange(W)[None, :] <= jnp.arange(s)[:, None]
            scores = jnp.where(mask[None, None], scores, -jnp.inf)
        attn = jax.nn.softmax(scores, axis=-1)
        out = jnp.einsum('bhsw,bhswd->bhsd', attn, Vw)
        out = out.transpose(0, 2, 1, 3).reshape(b, s, d)
        return out @ Wo.T + bo

    def _L0_ffn_ref(x, w_g, c_fc, c_proj):
        import jax, jax.numpy as jnp
        import numpy as np
        TOP_K = 2
        CAP_FACTOR = 1.25
        MIN_CAPACITY = 4
        B, T, C = x.shape
        E = w_g.shape[0]
        N = B * T
        capacity = max(MIN_CAPACITY, int(CAP_FACTOR * N * TOP_K / E))
        xf = x.reshape(N, C)
        logits = xf @ w_g.T
        top_logits, top_idx = jax.lax.top_k(logits, TOP_K)
        router_probs = jax.nn.softmax(top_logits, axis=-1)
        oh = jax.nn.one_hot(top_idx, E, dtype=jnp.int32)
        oh_t = oh.transpose(1, 0, 2).reshape(TOP_K * N, E)
        pos = jnp.cumsum(oh_t, axis=0).reshape(TOP_K, N, E).transpose(1, 0, 2)
        rank = jnp.sum((pos - 1) * oh, axis=-1)
        valid = rank < capacity
        probs_masked = router_probs * valid.astype(router_probs.dtype)
        rank_c = jnp.clip(rank, 0, capacity - 1)
        contrib = xf[:, None, :] * valid[..., None].astype(xf.dtype)
        buf = jnp.zeros((E, capacity, C), dtype=xf.dtype).at[top_idx, rank_c].add(contrib)
        h = jnp.einsum('ecd,edf->ecf', buf, c_fc)
        h = jnp.square(jax.nn.relu(h))
        expert_out = jnp.einsum('ecf,efd->ecd', h, c_proj)
        gathered = expert_out[top_idx, rank_c]
        out = jnp.sum(gathered * probs_masked[..., None], axis=1)
        return out.reshape(B, T, C)
    x = x + jnp.tanh(g_xattn[0]) * _L0_xattn_ref(_layernorm(x, axis=-1), ctx_1024, L0_xattn_Wq, L0_xattn_bq, L0_xattn_Wk, L0_xattn_bk, L0_xattn_Wv, L0_xattn_bv, L0_xattn_Wo, L0_xattn_bo, 1)
    x = x + jnp.tanh(g_ffn[0]) * _L0_ffn_ref(_layernorm(x, axis=-1), L0_ffn_w_g, L0_ffn_c_fc, L0_ffn_c_proj)
    return x

_drawn_inputs = setup_inputs


def setup_inputs(seed=0):
    import zlib

    import numpy as np

    out = dict(_drawn_inputs(seed))
    spreads = {}
    factors = {'L0_xattn_Wq': 8.0,
     'L0_xattn_bq': 63.064,
     'L0_xattn_Wk': 8.0,
     'L0_xattn_bk': 64.0,
     'L0_xattn_bv': 8.0,
     'L0_xattn_bo': 3.432}
    for name, (base, spread) in spreads.items():
        noise = np.random.default_rng([zlib.crc32(name.encode()), seed]).standard_normal(out[name].shape)
        drawn = base * np.exp(spread * noise) if base else spread * noise
        out[name] = jnp.asarray(drawn.astype(out[name].dtype))
    for name, factor in factors.items():
        out[name] = (out[name] * factor).astype(out[name].dtype)
    return out
```

```python
from contextlib import ExitStack

import concourse.bass as bass
from concourse import mybir

F32 = mybir.dt.float32
F32R = mybir.dt.float32r
F16 = mybir.dt.float16
BF16 = mybir.dt.bfloat16
I32 = mybir.dt.int32
ALU = mybir.AluOpType
ACT = mybir.ActivationFunctionType
AX = mybir.AxisListType.X

P = 128
B, S, D = 64, 128, 256
N = B * S
H, HD, W = 16, 16, 16
DC = D // P
GB = 4
GT = GB * S
NGROUP = B // GB
V4 = 4
QB = 32
KW = QB + W
SLOT = 64
KPAD = 16
KS = KPAD + S
EPS = 1e-5
E, TOPK, F = 8, 2, 1024
CAP = max(4, int(1.25 * N * TOPK / E))
NSLOT = E * CAP
ST = NSLOT // P
STE = CAP // P
MT = 512
MTE = CAP // MT
SUB = MT // P
FC = F // P
TRASH = CAP
SPARE = 2 * SUB
NEG = -1.0e30

C_ID, C_BAND, C_VM, C_TRI, C_ONE = 0, 128, 128 + 512, 128 + 512 + 4, 128 + 512 + 4 + 128
C_I128 = C_ONE + 128
C_I160 = C_I128 + 128
C_TOK = C_I160 + ST
C_E8 = C_TOK + TOPK * B
C_PB = C_E8 + E
C_END = C_PB + ST + SPARE


def cnt(k, r, per=1):
    return k * (8 * per) + (r + 1) * per


def gcnt(k, r, per=1):
    return k * (2 * per) + (r // 4 + 1) * per


def build_kernel(nc, x, ctxT, gx, gf, wqT, bq, wkT, bk, wvT, bv, woP, bo, wgT, w1, w2, consts, out):
    ctx = ExitStack()
    with ctx:
        def sb(name, shape, dt=F32):
            return ctx.enter_context(nc.sbuf_tensor(name, shape, dt))

        def sem(name):
            return ctx.enter_context(nc.semaphore(name))

        xn_rows = nc.dram_tensor("xn_rows", [N + TRASH, D], F32, kind="Internal").ap()

        cst = sb("cst", [P, C_END])
        ident = cst[:, C_ID:C_ID + P]
        vmask = cst[:, C_VM:C_VM + V4]
        tok_id = cst[:, C_TOK:C_TOK + TOPK * B]
        e_iota = cst[:, C_E8:C_E8 + E]
        identb = sb("identb", [P, P], BF16)
        bandb = sb("bandb", [P, 512], BF16)
        gates = sb("gates", [P, 2])
        gtanh = sb("gtanh", [P, 2])

        logits = sb("logits", [P, B, E])

        att = ctx.enter_context(ExitStack())

        def sa(name, shape, dt=F32):
            return att.enter_context(nc.sbuf_tensor(name, shape, dt))

        def pa(name, shape, dt=F32):
            return att.enter_context(nc.psum_tensor(name, shape, dt))

        ps_g = pa("ps_g", [P, 2, 512])
        ps_s = pa("ps_s", [P, 2, 512])
        ps_p = pa("ps_p", [P, 2, 512])
        ps_o = pa("ps_o", [P, 512])
        ps_m = pa("ps_m", [P, 512])

        w_raw = sa("w_raw", [P, 3, DC, D])
        w_hl = sa("w_hl", [P, 3, 2, DC, D], F32R)
        wo_sb = sa("wo_sb", [64, V4, D])
        wg_sb = sa("wg_sb", [P, DC, E])
        bqk = sa("bqk", [P, 2, DC])
        bv_raw = sa("bv_raw", [1, D])
        bv_hl = sa("bv_hl", [1, 2, D], F32R)
        one_h = sa("one_h", [P, 1], F16)
        one_r = sa("one_r", [1, P], F32R)
        gbo = sa("gbo", [P, D])

        xg = sa("xg", [P, 2, GB, D])
        cg = sa("cg", [P, 2, DC, GT])
        c_hl = sa("c_hl", [P, 2, DC, GT], F32R)
        xn = sa("xn", [P, GB, D])
        xT_hl = sa("xT_hl", [P, 2, DC, GT], F32R)
        stat = sa("stat", [P, GB, 6])
        mv = sa("mv", [P, GB, 2])
        rstd = sa("rstd", [P, GB])
        xb = sa("xb", [P, 2, GB, D])
        q_hl = sa("q_hl", [P, 2, DC, GT], F16)
        qd = sa("qd", [P, 2, 2, DC, GT // QB, V4, QB], F16)
        kT = sa("kT", [P, 2, 2, DC, GB, KS], F16)
        vw = sa("vw", [P, 2, 2, 2, GB, D], F16)

        mx = sa("mx", [P, 16])
        es = sa("es", [P, 2, 16, SLOT])
        rinv = sa("rinv", [P, 2, 8])
        pT = sa("pT", [P, 2, 8, P], F16)
        osb = sa("osb", [P, 16, HD])
        oT = sa("oT", [64, V4, 4, QB])
        x1 = sa("x1", [P, 2, D])
        stat2 = sa("stat2", [P, 6])
        mv2 = sa("mv2", [P, 2])
        rstd2 = sa("rstd2", [P, 1])
        xn2 = sa("xn2", [P, 2, D])
        x2T = sa("x2T", [P, DC, P])
        var_e = sa("var_e", [P, GB])
        var_e2 = sa("var_e2", [P, 1])
        mhalf = sa("mhalf", [P, GB])
        eps_t = sa("eps_t", [P, GB])
        zrow = sa("zrow", [P, D])

        const_in, weights_in, bias_in = sem("const_in"), sem("weights_in"), sem("bias_in")
        init_dve, init_pool, init_act = sem("init_dve"), sem("init_pool"), sem("init_act")
        x_in = [sem(f"x_in{i}") for i in range(2)]
        c_in = [sem(f"c_in{i}") for i in range(2)]
        dve_ln = sem("dve_ln")
        xn_done, xT_ps, xT_hi, xT_lo = sem("xn_done"), sem("xT_ps"), sem("xT_hi"), sem("xT_lo")
        c_hi, c_lo, xb_done = sem("c_hi"), sem("c_lo"), sem("xb_done")
        q_ps, q_hi, q_lo, qd_done = sem("q_ps"), sem("q_hi"), sem("q_lo"), sem("qd_done")
        k_ps, k_hi, k_lo = sem("k_ps"), sem("k_hi"), sem("k_lo")
        v_ps, v_hi, v_lo = sem("v_ps"), sem("v_hi"), sem("v_lo")
        v_shift = [sem(f"v_shift{i}") for i in range(2)]
        s_ps, mx_done, s_sub, e_done = sem("s_ps"), sem("mx_done"), sem("s_sub"), sem("e_done")
        pT_ps, pT_hi, pT_lo, rinv_done = sem("pT_ps"), sem("pT_hi"), sem("pT_lo"), sem("rinv_done")
        o_ps, o_done, oT_ps, oT_done = sem("o_ps"), sem("o_done"), sem("oT_ps"), sem("oT_done")
        y_ps, x1_done, st2_done, xn2_done = sem("y_ps"), sem("x1_done"), sem("st2_done"), sem("xn2_done")
        x2T_ps, x2T_done, lg_ps, lg_done = sem("x2T_ps"), sem("x2T_done"), sem("lg_ps"), sem("lg_done")
        x1_out = [sem(f"x1_out{i}") for i in range(2)]
        xn2_out = [sem(f"xn2_out{i}") for i in range(2)]
        zero_out = sem("zero_out")
        var_done, var2_done = sem("var_done"), sem("var2_done")
        rstd_done, rstd2_done = sem("rstd_done"), sem("rstd2_done")

        x_g = x.rearrange("(g b s) d -> g s b d", b=GB, s=S)
        c_g = ctxT.rearrange("(c p) (g t) -> g p c t", p=P, t=GT)

        def isint(k):
            return isinstance(k, int)

        def valid(k, r, lag):
            return not isint(k) or (8 * k + r - lag >= 0 and 8 * k + r - lag < B)

        LAGS = 3

        def schedule(eng, step):
            for r in range(4):
                step(0, r)
            with eng.Fori(0, (NGROUP - 2) // 2) as k:
                for r in range(4, 12):
                    step(k, r)
            for r in range(4, 8 + LAGS):
                step((NGROUP - 2) // 2, r)

        def has_next(k, r):
            return not isint(k) or 8 * k + r < B - 4

        block = att.enter_context(nc.Block())

        @block.sync
        def _(sp):
            sp.dma_start(cst[:, :], consts).then_inc(const_in, 16)
            sp.dma_start(gates[:, 0:1], gx.rearrange("(a n) -> a n", a=1).broadcast_to([P, 1])).then_inc(bias_in, 16)
            sp.dma_start(gates[:, 1:2], gf.rearrange("(a n) -> a n", a=1).broadcast_to([P, 1])).then_inc(bias_in, 16)
            sp.dma_start(gbo[:, :], bo.rearrange("(a n) -> a n", a=1).broadcast_to([P, D])).then_inc(bias_in, 16)
            sp.dma_start(bqk[:, 0, :], bq).then_inc(bias_in, 16)
            sp.dma_start(bqk[:, 1, :], bk).then_inc(bias_in, 16)
            sp.dma_start(bv_raw[:, :], bv.rearrange("(a n) -> a n", a=1)).then_inc(bias_in, 16)
            sp.dma_start(xg[:, 0], x_g[0]).then_inc(x_in[0], 16)
            for n, w in enumerate((wqT, wkT, wvT)):
                sp.dma_start(w_raw[:, n], w.rearrange("(c p) n -> p c n", p=P)).then_inc(weights_in, 16)
            sp.dma_start(cg[:, 0], c_g[0]).then_inc(c_in[0], 16)
            sp.dma_start(wo_sb[:, :, :], woP).then_inc(weights_in, 16)
            sp.dma_start(wg_sb[:, :, :], wgT.rearrange("(c p) e -> p c e", p=P)).then_inc(weights_in, 16)
            sp.dma_start(xg[:, 1], x_g[1]).then_inc(x_in[1], 16)
            sp.dma_start(cg[:, 1], c_g[1]).then_inc(c_in[1], 16)
            sp.wait_ge(init_pool, 1)
            for rows in (xn_rows, out):
                sp.dma_start(rows[N:N + TRASH, :].rearrange("(t p) d -> p t d", p=P),
                             zrow[:, :].unsqueeze(1).to_broadcast([P, STE, D])).then_inc(zero_out, 16)

            def shift_v(k, r):
                g = (r // 4) % 2
                sp.wait_ge(v_hi, gcnt(k, r))
                sp.wait_ge(v_lo, gcnt(k, r))
                sp.dma_start(vw[QB:P, g, 0], vw[0:P - QB, g, 1]).then_inc(v_shift[g], 16)

            sp.wait_ge(init_dve, 3)
            shift_v(0, 0)

            def step(k, r):
                g = (r // 4) % 2
                if r % 4 == 0 and (not isint(k) or 8 * k + r < B - 8):
                    nxt = (2 * k + r // 4 + 2) % NGROUP
                    sp.wait_ge(xn_done, gcnt(k, r))
                    sp.wait_ge(xb_done, gcnt(k, r))
                    sp.dma_start(xg[:, g], x_g[nxt]).then_inc(x_in[g], 16)
                    sp.wait_ge(c_hi, gcnt(k, r))
                    sp.wait_ge(c_lo, gcnt(k, r))
                    sp.dma_start(cg[:, g], c_g[nxt]).then_inc(c_in[g], 16)
                if valid(k, r, 2):
                    b = r % 2
                    row = (8 * k + r - 2) * S
                    sp.wait_ge(x1_done, cnt(k, r - 2))
                    sp.dma_start(out[bass.ds(row, S), :], x1[:, b]).then_inc(x1_out[b], 16)
                    sp.wait_ge(xn2_done, cnt(k, r - 2))
                    sp.dma_start(xn_rows[bass.ds(row, S), :], xn2[:, b]).then_inc(xn2_out[b], 16)
                if r % 4 == 3 and has_next(k, r):
                    shift_v(k, r + 4)

            schedule(sp, step)
            for b in range(2):
                sp.wait_ge(x1_out[b], 16 * (B // 2))
                sp.wait_ge(xn2_out[b], 16 * (B // 2))
            sp.wait_ge(zero_out, 32)
            for g in range(2):
                sp.wait_ge(x_in[g], 16 * 8)
                sp.wait_ge(c_in[g], 16 * 8)

        @block.gpsimd
        def _(pool):
            pool.memset(zrow[:, :], 0.0).then_inc(init_pool, 1)
            pool.memset(mhalf[:, :], -0.5)
            pool.memset(eps_t[:, :], EPS)
            pool.memset(es[:, :, :, :], 0.0).then_inc(init_pool, 1)
            pool.wait_ge(init_act, 1)
            pool.wait_ge(bias_in, 16 * 6)
            pool.tensor_scalar(gbo[:, :], gbo[:, :], gtanh[:, 0:1], None, ALU.mult).then_inc(init_pool, 1)
            pool.wait_ge(init_pool, 3)

            def split_c(k, r):
                g = (r // 4) % 2
                pool.wait_ge(c_hi, gcnt(k, r))
                pool.tensor_tensor(c_hl[:, 1], cg[:, g], c_hl[:, 0].bitcast(F32), ALU.subtract).then_inc(c_lo, 1)

            def add_xb(k, r):
                g = (r // 4) % 2
                pool.wait_ge(x_in[g], 16 * (k + r // 8 + 1))
                pool.tensor_tensor(xb[:, g], xg[:, g], gbo[:, :].unsqueeze(1).to_broadcast([P, GB, D]), ALU.add).then_inc(xb_done, 1)

            def rstd_in(k, r):
                pool.wait_ge(dve_ln, gcnt(k, r, 2))
                pool.tensor_tensor(var_e[:, :], mv[:, :, 1], eps_t[:, :], ALU.add).then_inc(var_done, 1)
                pool.wait_ge(var_done, gcnt(k, r))
                pool.tensor_tensor(rstd[:, :], var_e[:, :], mhalf[:, 0:GB], ALU.pow).then_inc(rstd_done, 1)

            rstd_in(0, 0)
            split_c(0, 0)
            add_xb(0, 0)
            rstd_in(0, 4)

            def step(k, r):
                if valid(k, r, 2):
                    pool.wait_ge(st2_done, cnt(k, r - 2, 2))
                    pool.tensor_tensor(var_e2[:, :], mv2[:, 1:2], eps_t[:, 0:1], ALU.add).then_inc(var2_done, 1)
                    pool.wait_ge(var2_done, cnt(k, r - 2))
                    pool.tensor_tensor(rstd2[:, :], var_e2[:, :], mhalf[:, 0:1], ALU.pow).then_inc(rstd2_done, 1)
                if has_next(k, r):
                    if r % 4 == 0:
                        split_c(k, r + 4)
                    if r % 4 == 2:
                        if not isint(k) or r >= 4:
                            pool.wait_ge(x1_done, cnt(k, r - 3))
                        add_xb(k, r + 4)
                if r % 4 == 3 and has_next(k, r) and (not isint(k) or 8 * k + r < B - 8):
                    rstd_in(k, r + 5)

            schedule(pool, step)

        @block.scalar
        def _(act):
            act.wait_ge(bias_in, 16 * 6)
            act.activation(gtanh[:, :], gates[:, :], ACT.Tanh).then_inc(init_act, 1)
            act.wait_ge(weights_in, 16 * 5)
            act.activation(w_hl[:, :, 0], w_raw[:, :], ACT.Copy).then_inc(init_act, 1)
            act.activation(bv_hl[:, 0], bv_raw[:, :], ACT.Copy).then_inc(init_act, 1)

            def ctx_hi(k, r):
                g = (r // 4) % 2
                act.wait_ge(c_in[g], 16 * (k + r // 8 + 1))
                if not isint(k) or r >= 4:
                    act.wait_ge(v_ps, gcnt(k, r - 4))
                act.activation(c_hl[:, 0], cg[:, g], ACT.Copy).then_inc(c_hi, 1)

            def prep(k, r, part):
                g = (r // 4) % 2
                if part == 0:
                    act.wait_ge(xT_ps, gcnt(k, r))
                    act.activation(xT_hl[:, 0], ps_g[:, :, :], ACT.Copy).then_inc(xT_hi, 1)
                if part == 1:
                    act.wait_ge(q_ps, gcnt(k, r))
                    if not isint(k) or r >= 4:
                        act.wait_ge(qd_done, gcnt(k, r - 4))
                    for c in range(DC):
                        i = act.activation(q_hl[:, 0, c], ps_g[:, c], ACT.Identity, bias=bqk[:, 0, c:c + 1])
                    i.then_inc(q_hi, 1)
                if part == 2:
                    act.wait_ge(k_ps, gcnt(k, r))
                    if k_first(k, r):
                        act.wait_ge(init_dve, 3)
                    for c in range(DC):
                        i = act.activation(kT[:, g, 0, c, :, KPAD:KS], ps_g[:, c].rearrange("p (b s) -> p b s", b=GB),
                                           ACT.Identity, bias=bqk[:, 1, c:c + 1])
                    i.then_inc(k_hi, 1)
                if part == 3:
                    act.wait_ge(v_ps, gcnt(k, r))
                    act.activation(vw[:, g, 1, 0], ps_g[:, :, :].rearrange("p a (b d) -> p (a b) d", d=D), ACT.Copy).then_inc(v_hi, 1)

            def k_first(k, r):
                return isint(k) and k == 0 and r < 8

            ctx_hi(0, 0)
            for part in range(4):
                prep(0, 0, part)

            def step(k, r):
                if r % 4 == 0 and has_next(k, r):
                    ctx_hi(k, r + 4)
                if valid(k, r, 0):
                    act.wait_ge(s_sub, cnt(k, r))
                    win = es[:, r % 2, :, SLOT - KW:SLOT]
                    act.activation(win, win, ACT.Exp, scale=HD ** -0.5).then_inc(e_done, 1)
                if has_next(k, r):
                    prep(k, r + 4, r % 4)
                if valid(k, r, 1):
                    act.wait_ge(oT_ps, cnt(k, r - 1))
                    act.activation(oT[:, :, :, :], ps_o[0:64, :].rearrange("p (q v s) -> p v q s", q=4, v=V4), ACT.Copy).then_inc(oT_done, 1)
                if valid(k, r, 2):
                    act.wait_ge(x2T_ps, cnt(k, r - 2))
                    act.activation(x2T[:, :, :], ps_m[:, D:2 * D].rearrange("p (c n) -> p c n", c=DC), ACT.Copy).then_inc(x2T_done, 1)
                if valid(k, r, 0):
                    act.wait_ge(pT_ps, cnt(k, r))
                    act.activation(pT[:, 0], ps_p[:, :, :].rearrange("p a (b n) -> p (a b) n", n=P), ACT.Copy).then_inc(pT_hi, 1)

            schedule(act, step)

        @block.tensor
        def _(pe):
            def prep(k, r, part):
                g = (r // 4) % 2
                if part == 0:
                    pe.wait_ge(xn_done, gcnt(k, r))
                    if not isint(k) or r >= 4:
                        pe.wait_ge(v_hi, gcnt(k, r - 4))
                        pe.wait_ge(v_lo, gcnt(k, r - 4))
                    for c in range(DC):
                        for b in range(GB):
                            i = pe.transpose(ps_g[:, c, b * P:(b + 1) * P], xn[:, b, c * P:(c + 1) * P], ident)
                    i.then_inc(xT_ps, 1)
                if part in (1, 2):
                    src = xT_hl if part == 1 else c_hl
                    if part == 1:
                        pe.wait_ge(xT_hi, gcnt(k, r))
                        pe.wait_ge(xT_lo, gcnt(k, r))
                    else:
                        pe.wait_ge(c_hi, gcnt(k, r))
                        pe.wait_ge(c_lo, gcnt(k, r))
                        pe.wait_ge(q_hi, gcnt(k, r))
                        pe.wait_ge(q_lo, gcnt(k, r))
                    for co in range(DC):
                        n = 0
                        for ci in range(DC):
                            for a, b in ((0, 0), (0, 1), (1, 0)):
                                i = pe.matmul(ps_g[:, co], w_hl[:, part - 1, a, ci, co * P:(co + 1) * P], src[:, b, ci],
                                              start=(n == 0), stop=(n == 3 * DC - 1))
                                n += 1
                    i.then_inc(q_ps if part == 1 else k_ps, 1)
                if part == 3:
                    pe.wait_ge(k_hi, gcnt(k, r))
                    pe.wait_ge(k_lo, gcnt(k, r))
                    for b in range(GB):
                        dst = ps_g[:, b // 2, (b % 2) * D:(b % 2 + 1) * D]
                        for hl in range(2):
                            pe.matmul(dst, one_r[:, :], bv_hl[:, hl], start=(hl == 0), stop=False)
                        n = 0
                        for ci in range(DC):
                            for a, w in ((0, 0), (0, 1), (1, 0)):
                                i = pe.matmul(dst, c_hl[:, a, ci, b * P:(b + 1) * P], w_hl[:, 2, w, ci],
                                              start=False, stop=(n == 3 * DC - 1))
                                n += 1
                    i.then_inc(v_ps, 1)

            pe.wait_ge(const_in, 16)
            pe.wait_ge(init_act, 3)
            pe.wait_ge(init_dve, 3)
            for part in range(4):
                prep(0, 0, part)

            def scores(k, r):
                g, b = (r // 4) % 2, r % 4
                if b == 0:
                    pe.wait_ge(qd_done, gcnt(k, r))
                    pe.wait_ge(k_hi, gcnt(k, r))
                    pe.wait_ge(k_lo, gcnt(k, r))
                if not isint(k) or r >= 1:
                    pe.wait_ge(rinv_done, cnt(k, r - 1))
                if not isint(k) or r >= 3:
                    pe.wait_ge(lg_done, cnt(k, r - 3))
                for half in range(2):
                    rows = slice(64 * half, 64 * half + 64)
                    bank = ps_s[:, half].rearrange("p (n s) -> p n s", s=SLOT)
                    pe.matmul(bank[:, :, 0:KW], identb[:, :], bandb[:, :].rearrange("p (n s) -> p n s", s=SLOT)[:, :, 0:KW],
                              start=True, stop=False)
                    for par in range(2):
                        for c in range(DC):
                            for j in range(2):
                                qb = 2 * j + par
                                for a, w in ((0, 0), (0, 1), (1, 0)):
                                    blk = b * 4 + qb
                                    i = pe.matmul(bank[:, par * 4 + c * 2 + j, 0:KW], qd[rows, g, a, c, blk].rearrange("p v s -> p (v s)"),
                                                  kT[rows, g, w, c, b, qb * QB:qb * QB + KW],
                                                  start=False, stop=(par == 1 and c == 1 and j == 1 and a == 1))
                i.then_inc(s_ps, 1)

            def turn_p(k, r):
                pe.wait_ge(e_done, cnt(k, r))
                if not isint(k) or r >= 1:
                    pe.wait_ge(o_done, cnt(k, r - 1))
                for n in range(8):
                    i = pe.transpose(ps_p[:, n // 4, (n % 4) * P:(n % 4 + 1) * P],
                                     es[:, r % 2, 2 * n:2 * n + 2].rearrange("p a s -> p (a s)"), ident)
                i.then_inc(pT_ps, 1)

            def turn_o(k, r):
                o = osb[:, :, :].rearrange("p (j a h c) d -> p j a (h c d)", j=2, h=2, a=2)
                for qb in range(4):
                    i = pe.transpose(ps_o[0:64, qb * P:(qb + 1) * P], o[:, qb // 2, qb % 2], ident)
                i.then_inc(oT_ps, 1)

            def heads_out(k, r):
                g, b = (r // 4) % 2, r % 4
                if b == 0:
                    pe.wait_ge(v_shift[g], 16 * (k + r // 8 + 1))
                pe.wait_ge(pT_hi, cnt(k, r))
                pe.wait_ge(pT_lo, cnt(k, r))
                for j in range(2):
                    rows = slice(64 * j, 64 * j + 64)
                    for n in range(8):
                        half, par, c = n // 4, (n // 2) % 2, n % 2
                        d0 = c * P + half * 64
                        m = par * 4 + half * 2 + c
                        for a, w in ((0, 0), (0, 1), (1, 0)):
                            pe.matmul(ps_p[:, j, m * 64:(m + 1) * 64], pT[rows, a, n], vw[rows, g, par, w, b, d0:d0 + 64],
                                      start=(a == 0 and w == 0), stop=(a == 1))
                        for a in range(2):
                            i = pe.matmul(ps_s[:, j, m * SLOT + KW:m * SLOT + KW + 1], pT[rows, a, n], one_h[rows, :],
                                          start=(a == 0), stop=(a == 1))
                i.then_inc(o_ps, 1)

            def project_o(k, r):
                pe.wait_ge(oT_done, cnt(k, r))
                if not isint(k) or r >= 1:
                    pe.wait_ge(x2T_done, cnt(k, r - 1))
                for v in range(V4):
                    i = pe.matmul(ps_m[:, 0:D], oT[:, v].rearrange("p q s -> p (q s)"), wo_sb[:, v], start=(v == 0), stop=(v == V4 - 1))
                i.then_inc(y_ps, 1)

            def turn_x2(k, r):
                for c in range(DC):
                    i = pe.transpose(ps_m[:, D + c * P:D + (c + 1) * P], xn2[:, r % 2, c * P:(c + 1) * P], ident)
                i.then_inc(x2T_ps, 1)

            def route(k, r):
                pe.wait_ge(x2T_done, cnt(k, r))
                if isint(k) and 8 * k + r == B - 2:
                    pe.wait_ge(rinv_done, B)
                if not isint(k) or r >= 1:
                    pe.wait_ge(lg_done, cnt(k, r - 1))
                for c in range(DC):
                    i = pe.matmul(ps_s[:, 0, SLOT - E:SLOT], x2T[:, c], wg_sb[:, c], start=(c == 0), stop=(c == DC - 1))
                i.then_inc(lg_ps, 1)

            def step(k, r):
                if valid(k, r, 0):
                    scores(k, r)
                if valid(k, r, 1):
                    pe.wait_ge(o_done, cnt(k, r - 1))
                    if valid(k, r, 2):
                        pe.wait_ge(oT_done, cnt(k, r - 2))
                if has_next(k, r):
                    prep(k, r + 4, r % 4)
                if valid(k, r, 1):
                    turn_o(k, r - 1)
                if valid(k, r, 2):
                    pe.wait_ge(xn2_done, cnt(k, r - 2))
                    turn_x2(k, r - 2)
                if valid(k, r, 0):
                    turn_p(k, r)
                if valid(k, r, 1):
                    project_o(k, r - 1)
                if valid(k, r, 2):
                    route(k, r - 2)
                if valid(k, r, 0):
                    heads_out(k, r)

            schedule(pe, step)

        @block.vector
        def _(dve):
            dve.memset(one_r[:, :].bitcast(F32), 1.0)
            dve.memset(one_h[:, :], 1.0)
            for g in range(2):
                dve.memset(kT[:, g, :, :, :, 0:KPAD].rearrange("p a c b s -> p (a c b) s"), 0.0)
                dve.memset(vw[0:QB, g, 0].rearrange("p a b d -> p (a b d)"), 0.0)
            dve.wait_ge(const_in, 16)
            dve.tensor_copy(identb[:, :], ident)
            dve.tensor_copy(bandb[:, :], cst[:, C_BAND:C_BAND + 512]).then_inc(init_dve, 1)
            dve.wait_ge(init_act, 3)
            dve.tensor_tensor(w_hl[:, :, 1], w_raw[:, :], w_hl[:, :, 0].bitcast(F32), ALU.subtract).then_inc(init_dve, 1)
            dve.tensor_tensor(bv_hl[:, 1], bv_raw[:, :], bv_hl[:, 0].bitcast(F32), ALU.subtract).then_inc(init_dve, 1)

            def norm_in(k, r):
                g = (r // 4) % 2
                dve.wait_ge(x_in[g], 16 * (k + r // 8 + 1))
                for b in range(GB):
                    i = dve.bn_stats(stat[:, b], xg[:, g, b])
                i.then_inc(dve_ln, 1)

            def aggregate_in(k, r):
                for b in range(GB):
                    i = dve.bn_aggr(mv[:, b], stat[:, b])
                i.then_inc(dve_ln, 1)

            def norm_out(k, r):
                g = (r // 4) % 2
                dve.wait_ge(rstd_done, gcnt(k, r))
                if not isint(k) or r >= 4:
                    dve.wait_ge(xT_ps, gcnt(k, r - 4))
                for b in range(GB):
                    i = dve.tensor_scalar(xn[:, b], xg[:, g, b], mv[:, b, 0:1], rstd[:, b:b + 1], ALU.subtract, ALU.mult)
                i.then_inc(xn_done, 1)

            def heads_of_q(k, r):
                g = (r // 4) % 2
                dve.wait_ge(q_lo, gcnt(k, r))
                for v in range(V4):
                    i = dve.tensor_scalar(qd[:, g, :, :, :, v].rearrange("p a c n s -> p (a c n) s"), q_hl[:, :, :, :].rearrange("p a c (n s) -> p (a c n) s", s=QB),
                                          vmask[:, v:v + 1], None, ALU.mult)
                i.then_inc(qd_done, 1)

            def prep(k, r, part):
                g = (r // 4) % 2
                if part == 0:
                    dve.wait_ge(xT_hi, gcnt(k, r))
                    dve.tensor_tensor(xT_hl[:, 1], ps_g[:, :, :], xT_hl[:, 0].bitcast(F32), ALU.subtract).then_inc(xT_lo, 1)
                if part == 1:
                    dve.wait_ge(q_hi, gcnt(k, r))
                    for c in range(DC):
                        i = dve.scalar_tensor_tensor(out=q_hl[:, 1, c], in0=ps_g[:, c], scalar=bqk[:, 0, c:c + 1], in1=q_hl[:, 0, c],
                                                     op0=ALU.add, op1=ALU.subtract)
                    i.then_inc(q_lo, 1)
                if part == 2:
                    dve.wait_ge(k_hi, gcnt(k, r))
                    for c in range(DC):
                        i = dve.scalar_tensor_tensor(out=kT[:, g, 1, c, :, KPAD:KS], in0=ps_g[:, c].rearrange("p (b s) -> p b s", b=GB),
                                                     scalar=bqk[:, 1, c:c + 1], in1=kT[:, g, 0, c, :, KPAD:KS],
                                                     op0=ALU.add, op1=ALU.subtract)
                    i.then_inc(k_lo, 1)
                if part == 3:
                    dve.wait_ge(v_hi, gcnt(k, r))
                    dve.tensor_tensor(vw[:, g, 1, 1], ps_g[:, :, :].rearrange("p a (b d) -> p (a b) d", d=D), vw[:, g, 1, 0],
                                      ALU.subtract).then_inc(v_lo, 1)

            norm_in(0, 0)
            dve.wait_ge(dve_ln, 1)
            aggregate_in(0, 0)
            norm_out(0, 0)
            for part in range(4):
                prep(0, 0, part)
                if part == 1:
                    heads_of_q(0, 0)
            norm_in(0, 4)
            dve.wait_ge(dve_ln, 3)
            aggregate_in(0, 4)

            def soft(k, r):
                sc = ps_s[:, :, :].rearrange("p a (n s) -> p (a n) s", s=SLOT)[:, :, 0:KW]
                dve.wait_ge(s_ps, cnt(k, r))
                dve.tensor_reduce(mx[:, :], sc, AX, ALU.max).then_inc(mx_done, 1)
                dve.wait_ge(mx_done, cnt(k, r))
                if r >= 2 or not isint(k):
                    dve.wait_ge(pT_ps, cnt(k, r - 2))
                else:
                    dve.wait_ge(init_pool, 3)
                dve.tensor_tensor(es[:, r % 2, :, SLOT - KW:SLOT], sc, mx[:, :].unsqueeze(2).to_broadcast([P, 16, KW]),
                                  ALU.subtract).then_inc(s_sub, 1)

            def low_p(k, r):
                dve.wait_ge(pT_hi, cnt(k, r))
                dve.tensor_tensor(pT[:, 1], ps_p[:, :, :].rearrange("p a (b n) -> p (a b) n", n=P), pT[:, 0], ALU.subtract).then_inc(pT_lo, 1)

            def invert_sums(k, r):
                dve.wait_ge(o_ps, cnt(k, r))
                if not isint(k) or r >= 1:
                    dve.wait_ge(o_done, cnt(k, r - 1))
                dve.reciprocal(rinv[:, :, :], ps_s[:, :, :].rearrange("p j (n s) -> p j n s", s=SLOT)[:, :, :, KW]).then_inc(rinv_done, 1)

            def take_o(k, r):
                dve.wait_ge(rinv_done, cnt(k, r))
                if not isint(k) or r >= 1:
                    dve.wait_ge(oT_ps, cnt(k, r - 1))
                o = ps_p[:, :, :].rearrange("p a (n d) -> p (a n) d", d=64)
                for v in range(V4):
                    rows = slice(32 * v, 32 * v + 32)
                    i = dve.tensor_tensor(osb[rows], o[rows, :, v * HD:(v + 1) * HD],
                                          rinv[rows].rearrange("p j n -> p (j n)").unsqueeze(2).to_broadcast([32, 16, HD]), ALU.mult)
                i.then_inc(o_done, 1)

            def residual(k, r):
                b, g = r % 2, (r // 4) % 2
                dve.wait_ge(y_ps, cnt(k, r))
                dve.wait_ge(xb_done, gcnt(k, r))
                if not isint(k) or r >= 2:
                    dve.wait_ge(x1_out[b], 16 * (4 * k + r // 2))
                dve.scalar_tensor_tensor(out=x1[:, b], in0=ps_m[:, 0:D], scalar=gtanh[:, 0:1], in1=xb[:, g, r % 4],
                                         op0=ALU.mult, op1=ALU.add).then_inc(x1_done, 1)
                dve.wait_ge(x1_done, cnt(k, r))
                dve.bn_stats(stat2[:, :], x1[:, b]).then_inc(st2_done, 1)

            def aggregate2(k, r):
                dve.bn_aggr(mv2[:, :], stat2[:, :]).then_inc(st2_done, 1)

            def norm2(k, r):
                b = r % 2
                dve.wait_ge(rstd2_done, cnt(k, r))
                if not isint(k) or r >= 2:
                    dve.wait_ge(xn2_out[b], 16 * (4 * k + r // 2))
                    dve.wait_ge(x2T_ps, cnt(k, r - 2))
                dve.tensor_scalar(xn2[:, b], x1[:, b], mv2[:, 0:1], rstd2[:, 0:1], ALU.subtract, ALU.mult).then_inc(xn2_done, 1)

            def keep_logits(k, r):
                dve.wait_ge(lg_ps, cnt(k, r))
                dve.tensor_copy(logits[:, bass.ds(8 * k + r, 1)].rearrange("p a e -> p (a e)"), ps_s[:, 0, SLOT - E:SLOT]).then_inc(lg_done, 1)

            def step(k, r):
                if valid(k, r, 2):
                    dve.wait_ge(st2_done, cnt(k, r - 2, 2) - 1)
                if valid(k, r, 1):
                    invert_sums(k, r - 1)
                if valid(k, r, 3):
                    keep_logits(k, r - 3)
                if valid(k, r, 1):
                    take_o(k, r - 1)
                if valid(k, r, 2):
                    aggregate2(k, r - 2)
                if r % 4 == 0 and has_next(k, r):
                    norm_out(k, r + 4)
                if valid(k, r, 0):
                    soft(k, r)
                if valid(k, r, 2):
                    norm2(k, r - 2)
                if has_next(k, r):
                    if r % 4 == 2:
                        heads_of_q(k, r + 4)
                    prep(k, r + 4, r % 4)
                ahead = r % 4 == 3 and has_next(k, r) and (not isint(k) or 8 * k + r < B - 8)
                if ahead:
                    norm_in(k, r + 5)
                    dve.wait_ge(dve_ln, gcnt(k, r + 5, 2) - 1)
                if valid(k, r, 0):
                    low_p(k, r)
                if ahead:
                    aggregate_in(k, r + 5)
                if valid(k, r, 1):
                    residual(k, r - 1)

            schedule(dve, step)
            dve.wait_ge(lg_done, B)

        att.close()
        route_and_experts(nc, ctx, cst, gtanh, logits, xn_rows, w1, w2, out)


def route_and_experts(nc, ctx, cst, gtanh, logits, xn_rows, w1, w2, out):
    def sb(name, shape, dt=F32):
        return ctx.enter_context(nc.sbuf_tensor(name, shape, dt))

    def sem(name):
        return ctx.enter_context(nc.semaphore(name))

    ident = cst[:, C_ID:C_ID + P]
    KT = TOPK * B

    idx_all = sb("idx_all", [P, ST + SPARE], I32)
    p_all = sb("p_all", [P, ST + SPARE])
    w_raw = sb("we_raw", [P, 2, DC * F])
    w_hl = sb("we_hl", [P, 2, 2, 2, DC * F], F32R)
    NPIECE = 8
    PIECE = 2 * DC * F // NPIECE

    raw_in, w_hi, w_lo = sem("raw_in"), sem("w_hi"), sem("w_lo")

    w1_e = w1.rearrange("e (c p) f -> e p c f", p=P)
    w2_e = w2.rearrange("e (c p) d -> e p c d", p=P)

    def load_weights(sp, e):
        sp.dma_start(w_raw[:, 0].rearrange("p (c f) -> p c f", c=DC), w1_e[e]).then_inc(raw_in, 16)
        sp.dma_start(w_raw[:, 1].rearrange("p (c d) -> p c d", c=FC), w2_e[e]).then_inc(raw_in, 16)

    def piece(t, n):
        return t.rearrange("p l n -> p (l n)")[:, n * PIECE:(n + 1) * PIECE]

    def split_hi(act, buf, n):
        return act.activation(piece(w_hl[:, buf, 0], n), piece(w_raw[:, :], n), ACT.Copy)

    def split_lo(eng, buf, n):
        return eng.tensor_tensor(piece(w_hl[:, buf, 1], n), piece(w_raw[:, :], n), piece(w_hl[:, buf, 0], n).bitcast(F32), ALU.subtract)

    with ExitStack() as rt:
        def sr(name, shape, dt=F32):
            return rt.enter_context(nc.sbuf_tensor(name, shape, dt))

        oh = sr("oh", [P, TOPK, B, E])
        lg2 = sr("lg2", [P, B, E])
        tmp = sr("tmp", [P, B, E])
        top = sr("top", [P, TOPK, B])
        eid = sr("eid", [P, TOPK, B])
        io8 = sr("io8", [P, E])
        dlt, ex, den, inv = sr("dlt", [P, B]), sr("ex", [P, B]), sr("den", [P, B]), sr("inv", [P, B])
        prob = sr("prob", [P, TOPK, B])
        tot = sr("tot", [P, KT, E])
        sc = [sr(f"scan{i}", [P, KT, E]) for i in range(2)]
        rank = sr("rank", [P, KT])
        valid_t = sr("valid_t", [P, KT])
        slot_f = sr("slot_f", [P, KT])
        slot_i, hi_i, lo_i = sr("slot_i", [P, KT], I32), sr("hi_i", [P, KT], I32), sr("lo_i", [P, KT], I32)
        hi_f, lo_f = sr("hi_f", [P, KT]), sr("lo_f", [P, KT])
        tokv, pval = sr("tokv", [P, KT]), sr("pval", [P, KT])
        NB = 4
        at_row = sr("at_row", [P, NB, P])
        at_col = sr("at_col", [P, NB, 2 * ST])
        ps_pre = rt.enter_context(nc.psum_tensor("ps_pre", [P, 2, 512], F32))
        ps_tot = rt.enter_context(nc.psum_tensor("ps_tot", [P, 2, 512], F32))
        ps_tab = rt.enter_context(nc.psum_tensor("ps_tab", [P, 512], F32))
        seq, exp_done, sums_ps = sem("seq"), sem("exp_done"), sem("sums_ps")
        hot_done, hot_used, table_ps = sem("hot_done"), sem("hot_used"), sem("table_ps")
        dlt_done = sem("dlt_done")

        def bc(ap):
            return ap.unsqueeze(2).to_broadcast([P, B, E])

        block = rt.enter_context(nc.Block())

        @block.sync
        def _(sp):
            load_weights(sp, 0)

        @block.gpsimd
        def _(pool):
            for n in range(NPIECE):
                pool.wait_ge(w_hi, n + 1)
                split_lo(pool, 0, n).then_inc(w_lo, 1)

        @block.scalar
        def _(act):
            act.wait_ge(raw_in, 32)
            for n in range(NPIECE):
                split_hi(act, 0, n).then_inc(w_hi, 1)
            act.wait_ge(dlt_done, 1)
            act.activation(ex[:, :], dlt[:, :], ACT.Exp).then_inc(exp_done, 1)

        @block.vector
        def _(dve):
            count = [0]

            def then(ins):
                count[0] += 1
                ins.then_inc(seq, 1)
                dve.wait_ge(seq, count[0])

            iota = cst[:, C_E8:C_E8 + E].unsqueeze(1).to_broadcast([P, B, E])
            then(dve.tensor_scalar(io8[:, :], cst[:, C_E8:C_E8 + E], float(E), None, ALU.add))
            src = logits[:, :, :]
            for k in range(TOPK):
                then(dve.tensor_reduce(top[:, k], src, AX, ALU.max))
                then(dve.tensor_tensor(tmp[:, :, :], src, bc(top[:, k]), ALU.is_equal))
                then(dve.scalar_tensor_tensor(out=tmp[:, :, :], in0=tmp[:, :, :], scalar=-float(E),
                                              in1=io8[:, :].unsqueeze(1).to_broadcast([P, B, E]), op0=ALU.mult, op1=ALU.add))
                then(dve.tensor_reduce(eid[:, k], tmp[:, :, :], AX, ALU.min))
                then(dve.tensor_tensor(oh[:, k], iota, bc(eid[:, k]), ALU.is_equal))
                if k == 0:
                    then(dve.scalar_tensor_tensor(out=lg2[:, :, :], in0=oh[:, 0], scalar=-3.0e38, in1=src, op0=ALU.mult, op1=ALU.add))
                    src = lg2[:, :, :]
            dve.tensor_tensor(dlt[:, :], top[:, 1], top[:, 0], ALU.subtract).then_inc(dlt_done, 1)
            dve.wait_ge(exp_done, 1)
            then(dve.tensor_scalar(den[:, :], ex[:, :], 1.0, None, ALU.add))
            then(dve.reciprocal(inv[:, :], den[:, :]))
            then(dve.tensor_scalar(prob[:, 0], inv[:, :], gtanh[:, 1:2], None, ALU.mult))
            then(dve.tensor_tensor(prob[:, 1], prob[:, 0], ex[:, :], ALU.mult))

            dve.wait_ge(sums_ps, 1)
            then(dve.tensor_copy(tot[:, :, :].rearrange("p t e -> p (t e)"), ps_tot[:, :, :].rearrange("p a b -> p (a b)")))
            a, d = tot, 1
            n = 0
            while d < KT:
                b = sc[n % 2]
                dve.tensor_copy(b[:, 0:d], a[:, 0:d])
                then(dve.tensor_tensor(b[:, d:KT], a[:, d:KT], a[:, 0:KT - d], ALU.add))
                a, d, n = b, 2 * d, n + 1
            b = sc[n % 2]
            then(dve.tensor_tensor(b[:, :, :], a[:, :, :], tot[:, :, :], ALU.subtract))
            flat = b[:, :, :].rearrange("p t e -> p (t e)")
            then(dve.tensor_tensor(flat, ps_pre[:, :, :].rearrange("p a b -> p (a b)"), flat, ALU.add))
            then(dve.tensor_tensor(b[:, :, :], b[:, :, :], oh[:, :, :, :].rearrange("p k t e -> p (k t) e"), ALU.mult))
            then(dve.tensor_reduce(rank[:, :], b[:, :, :], AX, ALU.add))
            then(dve.tensor_scalar(valid_t[:, :], rank[:, :], float(CAP), None, ALU.is_lt))
            then(dve.scalar_tensor_tensor(out=slot_f[:, :], in0=eid[:, :, :].rearrange("p k t -> p (k t)"), scalar=float(CAP), in1=rank[:, :],
                                          op0=ALU.mult, op1=ALU.add))
            then(dve.tensor_copy(slot_i[:, :], slot_f[:, :]))
            dve.tensor_scalar(hi_i[:, :], slot_i[:, :], 7, None, ALU.arith_shift_right)
            then(dve.tensor_scalar(lo_i[:, :], slot_i[:, :], P - 1, None, ALU.bitwise_and))
            dve.tensor_copy(hi_f[:, :], hi_i[:, :])
            then(dve.tensor_copy(lo_f[:, :], lo_i[:, :]))
            then(dve.scalar_tensor_tensor(out=hi_f[:, :], in0=hi_f[:, :], scalar=1.0, in1=valid_t[:, :], op0=ALU.add, op1=ALU.mult))
            dve.tensor_scalar(hi_f[:, :], hi_f[:, :], -1.0, None, ALU.add)
            dve.tensor_tensor(tokv[:, :], cst[:, C_TOK:C_TOK + KT], rank[:, :], ALU.subtract)
            then(dve.tensor_tensor(pval[:, :], prob[:, :, :].rearrange("p k t -> p (k t)"), valid_t[:, :], ALU.mult))

            def hot(t, j):
                dve.tensor_scalar(at_row[:, j], cst[:, C_I128:C_I128 + P], lo_f[:, bass.ds(t, 1)], None, ALU.is_equal)
                dve.tensor_scalar(at_col[:, j, 0:ST], cst[:, C_I160:C_I160 + ST], hi_f[:, bass.ds(t, 1)], tokv[:, bass.ds(t, 1)],
                                  ALU.is_equal, ALU.mult)
                dve.tensor_scalar(at_col[:, j, ST:2 * ST], cst[:, C_I160:C_I160 + ST], hi_f[:, bass.ds(t, 1)], pval[:, bass.ds(t, 1)],
                                  ALU.is_equal, ALU.mult).then_inc(hot_done, 1)

            for j in range(NB):
                hot(j, j)
            with dve.Fori(1, KT // NB) as q:
                for j in range(NB):
                    dve.wait_ge(hot_used, NB * q - NB + j + 1)
                    hot(NB * q + j, j)
            dve.wait_ge(table_ps, 1)
            dve.tensor_copy(p_all[:, 0:ST], ps_tab[:, ST:2 * ST])
            dve.memset(p_all[:, ST:ST + SPARE], 0.0)
            dve.tensor_tensor(idx_all[:, 0:ST], ps_tab[:, 0:ST], cst[:, C_PB:C_PB + ST], ALU.add)
            dve.tensor_copy(idx_all[:, ST:ST + SPARE], cst[:, C_PB + ST:C_PB + ST + SPARE])

        @block.tensor
        def _(pe):
            pe.wait_ge(dlt_done, 1)
            for k in range(TOPK):
                rows = oh[:, k].rearrange("p t e -> p (t e)")
                pe.matmul(ps_pre[:, k], cst[:, C_TRI:C_TRI + P], rows, start=True, stop=True)
                i = pe.matmul(ps_tot[:, k], cst[:, C_ONE:C_ONE + P], rows, start=True, stop=True)
            i.then_inc(sums_ps, 1)

            def place(n, j, first, last):
                pe.wait_ge(hot_done, n)
                return pe.matmul(ps_tab[:, 0:2 * ST], at_row[:, j], at_col[:, j], start=first, stop=last)

            for j in range(NB):
                place(j + 1, j, j == 0, False).then_inc(hot_used, 1)
            with pe.Fori(1, KT // NB - 1) as q:
                for j in range(NB):
                    place(NB * q + j + 1, j, False, False).then_inc(hot_used, 1)
            for j in range(NB):
                i = place(KT - NB + j + 1, j, False, j == NB - 1)
            i.then_inc(table_ps, 1)

    RM = 2 * MTE
    idx_st = sb("idx_st", [P, RM, SUB], I32)
    p_st = sb("p_st", [P, RM, SUB])
    rows_in = sb("rows_in", [P, 2, SUB, D])
    xT = sb("xe_T", [P, 2, 2, DC, MT], F32R)
    r_sb = sb("r_sb", [P, 2, MT])
    sq_sb = sb("sq_sb", [P, 2, MT])
    HR = 4
    h_hl = sb("h_hl", [P, HR, 2, MT], F32R)
    y_sb = sb("y_sb", [P, 2, SUB, D])
    ps_x = ctx.enter_context(nc.psum_tensor("pe_x", [P, DC, 512], F32))
    ps_h = ctx.enter_context(nc.psum_tensor("pe_h", [P, 2, 512], F32))
    ps_y = ctx.enter_context(nc.psum_tensor("pe_y", [P, SUB, 512], F32))

    gate_t = sb("gate_t", [P, 3])
    staged, gate_done = sem("staged"), sem("gate_done")
    g_in = [sem(f"g_in{i}") for i in range(2)]
    xe_ps, xe_hi, xe_lo = sem("xe_ps"), sem("xe_hi"), sem("xe_lo")
    h_ps, relu_done, sq_done, h_hi, h_lo, g2_done = sem("h_ps"), sem("relu_done"), sem("sq_done"), sem("h_hi"), sem("h_lo"), sem("g2_done")
    ye_ps, ye_sb, y_out = sem("ye_ps"), sem("ye_sb"), sem("y_out")

    X0 = 1
    GATES = 5 * RM + 1

    def mc(k, r):
        return k * RM + (r + 1)

    def nch(k, r, f):
        return k * (RM * FC) + (r * FC + f + 1)

    block = ctx.enter_context(nc.Block())

    @block.sync
    def _(sp):
        with sp.Fori(0, E // 2) as k:
            for h in range(2):
                sp.wait_ge(w_hi, (2 * k + h + 1) * NPIECE)
                sp.wait_ge(w_lo, (2 * k + h + 1) * NPIECE)
                load_weights(sp, (2 * k + h + 1) % E)
        sp.wait_ge(raw_in, 32 * (E + 1))

    @block.gpsimd
    def _(pool):
        def gate(k, r, n):
            pool.wait_ge(gate_done, k * GATES + (5 * r + n + 1))
            pool.tensor_tensor(gate_t[:, 0:1], ident[:, 0:1], ident[:, 0:1], ALU.add).then_inc(gate_done, 1)

        def gather(k, r, first=False):
            b = r % 2
            pool.wait_ge(staged, mc(k, r))
            if not first:
                pool.wait_ge(xe_ps, X0 + mc(k, r) - 2)
                gate(k, r - 2, 0)
            for s in range(SUB):
                pool.indirect_dma_start(rows_in[:, b, s], None, xn_rows,
                                        bass.IndirectOffsetOnAxis(ap=idx_st[:, r % RM, s:s + 1], axis=0)).then_inc(g_in[b], 16)

        def scatter(k, r):
            for s in range(SUB):
                pool.wait_ge(ye_sb, X0 + 4 * mc(k, r) - 3 + s)
                if r % MTE == 0 and r > 0 and s == 0:
                    pool.wait_ge(y_out, 64 * mc(k, r - 1))
                gate(k, r, s + 1)
                pool.indirect_dma_start(out, bass.IndirectOffsetOnAxis(ap=idx_st[:, r % RM, s:s + 1], axis=0),
                                        y_sb[:, r % 2, s], None, compute_op=ALU.add).then_inc(y_out, 16)

        pool.tensor_tensor(gate_t[:, 0:1], ident[:, 0:1], ident[:, 0:1], ALU.add).then_inc(gate_done, 1)
        gather(0, 0, True)
        gather(0, 1, True)
        with pool.Fori(0, E // 2) as k:
            for r in range(RM):
                gather(k, r + 2)
                if r % MTE in (1, 2):
                    for n in range(4):
                        m = (r % MTE - 1) * 4 + n
                        pool.wait_ge(w_hi, (2 * k + r // MTE + 1) * NPIECE + m + 1)
                        split_lo(pool, 1 - r // MTE, m).then_inc(w_lo, 1)
                scatter(k, r)
            pool.wait_ge(y_out, 64 * mc(k, RM - 1))
            gate(k, RM, 0)
        pool.wait_ge(y_out, 16 * ST)
        pool.wait_ge(g_in[0], 64 * (NSLOT // MT // 2 + 1))
        pool.wait_ge(g_in[1], 64 * (NSLOT // MT // 2 + 1))

    @block.scalar
    def _(act):
        def x_hi(k, r):
            act.wait_ge(xe_ps, X0 + mc(k, r))
            act.activation(xT[:, r % 2, 0], ps_x[:, :, :], ACT.Copy).then_inc(xe_hi, 1)

        def evac(k, r):
            for s in range(SUB):
                if s < SUB - 1:
                    act.wait_ge(ye_ps, (SUB - 1) * (mc(k, r) - 1) + s + 1)
                else:
                    act.wait_ge(g2_done, nch(k, r, FC - 1))
                act.activation(y_sb[:, r % 2, s], ps_y[:, s, 0:D], ACT.Copy, scale=p_st[:, r, s:s + 1]).then_inc(ye_sb, 1)

        act.activation(gate_t[:, 2:3], ident[:, 0:1], ACT.Copy).then_inc(ye_sb, X0)
        x_hi(0, 0)
        with act.Fori(0, E // 2) as k:
            for r in range(RM):
                for f in range(FC):
                    n = r * FC + f
                    if f == 2 and r > 0:
                        if r > 1:
                            act.wait_ge(y_out, 64 * mc(k, r - 3))
                        else:
                            act.wait_ge(gate_done, X0 + k * GATES)
                        evac(k, r - 1)
                    act.wait_ge(h_ps, nch(k, r, f))
                    if n >= 2:
                        act.wait_ge(sq_done, nch(k, r, f) - 2)
                    act.activation(r_sb[:, f % 2], ps_h[:, f % 2], ACT.Relu).then_inc(relu_done, 1)
                    act.wait_ge(relu_done, nch(k, r, f))
                    if n >= HR:
                        act.wait_ge(g2_done, nch(k, r, f) - HR)
                    act.activation(h_hl[:, f % HR, 0], r_sb[:, f % 2], ACT.Square).then_inc(h_hi, 1)
                    if f == 5:
                        x_hi(k, r + 1)
                    if r % MTE == 1:
                        if f == 0:
                            act.wait_ge(raw_in, 32 * (2 * k + r // MTE + 2))
                        split_hi(act, 1 - r // MTE, f).then_inc(w_hi, 1)
            act.wait_ge(y_out, 64 * mc(k, RM - 3))
            evac(k, RM - 1)

    @block.tensor
    def _(pe):
        def turn(k, r):
            b = r % 2
            pe.wait_ge(g_in[b], 64 * (MTE * k + r // 2 + 1))
            if not (isinstance(k, int) and r == 0):
                pe.wait_ge(xe_lo, mc(k, r) - 1)
            for c in range(DC):
                for s in range(SUB):
                    i = pe.transpose(ps_x[:, c, s * P:(s + 1) * P], rows_in[:, b, s, c * P:(c + 1) * P], ident)
            i.then_inc(xe_ps, 1)

        def first_layer(k, r, f):
            e = r // MTE
            if f == 0:
                pe.wait_ge(xe_hi, mc(k, r))
                pe.wait_ge(xe_lo, mc(k, r))
                if r % MTE == 0:
                    pe.wait_ge(w_hi, (2 * k + e + 1) * NPIECE)
                    pe.wait_ge(w_lo, (2 * k + e + 1) * NPIECE)
            if r * FC + f >= 2:
                pe.wait_ge(relu_done, nch(k, r, f) - 2)
            n = 0
            for c in range(DC):
                for w, a in ((0, 0), (0, 1), (1, 0)):
                    i = pe.matmul(ps_h[:, f % 2], w_hl[:, e, w, 0, c * F + f * P:c * F + (f + 1) * P], xT[:, r % 2, a, c],
                                  start=(n == 0), stop=(n == 3 * DC - 1))
                    n += 1
            i.then_inc(h_ps, 1)

        def second_layer(k, r, f):
            e = r // MTE
            pe.wait_ge(h_hi, nch(k, r, f))
            pe.wait_ge(h_lo, nch(k, r, f))
            for s in range(SUB):
                if f == 0 and r > 0:
                    pe.wait_ge(ye_sb, X0 + 4 * mc(k, r - 1) - 3 + s)
                if f == 0 and r == 0 and s == 0:
                    pe.wait_ge(ye_sb, X0 + k * (4 * RM))
                for a, w in ((0, 0), (0, 1), (1, 0)):
                    i = pe.matmul(ps_y[:, s, 0:D], h_hl[:, f % HR, a, s * P:(s + 1) * P], w_hl[:, e, w, 1, f * D:(f + 1) * D],
                                  start=(f == 0 and a == 0 and w == 0), stop=(f == FC - 1 and a == 1))
                if f == FC - 1 and s < SUB - 1:
                    i.then_inc(ye_ps, 1)
            i.then_inc(g2_done, 1)

        LAG = 2
        pe.transpose(ps_h[:, 0, 0:P], ident, ident).then_inc(xe_ps, X0)
        turn(0, 0)
        with pe.Fori(0, E // 2) as k:
            for r in range(RM):
                for f in range(FC):
                    first_layer(k, r, f)
                    if f == 4:
                        turn(k, r + 1)
                    n = r * FC + f - LAG
                    if n >= 0:
                        second_layer(k, n // FC, n % FC)
            for n in range(RM * FC - LAG, RM * FC):
                second_layer(k, n // FC, n % FC)

    @block.vector
    def _(dve):
        def stage(k, r):
            dve.tensor_copy(p_st[:, r % RM], p_all[:, bass.ds((k * RM + r) * SUB, SUB)])
            dve.tensor_copy(idx_st[:, r % RM], idx_all[:, bass.ds((k * RM + r) * SUB, SUB)]).then_inc(staged, 1)

        def x_lo(k, r):
            dve.wait_ge(xe_hi, mc(k, r))
            dve.tensor_tensor(xT[:, r % 2, 1], ps_x[:, :, :], xT[:, r % 2, 0].bitcast(F32), ALU.subtract).then_inc(xe_lo, 1)

        stage(0, 0)
        stage(0, 1)
        x_lo(0, 0)
        with dve.Fori(0, E // 2) as k:
            for r in range(RM):
                for f in range(FC):
                    n = r * FC + f
                    dve.wait_ge(relu_done, nch(k, r, f))
                    dve.tensor_tensor(sq_sb[:, f % 2], r_sb[:, f % 2], r_sb[:, f % 2], ALU.mult).then_inc(sq_done, 1)
                    dve.wait_ge(sq_done, nch(k, r, f))
                    dve.wait_ge(h_hi, nch(k, r, f))
                    dve.tensor_tensor(h_hl[:, f % HR, 1], sq_sb[:, f % 2], h_hl[:, f % HR, 0].bitcast(F32), ALU.subtract).then_inc(h_lo, 1)
                    if f == 3:
                        stage(k, r + 2)
                    if f == 5:
                        x_lo(k, r + 1)


def pack_constants():
    import numpy as np

    c = np.zeros((P, C_END), np.float32)
    p = np.arange(P)
    c[:, C_ID:C_ID + P] = np.eye(P)
    q = p % QB
    for half_block in range(8):
        par, j = half_block // 4, half_block % 2
        qb = 2 * j + par
        k = np.arange(KW)
        ok = (k[None] >= q[:, None] + 1) & (k[None] <= q[:, None] + W)
        if qb == 0:
            ok &= (k[None] - q[:, None] - 1) <= q[:, None]
        c[:, C_BAND + half_block * SLOT:C_BAND + half_block * SLOT + KW] = np.where(ok, 0.0, NEG)
    c[:, C_VM:C_VM + V4] = ((p[:, None] % 64) // 16) == np.arange(V4)[None]
    c[:, C_TRI:C_TRI + P] = p[:, None] < p[None]
    c[:, C_ONE:C_ONE + P] = 1.0
    c[:, C_I128:C_I128 + P] = p[None]
    c[:, C_I160:C_I160 + ST] = np.arange(ST)[None]
    c[:, C_TOK:C_TOK + TOPK * B] = (np.arange(TOPK * B)[None] % B) * S + p[:, None] - N
    c[:, C_E8:C_E8 + E] = np.arange(E)[None]
    c[:, C_PB:C_END] = N + (np.arange(ST + SPARE)[None] % STE) * P + p[:, None]
    return c


def kernel(x, ctx_1024, g_xattn, g_ffn, L0_xattn_Wq, L0_xattn_bq, L0_xattn_Wk, L0_xattn_bk, L0_xattn_Wv, L0_xattn_bv,
           L0_xattn_Wo, L0_xattn_bo, L0_ffn_w_g, L0_ffn_c_fc, L0_ffn_c_proj):
    import numpy as np
    import concourse.bacc as bacc
    from concourse.bass_utils import run_bass_kernel_spmd

    def lay(a, *steps):
        a = np.asarray(a)
        for kind, how in steps:
            a = a.reshape(how) if kind == "reshape" else a.transpose(how)
        return np.ascontiguousarray(a)

    arrays = {
        "x": lay(x, ("reshape", (N, D))),
        "ctxT": lay(ctx_1024, ("reshape", (N, D)), ("turn", (1, 0))),
        "gx": lay(g_xattn),
        "gf": lay(g_ffn),
        "wqT": lay(L0_xattn_Wq, ("turn", (1, 0))),
        "bq": lay(L0_xattn_bq, ("reshape", (DC, P)), ("turn", (1, 0))),
        "wkT": lay(L0_xattn_Wk, ("turn", (1, 0))),
        "bk": lay(L0_xattn_bk, ("reshape", (DC, P)), ("turn", (1, 0))),
        "wvT": lay(L0_xattn_Wv, ("turn", (1, 0))),
        "bv": lay(L0_xattn_bv),
        "woP": lay(L0_xattn_Wo, ("turn", (1, 0)), ("reshape", (DC, 2, V4, HD, D)), ("turn", (1, 0, 3, 2, 4)), ("reshape", (64, V4, D))),
        "bo": lay(L0_xattn_bo),
        "wgT": lay(L0_ffn_w_g, ("turn", (1, 0))),
        "w1": lay(L0_ffn_c_fc),
        "w2": lay(L0_ffn_c_proj),
        "consts": pack_constants(),
    }
    nc = bacc.Bacc("TRN2", target_bir_lowering=False, num_devices=1)
    args = [nc.dram_tensor(f"in_{n}", a.shape, mybir.dt.from_np(a.dtype), kind="ExternalInput").ap() for n, a in arrays.items()]
    args.append(nc.dram_tensor("out_rows", (N + TRASH, D), F32, kind="ExternalOutput").ap())
    build_kernel(nc, *args)
    r = run_bass_kernel_spmd(nc, [{f"in_{n}": a for n, a in arrays.items()}], core_ids=[0])
    return r.results[0]["out_rows"][:N].reshape(B, S, D)
```

```python
from contextlib import ExitStack

import concourse.bass as bass
from concourse import mybir

F32 = mybir.dt.float32
F32R = mybir.dt.float32r
F16 = mybir.dt.float16
BF16 = mybir.dt.bfloat16
I32 = mybir.dt.int32
ALU = mybir.AluOpType
ACT = mybir.ActivationFunctionType
AX = mybir.AxisListType.X

P = 128
B, S, D = 64, 128, 256
N = B * S
H, HD, W = 16, 16, 16
DC = D // P
GB = 4
GT = GB * S
NGROUP = B // GB
V4 = 4
QB = 32
KW = QB + W
SLOT = 64
KPAD = 16
KS = KPAD + S
EPS = 1e-5
E, TOPK, F = 8, 2, 1024
CAP = max(4, int(1.25 * N * TOPK / E))
NSLOT = E * CAP
ST = NSLOT // P
STE = CAP // P
MT = 512
MTE = CAP // MT
SUB = MT // P
FC = F // P
TRASH = CAP
SPARE = 2 * SUB
NEG = -1.0e30

C_ID, C_BAND, C_VM, C_TRI, C_ONE = 0, 128, 128 + 512, 128 + 512 + 4, 128 + 512 + 4 + 128
C_I128 = C_ONE + 128
C_I160 = C_I128 + 128
C_TOK = C_I160 + ST
C_E8 = C_TOK + TOPK * B
C_PB = C_E8 + E
C_END = C_PB + ST + SPARE


def cnt(k, r, per=1):
    return k * (8 * per) + (r + 1) * per


def gcnt(k, r, per=1):
    return k * (2 * per) + (r // 4 + 1) * per


def build_kernel(nc, x, ctxT, gx, gf, wqT, bq, wkT, bk, wvT, bv, woP, bo, wgT, w1, w2, consts, out):
    ctx = ExitStack()
    with ctx:
        def sb(name, shape, dt=F32):
            return ctx.enter_context(nc.sbuf_tensor(name, shape, dt))

        def sem(name):
            return ctx.enter_context(nc.semaphore(name))

        xn_rows = nc.dram_tensor("xn_rows", [N + TRASH, D], F32, kind="Internal").ap()

        cst = sb("cst", [P, C_END])
        ident = cst[:, C_ID:C_ID + P]
        vmask = cst[:, C_VM:C_VM + V4]
        tok_id = cst[:, C_TOK:C_TOK + TOPK * B]
        e_iota = cst[:, C_E8:C_E8 + E]
        identb = sb("identb", [P, P], BF16)
        bandb = sb("bandb", [P, 512], BF16)
        gates = sb("gates", [P, 2])
        gtanh = sb("gtanh", [P, 2])

        logits = sb("logits", [P, B, E])

        att = ctx.enter_context(ExitStack())

        def sa(name, shape, dt=F32):
            return att.enter_context(nc.sbuf_tensor(name, shape, dt))

        def pa(name, shape, dt=F32):
            return att.enter_context(nc.psum_tensor(name, shape, dt))

        ps_g = pa("ps_g", [P, 2, 512])
        ps_s = pa("ps_s", [P, 2, 512])
        ps_p = pa("ps_p", [P, 2, 512])
        ps_o = pa("ps_o", [P, 512])
        ps_m = pa("ps_m", [P, 512])

        w_raw = sa("w_raw", [P, 3, DC, D])
        w_hl = sa("w_hl", [P, 3, 2, DC, D], F32R)
        wo_sb = sa("wo_sb", [P, 2, D])
        wg_sb = sa("wg_sb", [P, DC, E])
        bqk = sa("bqk", [P, 2, DC])
        bv_raw = sa("bv_raw", [33, D])
        bv_hl = sa("bv_hl", [33, D], F32R)
        one_r = sa("one_r", [33, P], F32R)
        gbo = sa("gbo", [P, D])

        xg = sa("xg", [P, 2, GB, D])
        cg = sa("cg", [P, 2, DC, GT])
        c_hl = sa("c_hl", [P, 2, DC, GT], F32R)
        xn = sa("xn", [P, GB, D])
        xT_hl = sa("xT_hl", [P, 2, DC, GT], F32R)
        stat = sa("stat", [P, GB, 6])
        mv = sa("mv", [P, GB, 2])
        rstd = sa("rstd", [P, GB])
        xb = sa("xb", [P, 2, GB, D])
        q_hl = sa("q_hl", [P, 2, DC, GT], F16)
        qd = sa("qd", [P, 2, 2, DC, GT // QB, V4, QB], F16)
        kT = sa("kT", [P, 2, 2, DC, GB, KS], F16)
        vw = sa("vw", [P, 2, 2, 2, GB, D], F16)

        mx = sa("mx", [P, 16])
        es = sa("es", [P, 2, 16, SLOT])
        esum = sa("esum", [P, 16])
        rinv = sa("rinv", [P, 2, 4, 2])
        pT = sa("pT", [P, 2, 8, P], F16)
        osb = sa("osb", [P, 16, HD])
        oT = sa("oT", [P, 2, 4, QB])
        x1 = sa("x1", [P, 2, D])
        stat2 = sa("stat2", [P, 6])
        mv2 = sa("mv2", [P, 2])
        rstd2 = sa("rstd2", [P, 1])
        xn2 = sa("xn2", [P, 2, D])
        x2T = sa("x2T", [P, DC, P])
        var_e = sa("var_e", [P, GB])
        var_e2 = sa("var_e2", [P, 1])
        mhalf = sa("mhalf", [P, GB])
        eps_t = sa("eps_t", [P, GB])
        zrow = sa("zrow", [P, D])
        mr, shift = sa("mr", [P, GB]), sa("shift", [P, GB])
        mr2, shift2 = sa("mr2", [P, 1]), sa("shift2", [P, 1])

        const_in, weights_in, bias_in = sem("const_in"), sem("weights_in"), sem("bias_in")
        init_dve, init_pool, init_act = sem("init_dve"), sem("init_pool"), sem("init_act")
        x_in = [sem(f"x_in{i}") for i in range(2)]
        c_in = [sem(f"c_in{i}") for i in range(2)]
        dve_ln = sem("dve_ln")
        xn_done, xT_ps, xT_hi, xT_lo = sem("xn_done"), sem("xT_ps"), sem("xT_hi"), sem("xT_lo")
        c_hi, c_lo, xb_done = sem("c_hi"), sem("c_lo"), sem("xb_done")
        q_ps, q_hi, q_lo, qd_done = sem("q_ps"), sem("q_hi"), sem("q_lo"), sem("qd_done")
        k_ps, k_hi, k_lo = sem("k_ps"), sem("k_hi"), sem("k_lo")
        v_ps, v_hi, v_lo = sem("v_ps"), sem("v_hi"), sem("v_lo")
        v_shift = [sem(f"v_shift{i}") for i in range(2)]
        s_ps, mx_done, s_sub, e_done = sem("s_ps"), sem("mx_done"), sem("s_sub"), sem("e_done")
        sum_done, bv_zero = sem("sum_done"), sem("bv_zero")
        pT_ps, pT_hi, pT_lo, rinv_done = sem("pT_ps"), sem("pT_hi"), sem("pT_lo"), sem("rinv_done")
        o_ps, o_done, oT_ps, oT_done = sem("o_ps"), sem("o_done"), sem("oT_ps"), sem("oT_done")
        y_ps, x1_done, st2_done, xn2_done = sem("y_ps"), sem("x1_done"), sem("st2_done"), sem("xn2_done")
        x2T_ps, x2T_done, lg_ps, lg_done = sem("x2T_ps"), sem("x2T_done"), sem("lg_ps"), sem("lg_done")
        x1_out = [sem(f"x1_out{i}") for i in range(2)]
        xn2_out = [sem(f"xn2_out{i}") for i in range(2)]
        zero_out = sem("zero_out")
        var_done, var2_done = sem("var_done"), sem("var2_done")
        rstd_done, rstd2_done = sem("rstd_done"), sem("rstd2_done")
        mr_done, mr2_done = sem("mr_done"), sem("mr2_done")
        shift_done, shift2_done = sem("shift_done"), sem("shift2_done")

        x_g = x.rearrange("(g b s) d -> g s b d", b=GB, s=S)
        c_g = ctxT.rearrange("(c p) (g t) -> g p c t", p=P, t=GT)

        def isint(k):
            return isinstance(k, int)

        def valid(k, r, lag):
            return not isint(k) or (8 * k + r - lag >= 0 and 8 * k + r - lag < B)

        LAGS = 2

        def schedule(eng, step):
            for r in range(4):
                step(0, r)
            with eng.Fori(0, (NGROUP - 2) // 2) as k:
                for r in range(4, 12):
                    step(k, r)
            for r in range(4, 8 + LAGS):
                step((NGROUP - 2) // 2, r)

        def has_next(k, r):
            return not isint(k) or 8 * k + r < B - 4

        def ahead(k, r):
            return not isint(k) or 8 * k + r < B - 8

        block = att.enter_context(nc.Block())

        @block.sync
        def _(sp):
            sp.dma_start(cst[:, :], consts).then_inc(const_in, 16)
            sp.dma_start(gates[:, 0:1], gx.rearrange("(a n) -> a n", a=1).broadcast_to([P, 1])).then_inc(bias_in, 16)
            sp.dma_start(gates[:, 1:2], gf.rearrange("(a n) -> a n", a=1).broadcast_to([P, 1])).then_inc(bias_in, 16)
            sp.dma_start(gbo[:, :], bo.rearrange("(a n) -> a n", a=1).broadcast_to([P, D])).then_inc(bias_in, 16)
            sp.dma_start(bqk[:, 0, :], bq).then_inc(bias_in, 16)
            sp.dma_start(bqk[:, 1, :], bk).then_inc(bias_in, 16)
            sp.dma_start(bv_raw[0:1, :], bv.rearrange("(a n) -> a n", a=1)).then_inc(bias_in, 16)
            sp.dma_start(bv_raw[32:33, :], bv.rearrange("(a n) -> a n", a=1)).then_inc(bias_in, 16)
            sp.dma_start(xg[:, 0], x_g[0]).then_inc(x_in[0], 16)
            for n, w in enumerate((wqT, wkT, wvT)):
                sp.dma_start(w_raw[:, n], w.rearrange("(c p) n -> p c n", p=P)).then_inc(weights_in, 16)
            sp.dma_start(cg[:, 0], c_g[0]).then_inc(c_in[0], 16)
            sp.dma_start(wo_sb[:, :, :], woP).then_inc(weights_in, 16)
            sp.dma_start(wg_sb[:, :, :], wgT.rearrange("(c p) e -> p c e", p=P)).then_inc(weights_in, 16)
            sp.dma_start(xg[:, 1], x_g[1]).then_inc(x_in[1], 16)
            sp.dma_start(cg[:, 1], c_g[1]).then_inc(c_in[1], 16)
            sp.wait_ge(init_pool, 1)
            for rows in (xn_rows, out):
                sp.dma_start(rows[N:N + TRASH, :].rearrange("(t p) d -> p t d", p=P),
                             zrow[:, :].unsqueeze(1).to_broadcast([P, STE, D])).then_inc(zero_out, 16)

            def shift_v(k, r):
                g = (r // 4) % 2
                sp.wait_ge(v_hi, gcnt(k, r))
                sp.wait_ge(v_lo, gcnt(k, r))
                sp.dma_start(vw[QB:P, g, 0], vw[0:P - QB, g, 1]).then_inc(v_shift[g], 16)

            def load_ahead(k, r):
                g = (r // 4) % 2
                nxt = (2 * k + r // 4 + 2) % NGROUP
                sp.wait_ge(xn_done, gcnt(k, r))
                sp.wait_ge(xb_done, gcnt(k, r))
                sp.dma_start(xg[:, g], x_g[nxt]).then_inc(x_in[g], 16)
                sp.wait_ge(c_hi, gcnt(k, r))
                sp.wait_ge(c_lo, gcnt(k, r))
                sp.dma_start(cg[:, g], c_g[nxt]).then_inc(c_in[g], 16)

            sp.wait_ge(init_dve, 3)
            shift_v(0, 0)
            load_ahead(0, 0)

            def step(k, r):
                if r % 4 == 3 and has_next(k, r) and ahead(k, r + 1):
                    load_ahead(k, r + 1)
                if valid(k, r, 2):
                    b = r % 2
                    row = (8 * k + r - 2) * S
                    sp.wait_ge(x1_done, cnt(k, r - 2))
                    sp.dma_start(out[bass.ds(row, S), :], x1[:, b]).then_inc(x1_out[b], 16)
                    sp.wait_ge(xn2_done, cnt(k, r - 2))
                    sp.dma_start(xn_rows[bass.ds(row, S), :], xn2[:, b]).then_inc(xn2_out[b], 16)
                if r % 4 == 3 and has_next(k, r):
                    shift_v(k, r + 4)

            schedule(sp, step)
            for b in range(2):
                sp.wait_ge(x1_out[b], 16 * (B // 2))
                sp.wait_ge(xn2_out[b], 16 * (B // 2))
            sp.wait_ge(zero_out, 32)
            for g in range(2):
                sp.wait_ge(x_in[g], 16 * 9)
                sp.wait_ge(c_in[g], 16 * 9)

        @block.gpsimd
        def _(pool):
            pool.memset(zrow[:, :], 0.0).then_inc(init_pool, 1)
            pool.memset(mhalf[:, :], -0.5)
            pool.memset(eps_t[:, :], EPS)
            pool.memset(es[:, :, :, :], 0.0).then_inc(init_pool, 1)
            pool.wait_ge(init_act, 1)
            pool.wait_ge(bias_in, 16 * 7)
            pool.tensor_scalar(gbo[:, :], gbo[:, :], gtanh[:, 0:1], None, ALU.mult).then_inc(init_pool, 1)
            pool.wait_ge(init_pool, 3)

            def split_c(k, r):
                g = (r // 4) % 2
                pool.wait_ge(c_hi, gcnt(k, r))
                pool.tensor_tensor(c_hl[:, 1], cg[:, g], c_hl[:, 0].bitcast(F32), ALU.subtract).then_inc(c_lo, 1)

            def add_xb(k, r):
                g = (r // 4) % 2
                pool.wait_ge(x_in[g], 16 * (k + r // 8 + 1))
                pool.tensor_tensor(xb[:, g], xg[:, g], gbo[:, :].unsqueeze(1).to_broadcast([P, GB, D]), ALU.add).then_inc(xb_done, 1)

            def rstd_in(k, r):
                pool.wait_ge(dve_ln, gcnt(k, r, 2))
                pool.tensor_tensor(var_e[:, :], mv[:, :, 1], eps_t[:, :], ALU.add).then_inc(var_done, 1)
                pool.wait_ge(var_done, gcnt(k, r))
                if not isint(k) or r >= 4:
                    pool.wait_ge(xn_done, gcnt(k, r - 4))
                pool.tensor_tensor(rstd[:, :], var_e[:, :], mhalf[:, 0:GB], ALU.pow).then_inc(rstd_done, 1)
                pool.wait_ge(rstd_done, gcnt(k, r))
                pool.tensor_tensor(mr[:, :], mv[:, :, 0], rstd[:, :], ALU.mult).then_inc(mr_done, 1)
                pool.wait_ge(mr_done, gcnt(k, r))
                pool.tensor_tensor(shift[:, :], zrow[:, 0:GB], mr[:, :], ALU.subtract).then_inc(shift_done, 1)

            rstd_in(0, 0)
            split_c(0, 0)
            rstd_in(0, 4)
            add_xb(0, 0)

            def step(k, r):
                if valid(k, r, 2):
                    pool.wait_ge(st2_done, cnt(k, r - 2, 2))
                    pool.tensor_tensor(var_e2[:, :], mv2[:, 1:2], eps_t[:, 0:1], ALU.add).then_inc(var2_done, 1)
                    pool.wait_ge(var2_done, cnt(k, r - 2))
                    if valid(k, r, 3):
                        pool.wait_ge(xn2_done, cnt(k, r - 3))
                    pool.tensor_tensor(rstd2[:, :], var_e2[:, :], mhalf[:, 0:1], ALU.pow).then_inc(rstd2_done, 1)
                    pool.wait_ge(rstd2_done, cnt(k, r - 2))
                    pool.tensor_tensor(mr2[:, :], mv2[:, 0:1], rstd2[:, :], ALU.mult).then_inc(mr2_done, 1)
                    pool.wait_ge(mr2_done, cnt(k, r - 2))
                    pool.tensor_tensor(shift2[:, :], zrow[:, 0:1], mr2[:, :], ALU.subtract).then_inc(shift2_done, 1)
                if has_next(k, r):
                    if r % 4 == 0:
                        split_c(k, r + 4)
                    if r % 4 == 1 and ahead(k, r):
                        rstd_in(k, r + 7)
                    if r % 4 == 2:
                        if not isint(k) or r >= 4:
                            pool.wait_ge(x1_done, cnt(k, r - 3))
                        add_xb(k, r + 4)

            schedule(pool, step)

        @block.scalar
        def _(act):
            act.wait_ge(bias_in, 16 * 7)
            act.activation(gtanh[:, :], gates[:, :], ACT.Tanh).then_inc(init_act, 1)
            act.wait_ge(weights_in, 16 * 5)
            act.activation(w_hl[:, :, 0], w_raw[:, :], ACT.Copy).then_inc(init_act, 1)
            act.wait_ge(bv_zero, 1)
            act.activation(bv_hl[0:1, :], bv_raw[0:1, :], ACT.Copy).then_inc(init_act, 1)
            act.activation(bv_hl[32:33, :], bv_raw[32:33, :], ACT.Copy).then_inc(init_act, 1)

            def ctx_hi(k, r):
                g = (r // 4) % 2
                act.wait_ge(c_in[g], 16 * (k + r // 8 + 1))
                if not isint(k) or r >= 4:
                    act.wait_ge(v_ps, gcnt(k, r - 4))
                act.activation(c_hl[:, 0], cg[:, g], ACT.Copy).then_inc(c_hi, 1)

            def prep(k, r, part):
                g = (r // 4) % 2
                if part == 0:
                    act.wait_ge(xT_ps, gcnt(k, r))
                    act.activation(xT_hl[:, 0], ps_g[:, :, :], ACT.Copy).then_inc(xT_hi, 1)
                if part == 1:
                    act.wait_ge(q_ps, gcnt(k, r))
                    if not isint(k) or r >= 4:
                        act.wait_ge(qd_done, gcnt(k, r - 4))
                    for c in range(DC):
                        i = act.activation(q_hl[:, 0, c], ps_g[:, c], ACT.Identity, bias=bqk[:, 0, c:c + 1])
                    i.then_inc(q_hi, 1)
                if part == 2:
                    act.wait_ge(k_ps, gcnt(k, r))
                    if k_first(k, r):
                        act.wait_ge(init_dve, 3)
                    for c in range(DC):
                        i = act.activation(kT[:, g, 0, c, :, KPAD:KS], ps_g[:, c].rearrange("p (b s) -> p b s", b=GB),
                                           ACT.Identity, bias=bqk[:, 1, c:c + 1])
                    i.then_inc(k_hi, 1)
                if part == 3:
                    act.wait_ge(v_ps, gcnt(k, r))
                    act.activation(vw[:, g, 1, 0], ps_g[:, :, :].rearrange("p a (b d) -> p (a b) d", d=D), ACT.Copy).then_inc(v_hi, 1)

            def k_first(k, r):
                return isint(k) and k == 0 and r < 8

            def norm_out(k, r):
                g = (r // 4) % 2
                act.wait_ge(shift_done, gcnt(k, r))
                if not isint(k) or r >= 4:
                    act.wait_ge(xT_ps, gcnt(k, r - 4))
                for b in range(GB):
                    i = act.activation(xn[:, b], xg[:, g, b], ACT.Identity, bias=shift[:, b:b + 1], scale=rstd[:, b:b + 1])
                i.then_inc(xn_done, 1)

            def norm2(k, r):
                b = r % 2
                act.wait_ge(shift2_done, cnt(k, r))
                if not isint(k) or r >= 2:
                    act.wait_ge(xn2_out[b], 16 * (4 * k + r // 2))
                    act.wait_ge(x2T_ps, cnt(k, r - 2))
                act.activation(xn2[:, b], x1[:, b], ACT.Identity, bias=shift2[:, 0:1], scale=rstd2[:, 0:1]).then_inc(xn2_done, 1)

            def heads_of_q(k, r, heads):
                g = (r // 4) % 2
                act.wait_ge(q_lo, gcnt(k, r))
                for v in heads:
                    i = act.activation(qd[:, g, :, :, :, v].rearrange("p a c n s -> p (a c n) s"), q_hl[:, :, :, :].rearrange("p a c (n s) -> p (a c n) s", s=QB),
                                       ACT.Copy, scale=vmask[:, v:v + 1])
                if V4 - 1 in heads:
                    i.then_inc(qd_done, 1)

            norm_out(0, 0)
            ctx_hi(0, 0)
            prep(0, 0, 0)
            norm_out(0, 4)
            prep(0, 0, 1)
            heads_of_q(0, 0, range(V4))
            prep(0, 0, 2)
            prep(0, 0, 3)

            def step(k, r):
                if r % 4 == 0 and has_next(k, r):
                    ctx_hi(k, r + 4)
                if valid(k, r, 2):
                    norm2(k, r - 2)
                if valid(k, r, 0):
                    act.wait_ge(s_sub, cnt(k, r))
                    win = es[:, r % 2, :, SLOT - KW:SLOT]
                    act.activation(win, win, ACT.Exp, scale=HD ** -0.5).then_inc(e_done, 1)
                if valid(k, r, 1):
                    act.wait_ge(oT_ps, cnt(k, r - 1))
                    for half in range(2):
                        i = act.activation(oT[64 * half:64 * half + 64], ps_o[0:64, :].rearrange("p (q v s) -> p v q s", q=4, v=V4)[:, 2 * half:2 * half + 2],
                                           ACT.Copy)
                    i.then_inc(oT_done, 1)
                if valid(k, r, 2):
                    act.wait_ge(x2T_ps, cnt(k, r - 2))
                    act.activation(x2T[:, :, :], ps_m[:, D:2 * D].rearrange("p (c n) -> p c n", c=DC), ACT.Copy).then_inc(x2T_done, 1)
                if valid(k, r, 0):
                    for h in range(2):
                        act.wait_ge(pT_ps, cnt(k, r, 2) - 1 + h)
                        act.activation(pT[:, 0, 4 * h:4 * h + 4], ps_p[:, h].rearrange("p (b n) -> p b n", n=P), ACT.Copy).then_inc(pT_hi, 1)
                if has_next(k, r):
                    prep(k, r + 4, r % 4)
                    if r % 4 == 1 and ahead(k, r):
                        norm_out(k, r + 7)
                    if r % 4 >= 1:
                        heads_of_q(k, r + 4, ((0,), (1, 2), (3,))[r % 4 - 1])

            schedule(act, step)

        @block.tensor
        def _(pe):
            def prep(k, r, part, halfway=lambda: None):
                g = (r // 4) % 2
                if part == 0:
                    pe.wait_ge(xn_done, gcnt(k, r))
                    if not isint(k) or r >= 4:
                        pe.wait_ge(v_hi, gcnt(k, r - 4))
                        pe.wait_ge(v_lo, gcnt(k, r - 4))
                    for c in range(DC):
                        if c == 1:
                            halfway()
                        for b in range(GB):
                            i = pe.transpose(ps_g[:, c, b * P:(b + 1) * P], xn[:, b, c * P:(c + 1) * P], ident)
                    i.then_inc(xT_ps, 1)
                if part in (1, 2):
                    src = xT_hl if part == 1 else c_hl
                    if part == 1:
                        pe.wait_ge(xT_hi, gcnt(k, r))
                        pe.wait_ge(xT_lo, gcnt(k, r))
                    else:
                        pe.wait_ge(c_hi, gcnt(k, r))
                        pe.wait_ge(c_lo, gcnt(k, r))
                        pe.wait_ge(q_hi, gcnt(k, r))
                        pe.wait_ge(q_lo, gcnt(k, r))
                    for co in range(DC):
                        if co == 1:
                            halfway()
                        n = 0
                        for ci in range(DC):
                            for a, b in ((0, 0), (0, 1), (1, 0)):
                                i = pe.matmul(ps_g[:, co], w_hl[:, part - 1, a, ci, co * P:(co + 1) * P], src[:, b, ci],
                                              start=(n == 0), stop=(n == 3 * DC - 1))
                                n += 1
                    i.then_inc(q_ps if part == 1 else k_ps, 1)
                if part == 3:
                    pe.wait_ge(k_hi, gcnt(k, r))
                    pe.wait_ge(k_lo, gcnt(k, r))
                    for b in range(GB):
                        dst = ps_g[:, b // 2, (b % 2) * D:(b % 2 + 1) * D]
                        n = 0
                        if b == 2:
                            halfway()
                        pe.matmul(dst, one_r[:, :], bv_hl[:, :], start=True, stop=False)
                        for ci in range(DC):
                            for a, w in ((0, 0), (0, 1), (1, 0)):
                                i = pe.matmul(dst, c_hl[:, a, ci, b * P:(b + 1) * P], w_hl[:, 2, w, ci],
                                              start=False, stop=(n == 3 * DC - 1))
                                n += 1
                    i.then_inc(v_ps, 1)

            pe.wait_ge(const_in, 16)
            pe.wait_ge(init_act, 4)
            pe.wait_ge(init_dve, 3)
            for part in range(4):
                prep(0, 0, part)

            def scores(k, r):
                g, b = (r // 4) % 2, r % 4
                if b == 0:
                    pe.wait_ge(qd_done, gcnt(k, r))
                    pe.wait_ge(k_hi, gcnt(k, r))
                    pe.wait_ge(k_lo, gcnt(k, r))
                if not isint(k) or r >= 1:
                    pe.wait_ge(s_sub, cnt(k, r - 1))
                if not isint(k) or r >= 3:
                    pe.wait_ge(lg_done, cnt(k, r - 3))
                for half in range(2):
                    rows = slice(64 * half, 64 * half + 64)
                    bank = ps_s[:, half].rearrange("p (n s) -> p n s", s=SLOT)
                    pe.matmul(bank[:, :, 0:KW], identb[:, :], bandb[:, :].rearrange("p (n s) -> p n s", s=SLOT)[:, :, 0:KW],
                              start=True, stop=False)
                    for par in range(2):
                        for c in range(DC):
                            for j in range(2):
                                qb = 2 * j + par
                                for a, w in ((0, 0), (0, 1), (1, 0)):
                                    blk = b * 4 + qb
                                    i = pe.matmul(bank[:, par * 4 + c * 2 + j, 0:KW], qd[rows, g, a, c, blk].rearrange("p v s -> p (v s)"),
                                                  kT[rows, g, w, c, b, qb * QB:qb * QB + KW],
                                                  start=False, stop=(par == 1 and c == 1 and j == 1 and a == 1))
                i.then_inc(s_ps, 1)

            def turn_p(k, r):
                pe.wait_ge(e_done, cnt(k, r))
                if not isint(k) or r >= 1:
                    pe.wait_ge(o_done, cnt(k, r - 1))
                for n in range(8):
                    i = pe.transpose(ps_p[:, n // 4, (n % 4) * P:(n % 4 + 1) * P],
                                     es[:, r % 2, 2 * n:2 * n + 2].rearrange("p a s -> p (a s)"), ident)
                    if n % 4 == 3:
                        i.then_inc(pT_ps, 1)

            def turn_o(k, r):
                o = osb[:, :, :].rearrange("p (j a c h) d -> p j a (c h d)", j=2, h=2, a=2)
                for qb in range(4):
                    i = pe.transpose(ps_o[0:64, qb * P:(qb + 1) * P], o[:, qb // 2, qb % 2], ident)
                i.then_inc(oT_ps, 1)

            def heads_out(k, r):
                g, b = (r // 4) % 2, r % 4
                if b == 0:
                    pe.wait_ge(v_shift[g], 16 * (k + r // 8 + 1))
                pe.wait_ge(pT_hi, cnt(k, r, 2))
                pe.wait_ge(pT_lo, cnt(k, r, 2))
                for n in range(8):
                    half, par, c = n // 4, (n // 2) % 2, n % 2
                    d0 = c * P + half * 64
                    m = par * 4 + c * 2 + half
                    for a, w in ((0, 0), (0, 1), (1, 0)):
                        for j in range(2):
                            rows = slice(64 * j, 64 * j + 64)
                            i = pe.matmul(ps_p[:, j, m * 64:(m + 1) * 64], pT[rows, a, n], vw[rows, g, par, w, b, d0:d0 + 64],
                                          start=(a == 0 and w == 0), stop=(a == 1))
                i.then_inc(o_ps, 1)

            def project_o(k, r):
                pe.wait_ge(oT_done, cnt(k, r))
                if not isint(k) or r >= 1:
                    pe.wait_ge(x2T_done, cnt(k, r - 1))
                for v in range(2):
                    i = pe.matmul(ps_m[:, 0:D], oT[:, v].rearrange("p q s -> p (q s)"), wo_sb[:, v], start=(v == 0), stop=(v == 1))
                i.then_inc(y_ps, 1)

            def turn_x2(k, r):
                for c in range(DC):
                    i = pe.transpose(ps_m[:, D + c * P:D + (c + 1) * P], xn2[:, r % 2, c * P:(c + 1) * P], ident)
                i.then_inc(x2T_ps, 1)

            def route(k, r):
                pe.wait_ge(x2T_done, cnt(k, r))
                if not isint(k) or r >= 1:
                    pe.wait_ge(lg_done, cnt(k, r - 1))
                for c in range(DC):
                    i = pe.matmul(ps_s[:, 0, SLOT - E:SLOT], x2T[:, c], wg_sb[:, c], start=(c == 0), stop=(c == DC - 1))
                i.then_inc(lg_ps, 1)

            def step(k, r):
                if valid(k, r, 0):
                    scores(k, r)
                def before_turn_o():
                    if valid(k, r, 1):
                        pe.wait_ge(o_done, cnt(k, r - 1))
                        if valid(k, r, 2):
                            pe.wait_ge(oT_done, cnt(k, r - 2))

                if has_next(k, r):
                    prep(k, r + 4, r % 4, before_turn_o)
                else:
                    before_turn_o()
                if valid(k, r, 1):
                    turn_o(k, r - 1)
                if valid(k, r, 2):
                    pe.wait_ge(xn2_done, cnt(k, r - 2))
                    turn_x2(k, r - 2)
                if valid(k, r, 0):
                    turn_p(k, r)
                if valid(k, r, 1):
                    project_o(k, r - 1)
                if valid(k, r, 2):
                    route(k, r - 2)
                if valid(k, r, 0):
                    heads_out(k, r)

            schedule(pe, step)

        @block.vector
        def _(dve):
            dve.memset(one_r[:, :].bitcast(F32), 1.0)
            dve.memset(bv_hl[:, :].bitcast(F32), 0.0).then_inc(bv_zero, 1)
            for g in range(2):
                dve.memset(kT[:, g, :, :, :, 0:KPAD].rearrange("p a c b s -> p (a c b) s"), 0.0)
                dve.memset(vw[0:QB, g, 0].rearrange("p a b d -> p (a b d)"), 0.0)
            dve.wait_ge(const_in, 16)
            dve.tensor_copy(identb[:, :], ident)
            dve.tensor_copy(bandb[:, :], cst[:, C_BAND:C_BAND + 512]).then_inc(init_dve, 1)
            dve.wait_ge(init_act, 2)
            dve.tensor_tensor(w_hl[:, :, 1], w_raw[:, :], w_hl[:, :, 0].bitcast(F32), ALU.subtract).then_inc(init_dve, 1)
            dve.wait_ge(init_act, 4)
            dve.tensor_tensor(bv_hl[32:33, :], bv_raw[32:33, :], bv_hl[32:33, :].bitcast(F32), ALU.subtract).then_inc(init_dve, 1)

            def norm_in(k, r, batches):
                g = (r // 4) % 2
                dve.wait_ge(x_in[g], 16 * (k + r // 8 + 1))
                for b in batches:
                    i = dve.bn_stats(stat[:, b], xg[:, g, b])
                if GB - 1 in batches:
                    i.then_inc(dve_ln, 1)

            def aggregate_in(k, r):
                for b in range(GB):
                    i = dve.bn_aggr(mv[:, b], stat[:, b])
                i.then_inc(dve_ln, 1)

            def prep(k, r, part):
                g = (r // 4) % 2
                if part == 0:
                    dve.wait_ge(xT_hi, gcnt(k, r))
                    dve.tensor_tensor(xT_hl[:, 1], ps_g[:, :, :], xT_hl[:, 0].bitcast(F32), ALU.subtract).then_inc(xT_lo, 1)
                if part == 1:
                    dve.wait_ge(q_hi, gcnt(k, r))
                    for c in range(DC):
                        i = dve.scalar_tensor_tensor(out=q_hl[:, 1, c], in0=ps_g[:, c], scalar=bqk[:, 0, c:c + 1], in1=q_hl[:, 0, c],
                                                     op0=ALU.add, op1=ALU.subtract)
                    i.then_inc(q_lo, 1)
                if part == 2:
                    dve.wait_ge(k_hi, gcnt(k, r))
                    for c in range(DC):
                        i = dve.scalar_tensor_tensor(out=kT[:, g, 1, c, :, KPAD:KS], in0=ps_g[:, c].rearrange("p (b s) -> p b s", b=GB),
                                                     scalar=bqk[:, 1, c:c + 1], in1=kT[:, g, 0, c, :, KPAD:KS],
                                                     op0=ALU.add, op1=ALU.subtract)
                    i.then_inc(k_lo, 1)
                if part == 3:
                    dve.wait_ge(v_hi, gcnt(k, r))
                    dve.tensor_tensor(vw[:, g, 1, 1], ps_g[:, :, :].rearrange("p a (b d) -> p (a b) d", d=D), vw[:, g, 1, 0],
                                      ALU.subtract).then_inc(v_lo, 1)

            norm_in(0, 0, range(GB))
            dve.wait_ge(dve_ln, 1)
            aggregate_in(0, 0)
            prep(0, 0, 0)
            norm_in(0, 4, range(GB))
            dve.wait_ge(dve_ln, 3)
            aggregate_in(0, 4)
            for part in range(1, 4):
                prep(0, 0, part)

            def soft(k, r):
                sc = ps_s[:, :, :].rearrange("p a (n s) -> p (a n) s", s=SLOT)[:, :, 0:KW]
                dve.wait_ge(s_ps, cnt(k, r))
                dve.tensor_reduce(mx[:, :], sc, AX, ALU.max).then_inc(mx_done, 1)
                dve.wait_ge(mx_done, cnt(k, r))
                if r >= 2 or not isint(k):
                    dve.wait_ge(pT_ps, cnt(k, r - 2, 2))
                else:
                    dve.wait_ge(init_pool, 3)
                dve.tensor_tensor(es[:, r % 2, :, SLOT - KW:SLOT], sc, mx[:, :].unsqueeze(2).to_broadcast([P, 16, KW]),
                                  ALU.subtract).then_inc(s_sub, 1)

            def low_p(k, r):
                for h in range(2):
                    dve.wait_ge(pT_hi, cnt(k, r, 2) - 1 + h)
                    dve.tensor_tensor(pT[:, 1, 4 * h:4 * h + 4], ps_p[:, h].rearrange("p (b n) -> p b n", n=P), pT[:, 0, 4 * h:4 * h + 4],
                                      ALU.subtract).then_inc(pT_lo, 1)

            def sum_weights(k, r):
                dve.wait_ge(e_done, cnt(k, r))
                dve.tensor_reduce(esum[:, :], es[:, r % 2, :, SLOT - KW:SLOT], AX, ALU.add).then_inc(sum_done, 1)

            def invert_sums(k, r):
                dve.wait_ge(sum_done, cnt(k, r))
                if not isint(k) or r >= 1:
                    dve.wait_ge(o_done, cnt(k, r - 1))
                dve.reciprocal(rinv[:, :, :, :].rearrange("p j x h -> p h x j"), esum[:, :].rearrange("p (h x j) -> p h x j", h=2, j=2)).then_inc(rinv_done, 1)

            def take_o(k, r):
                dve.wait_ge(rinv_done, cnt(k, r))
                dve.wait_ge(o_ps, cnt(k, r))
                if not isint(k) or r >= 1:
                    dve.wait_ge(oT_ps, cnt(k, r - 1))
                o = ps_p[:, :, :].rearrange("p a (n d) -> p (a n) d", d=64)
                for v in range(V4):
                    rows = slice(32 * v, 32 * v + 32)
                    i = dve.tensor_tensor(osb[rows], o[rows, :, v * HD:(v + 1) * HD],
                                          rinv[rows].rearrange("p j x h -> p (j x h)").unsqueeze(2).to_broadcast([32, 16, HD]), ALU.mult)
                i.then_inc(o_done, 1)

            def residual(k, r):
                b, g = r % 2, (r // 4) % 2
                dve.wait_ge(y_ps, cnt(k, r))
                dve.wait_ge(xb_done, gcnt(k, r))
                if not isint(k) or r >= 2:
                    dve.wait_ge(x1_out[b], 16 * (4 * k + r // 2))
                    dve.wait_ge(xn2_done, cnt(k, r - 2))
                dve.scalar_tensor_tensor(out=x1[:, b], in0=ps_m[:, 0:D], scalar=gtanh[:, 0:1], in1=xb[:, g, r % 4],
                                         op0=ALU.mult, op1=ALU.add).then_inc(x1_done, 1)

            def stats2(k, r):
                b = r % 2
                dve.wait_ge(x1_done, cnt(k, r))
                dve.bn_stats(stat2[:, :], x1[:, b]).then_inc(st2_done, 1)

            def aggregate2(k, r):
                dve.bn_aggr(mv2[:, :], stat2[:, :]).then_inc(st2_done, 1)

            def keep_logits(k, r):
                dve.wait_ge(lg_ps, cnt(k, r))
                dve.tensor_copy(logits[:, bass.ds(8 * k + r, 1)].rearrange("p a e -> p (a e)"), ps_s[:, 0, SLOT - E:SLOT]).then_inc(lg_done, 1)

            def step(k, r):
                if valid(k, r, 2):
                    dve.wait_ge(st2_done, cnt(k, r - 2, 2) - 1)
                    if valid(k, r, 3):
                        dve.wait_ge(shift2_done, cnt(k, r - 3))
                if valid(k, r, 1):
                    take_o(k, r - 1)
                if valid(k, r, 2):
                    aggregate2(k, r - 2)
                if valid(k, r, 0):
                    soft(k, r)
                if r % 4 == 0 and ahead(k, r):
                    norm_in(k, r + 8, (0, 1))
                if r % 4 == 1 and ahead(k, r):
                    norm_in(k, r + 7, (2, 3))
                    dve.wait_ge(dve_ln, gcnt(k, r + 7, 2) - 1)
                    dve.wait_ge(shift_done, gcnt(k, r + 3))
                if valid(k, r, 0):
                    sum_weights(k, r)
                if r % 4 == 1 and ahead(k, r):
                    aggregate_in(k, r + 7)
                if valid(k, r, 0):
                    invert_sums(k, r)
                    low_p(k, r)
                if valid(k, r, 1):
                    residual(k, r - 1)
                if valid(k, r, 2):
                    keep_logits(k, r - 2)
                if valid(k, r, 1):
                    stats2(k, r - 1)
                if has_next(k, r):
                    prep(k, r + 4, r % 4)

            schedule(dve, step)
            dve.wait_ge(lg_done, B)

        att.close()
        route_and_experts(nc, ctx, cst, gtanh, logits, xn_rows, w1, w2, out)


def route_and_experts(nc, ctx, cst, gtanh, logits, xn_rows, w1, w2, out):
    def sb(name, shape, dt=F32):
        return ctx.enter_context(nc.sbuf_tensor(name, shape, dt))

    def sem(name):
        return ctx.enter_context(nc.semaphore(name))

    ident = cst[:, C_ID:C_ID + P]
    KT = TOPK * B

    idx_all = sb("idx_all", [P, ST + SPARE], I32)
    p_all = sb("p_all", [P, ST + SPARE])
    w_raw = sb("we_raw", [P, 2, DC * F])
    w_hl = sb("we_hl", [P, 2, 2, 2, DC * F], F32R)
    NPIECE = 8
    PIECE = 2 * DC * F // NPIECE

    raw_in, w_hi, w_lo = sem("raw_in"), sem("w_hi"), sem("w_lo")

    w1_e = w1.rearrange("e (c p) f -> e p c f", p=P)
    w2_e = w2.rearrange("e (c p) d -> e p c d", p=P)

    def load_weights(sp, e):
        sp.dma_start(w_raw[:, 0].rearrange("p (c f) -> p c f", c=DC), w1_e[e]).then_inc(raw_in, 16)
        sp.dma_start(w_raw[:, 1].rearrange("p (c d) -> p c d", c=FC), w2_e[e]).then_inc(raw_in, 16)

    def piece(t, n):
        return t.rearrange("p l n -> p (l n)")[:, n * PIECE:(n + 1) * PIECE]

    def split_hi(act, buf, n):
        return act.activation(piece(w_hl[:, buf, 0], n), piece(w_raw[:, :], n), ACT.Copy)

    def split_lo(eng, buf, n):
        return eng.tensor_tensor(piece(w_hl[:, buf, 1], n), piece(w_raw[:, :], n), piece(w_hl[:, buf, 0], n).bitcast(F32), ALU.subtract)

    with ExitStack() as rt:
        def sr(name, shape, dt=F32):
            return rt.enter_context(nc.sbuf_tensor(name, shape, dt))

        oh = sr("oh", [P, TOPK, B, E])
        lg2 = sr("lg2", [P, B, E])
        tmp = sr("tmp", [P, B, E])
        top = sr("top", [P, TOPK, B])
        eid = sr("eid", [P, TOPK, B])
        io8 = sr("io8", [P, E])
        dlt, ex, den, inv = sr("dlt", [P, B]), sr("ex", [P, B]), sr("den", [P, B]), sr("inv", [P, B])
        prob = sr("prob", [P, TOPK, B])
        tot = sr("tot", [P, KT, E])
        sc = [sr(f"scan{i}", [P, KT, E]) for i in range(2)]
        rank = sr("rank", [P, KT])
        valid_t = sr("valid_t", [P, KT])
        slot_f = sr("slot_f", [P, KT])
        slot_i, hi_i, lo_i = sr("slot_i", [P, KT], I32), sr("hi_i", [P, KT], I32), sr("lo_i", [P, KT], I32)
        hi_f, lo_f = sr("hi_f", [P, KT]), sr("lo_f", [P, KT])
        tokv, pval = sr("tokv", [P, KT]), sr("pval", [P, KT])
        NB = 4
        at_row = sr("at_row", [P, NB, P])
        tok_row, prob_row = sr("tok_row", [P, NB, P]), sr("prob_row", [P, NB, P])
        at_col = sr("at_col", [P, NB, ST])
        ps_pre = rt.enter_context(nc.psum_tensor("ps_pre", [P, 2, 512], F32))
        ps_tot = rt.enter_context(nc.psum_tensor("ps_tot", [P, 2, 512], F32))
        ps_tab = rt.enter_context(nc.psum_tensor("ps_tab", [P, 2, 512], F32))
        seq, exp_done, sums_ps = sem("seq"), sem("exp_done"), sem("sums_ps")
        hot_done, hot_used, table_ps = sem("hot_done"), sem("hot_used"), sem("table_ps")
        dlt_done, tok_done, prob_done = sem("dlt_done"), sem("tok_done"), sem("prob_done")

        def bc(ap):
            return ap.unsqueeze(2).to_broadcast([P, B, E])

        block = rt.enter_context(nc.Block())

        @block.sync
        def _(sp):
            load_weights(sp, 0)

        @block.gpsimd
        def _(pool):
            for n in range(NPIECE):
                pool.wait_ge(w_hi, n + 1)
                split_lo(pool, 0, n).then_inc(w_lo, 1)

            def token_row(t, j):
                pool.tensor_tensor(tok_row[:, j], at_row[:, j], tokv[:, bass.ds(t, 1)].to_broadcast([P, P]), ALU.mult).then_inc(tok_done, 1)

            for j in range(NB):
                pool.wait_ge(hot_done, j + 1)
                token_row(j, j)
            with pool.Fori(1, KT // NB) as q:
                for j in range(NB):
                    pool.wait_ge(hot_used, NB * q - NB + j + 1)
                    pool.wait_ge(hot_done, NB * q + j + 1)
                    token_row(NB * q + j, j)

        @block.scalar
        def _(act):
            act.wait_ge(raw_in, 32)
            for n in range(NPIECE):
                split_hi(act, 0, n).then_inc(w_hi, 1)
            act.wait_ge(dlt_done, 1)
            act.activation(ex[:, :], dlt[:, :], ACT.Exp).then_inc(exp_done, 1)

            def weight_row(t, j):
                act.activation(prob_row[:, j], at_row[:, j], ACT.Copy, scale=pval[:, bass.ds(t, 1)]).then_inc(prob_done, 1)

            for j in range(NB):
                act.wait_ge(hot_done, j + 1)
                weight_row(j, j)
            with act.Fori(1, KT // NB) as q:
                for j in range(NB):
                    act.wait_ge(hot_used, NB * q - NB + j + 1)
                    act.wait_ge(hot_done, NB * q + j + 1)
                    weight_row(NB * q + j, j)

        @block.vector
        def _(dve):
            count = [0]

            def then(ins):
                count[0] += 1
                ins.then_inc(seq, 1)
                dve.wait_ge(seq, count[0])

            iota = cst[:, C_E8:C_E8 + E].unsqueeze(1).to_broadcast([P, B, E])
            then(dve.tensor_scalar(io8[:, :], cst[:, C_E8:C_E8 + E], float(E), None, ALU.add))
            src = logits[:, :, :]
            for k in range(TOPK):
                then(dve.tensor_reduce(top[:, k], src, AX, ALU.max))
                then(dve.tensor_tensor(tmp[:, :, :], src, bc(top[:, k]), ALU.is_equal))
                then(dve.scalar_tensor_tensor(out=tmp[:, :, :], in0=tmp[:, :, :], scalar=-float(E),
                                              in1=io8[:, :].unsqueeze(1).to_broadcast([P, B, E]), op0=ALU.mult, op1=ALU.add))
                then(dve.tensor_reduce(eid[:, k], tmp[:, :, :], AX, ALU.min))
                then(dve.tensor_tensor(oh[:, k], iota, bc(eid[:, k]), ALU.is_equal))
                if k == 0:
                    then(dve.scalar_tensor_tensor(out=lg2[:, :, :], in0=oh[:, 0], scalar=-3.0e38, in1=src, op0=ALU.mult, op1=ALU.add))
                    src = lg2[:, :, :]
            dve.tensor_tensor(dlt[:, :], top[:, 1], top[:, 0], ALU.subtract).then_inc(dlt_done, 1)
            dve.wait_ge(exp_done, 1)
            then(dve.tensor_scalar(den[:, :], ex[:, :], 1.0, None, ALU.add))
            then(dve.reciprocal(inv[:, :], den[:, :]))
            then(dve.tensor_scalar(prob[:, 0], inv[:, :], gtanh[:, 1:2], None, ALU.mult))
            then(dve.tensor_tensor(prob[:, 1], prob[:, 0], ex[:, :], ALU.mult))

            dve.wait_ge(sums_ps, 1)
            then(dve.tensor_copy(tot[:, :, :].rearrange("p t e -> p (t e)"), ps_tot[:, :, :].rearrange("p a b -> p (a b)")))
            a, d = tot, 1
            n = 0
            while d < KT:
                b = sc[n % 2]
                dve.tensor_copy(b[:, 0:d], a[:, 0:d])
                then(dve.tensor_tensor(b[:, d:KT], a[:, d:KT], a[:, 0:KT - d], ALU.add))
                a, d, n = b, 2 * d, n + 1
            b = sc[n % 2]
            then(dve.tensor_tensor(b[:, :, :], a[:, :, :], tot[:, :, :], ALU.subtract))
            flat = b[:, :, :].rearrange("p t e -> p (t e)")
            then(dve.tensor_tensor(flat, ps_pre[:, :, :].rearrange("p a b -> p (a b)"), flat, ALU.add))
            then(dve.tensor_tensor(b[:, :, :], b[:, :, :], oh[:, :, :, :].rearrange("p k t e -> p (k t) e"), ALU.mult))
            then(dve.tensor_reduce(rank[:, :], b[:, :, :], AX, ALU.add))
            then(dve.tensor_scalar(valid_t[:, :], rank[:, :], float(CAP), None, ALU.is_lt))
            then(dve.scalar_tensor_tensor(out=slot_f[:, :], in0=eid[:, :, :].rearrange("p k t -> p (k t)"), scalar=float(CAP), in1=rank[:, :],
                                          op0=ALU.mult, op1=ALU.add))
            then(dve.tensor_copy(slot_i[:, :], slot_f[:, :]))
            dve.tensor_scalar(hi_i[:, :], slot_i[:, :], 7, None, ALU.arith_shift_right)
            then(dve.tensor_scalar(lo_i[:, :], slot_i[:, :], P - 1, None, ALU.bitwise_and))
            then(dve.tensor_copy(hi_f[:, :], hi_i[:, :]))
            dve.tensor_copy(lo_f[:, :], lo_i[:, :])
            then(dve.scalar_tensor_tensor(out=hi_f[:, :], in0=hi_f[:, :], scalar=1.0, in1=valid_t[:, :], op0=ALU.add, op1=ALU.mult))
            dve.tensor_scalar(hi_f[:, :], hi_f[:, :], -1.0, None, ALU.add)
            dve.tensor_tensor(tokv[:, :], cst[:, C_TOK:C_TOK + KT], rank[:, :], ALU.subtract)
            then(dve.tensor_tensor(pval[:, :], prob[:, :, :].rearrange("p k t -> p (k t)"), valid_t[:, :], ALU.mult))

            def hot(t, j):
                dve.tensor_scalar(at_row[:, j], cst[:, C_I128:C_I128 + P], lo_f[:, bass.ds(t, 1)], None, ALU.is_equal)
                dve.tensor_scalar(at_col[:, j], cst[:, C_I160:C_I160 + ST], hi_f[:, bass.ds(t, 1)], None, ALU.is_equal).then_inc(hot_done, 1)

            for j in range(NB):
                hot(j, j)
            with dve.Fori(1, KT // NB) as q:
                for j in range(NB):
                    dve.wait_ge(hot_used, NB * q - NB + j + 1)
                    hot(NB * q + j, j)
            dve.wait_ge(table_ps, 1)
            dve.tensor_copy(p_all[:, 0:ST], ps_tab[:, 1, 0:ST])
            dve.memset(p_all[:, ST:ST + SPARE], 0.0)
            dve.tensor_tensor(idx_all[:, 0:ST], ps_tab[:, 0, 0:ST], cst[:, C_PB:C_PB + ST], ALU.add)
            dve.tensor_copy(idx_all[:, ST:ST + SPARE], cst[:, C_PB + ST:C_PB + ST + SPARE])

        @block.tensor
        def _(pe):
            pe.wait_ge(dlt_done, 1)
            for k in range(TOPK):
                rows = oh[:, k].rearrange("p t e -> p (t e)")
                pe.matmul(ps_pre[:, k], cst[:, C_TRI:C_TRI + P], rows, start=True, stop=True)
                i = pe.matmul(ps_tot[:, k], cst[:, C_ONE:C_ONE + P], rows, start=True, stop=True)
            i.then_inc(sums_ps, 1)

            def place(n, j, first, last):
                pe.wait_ge(tok_done, n)
                pe.matmul(ps_tab[:, 0, 0:ST], tok_row[:, j], at_col[:, j], start=first, stop=last)
                pe.wait_ge(prob_done, n)
                return pe.matmul(ps_tab[:, 1, 0:ST], prob_row[:, j], at_col[:, j], start=first, stop=last)

            for j in range(NB):
                place(j + 1, j, j == 0, False).then_inc(hot_used, 1)
            with pe.Fori(1, KT // NB - 1) as q:
                for j in range(NB):
                    place(NB * q + j + 1, j, False, False).then_inc(hot_used, 1)
            for j in range(NB):
                i = place(KT - NB + j + 1, j, False, j == NB - 1)
            i.then_inc(table_ps, 1)

    RM = 2 * MTE
    idx_st = sb("idx_st", [P, RM, SUB], I32)
    p_st = sb("p_st", [P, RM, SUB])
    rows_in = sb("rows_in", [P, 2, SUB, D])
    xT = sb("xe_T", [P, 2, 2, DC, MT], F32R)
    r_sb = sb("r_sb", [P, 2, MT])
    sq_sb = sb("sq_sb", [P, 2, MT])
    HR = 4
    h_hl = sb("h_hl", [P, HR, 2, MT], F32R)
    y_sb = sb("y_sb", [P, 2, SUB, D])
    ps_x = ctx.enter_context(nc.psum_tensor("pe_x", [P, DC, 512], F32))
    ps_h = ctx.enter_context(nc.psum_tensor("pe_h", [P, 2, 512], F32))
    ps_y = ctx.enter_context(nc.psum_tensor("pe_y", [P, SUB, 512], F32))

    gate_t = sb("gate_t", [P, 3])
    staged, gate_done = sem("staged"), sem("gate_done")
    g_in = [sem(f"g_in{i}") for i in range(2)]
    xe_ps, xe_hi, xe_lo = sem("xe_ps"), sem("xe_hi"), sem("xe_lo")
    h_ps, relu_done, sq_done, h_hi, h_lo, g2_done = sem("h_ps"), sem("relu_done"), sem("sq_done"), sem("h_hi"), sem("h_lo"), sem("g2_done")
    ye_ps, ye_sb, y_out = sem("ye_ps"), sem("ye_sb"), sem("y_out")

    X0 = 1
    GATES = 5 * RM + 1

    def mc(k, r):
        return k * RM + (r + 1)

    def nch(k, r, f):
        return k * (RM * FC) + (r * FC + f + 1)

    block = ctx.enter_context(nc.Block())

    @block.sync
    def _(sp):
        with sp.Fori(0, E // 2) as k:
            for h in range(2):
                sp.wait_ge(w_hi, (2 * k + h + 1) * NPIECE)
                sp.wait_ge(w_lo, (2 * k + h + 1) * NPIECE)
                load_weights(sp, (2 * k + h + 1) % E)
        sp.wait_ge(raw_in, 32 * (E + 1))

    @block.gpsimd
    def _(pool):
        def gate(k, r, n):
            pool.wait_ge(gate_done, k * GATES + (5 * r + n + 1))
            pool.tensor_tensor(gate_t[:, 0:1], ident[:, 0:1], ident[:, 0:1], ALU.add).then_inc(gate_done, 1)

        def gather(k, r, first=False):
            b = r % 2
            pool.wait_ge(staged, mc(k, r))
            if not first:
                pool.wait_ge(xe_ps, X0 + mc(k, r) - 2)
                gate(k, r - 2, 0)
            for s in range(SUB):
                pool.indirect_dma_start(rows_in[:, b, s], None, xn_rows,
                                        bass.IndirectOffsetOnAxis(ap=idx_st[:, r % RM, s:s + 1], axis=0)).then_inc(g_in[b], 16)

        def scatter(k, r):
            for s in range(SUB):
                pool.wait_ge(ye_sb, X0 + 4 * mc(k, r) - 3 + s)
                if r % MTE == 0 and r > 0 and s == 0:
                    pool.wait_ge(y_out, 64 * mc(k, r - 1))
                gate(k, r, s + 1)
                pool.indirect_dma_start(out, bass.IndirectOffsetOnAxis(ap=idx_st[:, r % RM, s:s + 1], axis=0),
                                        y_sb[:, r % 2, s], None, compute_op=ALU.add).then_inc(y_out, 16)

        pool.tensor_tensor(gate_t[:, 0:1], ident[:, 0:1], ident[:, 0:1], ALU.add).then_inc(gate_done, 1)
        gather(0, 0, True)
        gather(0, 1, True)
        with pool.Fori(0, E // 2) as k:
            for r in range(RM):
                gather(k, r + 2)
                if r % MTE in (1, 2):
                    for n in range(4):
                        m = (r % MTE - 1) * 4 + n
                        pool.wait_ge(w_hi, (2 * k + r // MTE + 1) * NPIECE + m + 1)
                        split_lo(pool, 1 - r // MTE, m).then_inc(w_lo, 1)
                scatter(k, r)
            pool.wait_ge(y_out, 64 * mc(k, RM - 1))
            gate(k, RM, 0)
        pool.wait_ge(y_out, 16 * ST)
        pool.wait_ge(g_in[0], 64 * (NSLOT // MT // 2 + 1))
        pool.wait_ge(g_in[1], 64 * (NSLOT // MT // 2 + 1))

    @block.scalar
    def _(act):
        def x_hi(k, r):
            act.wait_ge(xe_ps, X0 + mc(k, r))
            act.activation(xT[:, r % 2, 0], ps_x[:, :, :], ACT.Copy).then_inc(xe_hi, 1)

        def evac(k, r):
            for s in range(SUB):
                if s < SUB - 1:
                    act.wait_ge(ye_ps, (SUB - 1) * (mc(k, r) - 1) + s + 1)
                else:
                    act.wait_ge(g2_done, nch(k, r, FC - 1))
                act.activation(y_sb[:, r % 2, s], ps_y[:, s, 0:D], ACT.Copy, scale=p_st[:, r, s:s + 1]).then_inc(ye_sb, 1)

        act.activation(gate_t[:, 2:3], ident[:, 0:1], ACT.Copy).then_inc(ye_sb, X0)
        x_hi(0, 0)
        with act.Fori(0, E // 2) as k:
            for r in range(RM):
                for f in range(FC):
                    n = r * FC + f
                    if f == 2 and r > 0:
                        if r > 1:
                            act.wait_ge(y_out, 64 * mc(k, r - 3))
                        else:
                            act.wait_ge(gate_done, X0 + k * GATES)
                        evac(k, r - 1)
                    act.wait_ge(h_ps, nch(k, r, f))
                    if n >= 2:
                        act.wait_ge(sq_done, nch(k, r, f) - 2)
                    act.activation(r_sb[:, f % 2], ps_h[:, f % 2], ACT.Relu).then_inc(relu_done, 1)
                    act.wait_ge(relu_done, nch(k, r, f))
                    if n >= HR:
                        act.wait_ge(g2_done, nch(k, r, f) - HR)
                    act.activation(h_hl[:, f % HR, 0], r_sb[:, f % 2], ACT.Square).then_inc(h_hi, 1)
                    if f == 5:
                        x_hi(k, r + 1)
                    if r % MTE == 1:
                        if f == 0:
                            act.wait_ge(raw_in, 32 * (2 * k + r // MTE + 2))
                        split_hi(act, 1 - r // MTE, f).then_inc(w_hi, 1)
            act.wait_ge(y_out, 64 * mc(k, RM - 3))
            evac(k, RM - 1)

    @block.tensor
    def _(pe):
        def turn(k, r):
            b = r % 2
            pe.wait_ge(g_in[b], 64 * (MTE * k + r // 2 + 1))
            if not (isinstance(k, int) and r == 0):
                pe.wait_ge(xe_lo, mc(k, r) - 1)
            for c in range(DC):
                for s in range(SUB):
                    i = pe.transpose(ps_x[:, c, s * P:(s + 1) * P], rows_in[:, b, s, c * P:(c + 1) * P], ident)
            i.then_inc(xe_ps, 1)

        def first_layer(k, r, f):
            e = r // MTE
            if f == 0:
                pe.wait_ge(xe_hi, mc(k, r))
                pe.wait_ge(xe_lo, mc(k, r))
                if r % MTE == 0:
                    pe.wait_ge(w_hi, (2 * k + e + 1) * NPIECE)
                    pe.wait_ge(w_lo, (2 * k + e + 1) * NPIECE)
            if r * FC + f >= 2:
                pe.wait_ge(relu_done, nch(k, r, f) - 2)
            n = 0
            for c in range(DC):
                for w, a in ((0, 0), (0, 1), (1, 0)):
                    i = pe.matmul(ps_h[:, f % 2], w_hl[:, e, w, 0, c * F + f * P:c * F + (f + 1) * P], xT[:, r % 2, a, c],
                                  start=(n == 0), stop=(n == 3 * DC - 1))
                    n += 1
            i.then_inc(h_ps, 1)

        def second_layer(k, r, f):
            e = r // MTE
            pe.wait_ge(h_hi, nch(k, r, f))
            pe.wait_ge(h_lo, nch(k, r, f))
            for s in range(SUB):
                if f == 0 and r > 0:
                    pe.wait_ge(ye_sb, X0 + 4 * mc(k, r - 1) - 3 + s)
                if f == 0 and r == 0 and s == 0:
                    pe.wait_ge(ye_sb, X0 + k * (4 * RM))
                for a, w in ((0, 0), (0, 1), (1, 0)):
                    i = pe.matmul(ps_y[:, s, 0:D], h_hl[:, f % HR, a, s * P:(s + 1) * P], w_hl[:, e, w, 1, f * D:(f + 1) * D],
                                  start=(f == 0 and a == 0 and w == 0), stop=(f == FC - 1 and a == 1))
                if f == FC - 1 and s < SUB - 1:
                    i.then_inc(ye_ps, 1)
            i.then_inc(g2_done, 1)

        LAG = 2
        pe.transpose(ps_h[:, 0, 0:P], ident, ident).then_inc(xe_ps, X0)
        turn(0, 0)
        with pe.Fori(0, E // 2) as k:
            for r in range(RM):
                for f in range(FC):
                    first_layer(k, r, f)
                    if f == 4:
                        turn(k, r + 1)
                    n = r * FC + f - LAG
                    if n >= 0:
                        second_layer(k, n // FC, n % FC)
            for n in range(RM * FC - LAG, RM * FC):
                second_layer(k, n // FC, n % FC)

    @block.vector
    def _(dve):
        def stage(k, r):
            dve.tensor_copy(p_st[:, r % RM], p_all[:, bass.ds((k * RM + r) * SUB, SUB)])
            dve.tensor_copy(idx_st[:, r % RM], idx_all[:, bass.ds((k * RM + r) * SUB, SUB)]).then_inc(staged, 1)

        def x_lo(k, r):
            dve.wait_ge(xe_hi, mc(k, r))
            dve.tensor_tensor(xT[:, r % 2, 1], ps_x[:, :, :], xT[:, r % 2, 0].bitcast(F32), ALU.subtract).then_inc(xe_lo, 1)

        stage(0, 0)
        stage(0, 1)
        x_lo(0, 0)
        with dve.Fori(0, E // 2) as k:
            for r in range(RM):
                for f in range(FC):
                    n = r * FC + f
                    dve.wait_ge(relu_done, nch(k, r, f))
                    dve.tensor_tensor(sq_sb[:, f % 2], r_sb[:, f % 2], r_sb[:, f % 2], ALU.mult).then_inc(sq_done, 1)
                    dve.wait_ge(sq_done, nch(k, r, f))
                    dve.wait_ge(h_hi, nch(k, r, f))
                    dve.tensor_tensor(h_hl[:, f % HR, 1], sq_sb[:, f % 2], h_hl[:, f % HR, 0].bitcast(F32), ALU.subtract).then_inc(h_lo, 1)
                    if f == 3:
                        stage(k, r + 2)
                    if f == 5:
                        x_lo(k, r + 1)


def pack_constants():
    import numpy as np

    c = np.zeros((P, C_END), np.float32)
    p = np.arange(P)
    c[:, C_ID:C_ID + P] = np.eye(P)
    q = p % QB
    for half_block in range(8):
        par, j = half_block // 4, half_block % 2
        qb = 2 * j + par
        k = np.arange(KW)
        ok = (k[None] >= q[:, None] + 1) & (k[None] <= q[:, None] + W)
        if qb == 0:
            ok &= (k[None] - q[:, None] - 1) <= q[:, None]
        c[:, C_BAND + half_block * SLOT:C_BAND + half_block * SLOT + KW] = np.where(ok, 0.0, NEG)
    c[:, C_VM:C_VM + V4] = ((p[:, None] % 64) // 16) == np.arange(V4)[None]
    c[:, C_TRI:C_TRI + P] = p[:, None] < p[None]
    c[:, C_ONE:C_ONE + P] = 1.0
    c[:, C_I128:C_I128 + P] = p[None]
    c[:, C_I160:C_I160 + ST] = np.arange(ST)[None]
    c[:, C_TOK:C_TOK + TOPK * B] = (np.arange(TOPK * B)[None] % B) * S + p[:, None] - N
    c[:, C_E8:C_E8 + E] = np.arange(E)[None]
    c[:, C_PB:C_END] = N + (np.arange(ST + SPARE)[None] % STE) * P + p[:, None]
    return c


def kernel(x, ctx_1024, g_xattn, g_ffn, L0_xattn_Wq, L0_xattn_bq, L0_xattn_Wk, L0_xattn_bk, L0_xattn_Wv, L0_xattn_bv,
           L0_xattn_Wo, L0_xattn_bo, L0_ffn_w_g, L0_ffn_c_fc, L0_ffn_c_proj):
    import numpy as np
    import concourse.bacc as bacc
    from concourse.bass_utils import run_bass_kernel_spmd

    def lay(a, *steps):
        a = np.asarray(a)
        for kind, how in steps:
            a = a.reshape(how) if kind == "reshape" else a.transpose(how)
        return np.ascontiguousarray(a)

    arrays = {
        "x": lay(x, ("reshape", (N, D))),
        "ctxT": lay(ctx_1024, ("reshape", (N, D)), ("turn", (1, 0))),
        "gx": lay(g_xattn),
        "gf": lay(g_ffn),
        "wqT": lay(L0_xattn_Wq, ("turn", (1, 0))),
        "bq": lay(L0_xattn_bq, ("reshape", (DC, P)), ("turn", (1, 0))),
        "wkT": lay(L0_xattn_Wk, ("turn", (1, 0))),
        "bk": lay(L0_xattn_bk, ("reshape", (DC, P)), ("turn", (1, 0))),
        "wvT": lay(L0_xattn_Wv, ("turn", (1, 0))),
        "bv": lay(L0_xattn_bv),
        "woP": lay(L0_xattn_Wo, ("turn", (1, 0)), ("reshape", (DC, 2, 2, 2, HD, D)), ("turn", (2, 0, 1, 4, 3, 5)), ("reshape", (P, 2, D))),
        "bo": lay(L0_xattn_bo),
        "wgT": lay(L0_ffn_w_g, ("turn", (1, 0))),
        "w1": lay(L0_ffn_c_fc),
        "w2": lay(L0_ffn_c_proj),
        "consts": pack_constants(),
    }
    nc = bacc.Bacc("TRN2", target_bir_lowering=False, num_devices=1)
    args = [nc.dram_tensor(f"in_{n}", a.shape, mybir.dt.from_np(a.dtype), kind="ExternalInput").ap() for n, a in arrays.items()]
    args.append(nc.dram_tensor("out_rows", (N + TRASH, D), F32, kind="ExternalOutput").ap())
    build_kernel(nc, *args)
    r = run_bass_kernel_spmd(nc, [{f"in_{n}": a for n, a in arrays.items()}], core_ids=[0])
    return r.results[0]["out_rows"][:N].reshape(B, S, D)
```

```python
from contextlib import ExitStack

import concourse.bass as bass
from concourse import mybir

F32 = mybir.dt.float32
F32R = mybir.dt.float32r
F16 = mybir.dt.float16
BF16 = mybir.dt.bfloat16
I32 = mybir.dt.int32
ALU = mybir.AluOpType
ACT = mybir.ActivationFunctionType
AX = mybir.AxisListType.X

P = 128
B, S, D = 64, 128, 256
N = B * S
HD, W = 16, 16
DC = D // P
GB = 4
GT = GB * S
NGROUP = B // GB
V4 = 4
QB = 32
KW = QB + W
SLOT = 64
KPAD = 16
KS = KPAD + S
EPS = 1e-5
E, TOPK, F = 8, 2, 1024
CAP = max(4, int(1.25 * N * TOPK / E))
NSLOT = E * CAP
ST = NSLOT // P
STE = CAP // P
MT = 512
MTE = CAP // MT
SUB = MT // P
FC = F // P
TRASH = CAP
SPARE = 2 * SUB
NEG = -1.0e30

C_ID, C_BAND, C_VM, C_TRI, C_ONE = 0, 128, 128 + 512, 128 + 512 + 4, 128 + 512 + 4 + 128
C_I128 = C_ONE + 128
C_I160 = C_I128 + 128
C_TOK = C_I160 + ST
C_E8 = C_TOK + TOPK * B
C_PB = C_E8 + E
C_END = C_PB + ST + SPARE


def cnt(k, r, per=1):
    return k * (8 * per) + (r + 1) * per


def gcnt(k, r, per=1):
    return k * (2 * per) + (r // 4 + 1) * per


def build_kernel(nc, x, ctxT, gx, gf, wqT, bq, wkT, bk, wvT, bv, woP, bo, wgT, w1, w2, consts, out):
    ctx = ExitStack()
    with ctx:
        def sb(name, shape, dt=F32):
            return ctx.enter_context(nc.sbuf_tensor(name, shape, dt))

        def sem(name):
            return ctx.enter_context(nc.semaphore(name))

        xn_rows = nc.dram_tensor("xn_rows", [N + TRASH, D], F32, kind="Internal").ap()

        cst = sb("cst", [P, C_END])
        ident = cst[:, C_ID:C_ID + P]
        vmask = cst[:, C_VM:C_VM + V4]
        identb = sb("identb", [P, P], BF16)
        bandb = sb("bandb", [P, 512], BF16)
        gates = sb("gates", [P, 2])
        gtanh = sb("gtanh", [P, 2])

        logits = sb("logits", [P, B, E])

        att = ctx.enter_context(ExitStack())

        def sa(name, shape, dt=F32):
            return att.enter_context(nc.sbuf_tensor(name, shape, dt))

        def pa(name, shape, dt=F32):
            return att.enter_context(nc.psum_tensor(name, shape, dt))

        ps_g = pa("ps_g", [P, 2, 512])
        ps_s = pa("ps_s", [P, 2, 512])
        ps_p = pa("ps_p", [P, 2, 512])
        ps_o = pa("ps_o", [P, 512])
        ps_m = pa("ps_m", [P, 512])

        w_raw = sa("w_raw", [P, 3, DC, D])
        w_hl = sa("w_hl", [P, 3, 2, DC, D], F32R)
        wo_sb = sa("wo_sb", [P, 2, D])
        wg_sb = sa("wg_sb", [P, DC, E])
        bqk = sa("bqk", [P, 2, DC])
        bv_raw = sa("bv_raw", [33, D])
        bv_hl = sa("bv_hl", [33, D], F32R)
        one_r = sa("one_r", [33, P], F32R)
        gbo = sa("gbo", [P, D])

        xg = sa("xg", [P, 2, GB, D])
        cg = sa("cg", [P, 2, DC, GT])
        c_hl = sa("c_hl", [P, 2, DC, GT], F32R)
        xn = sa("xn", [P, GB, D])
        xT_hl = sa("xT_hl", [P, 2, DC, GT], F32R)
        stat = sa("stat", [P, GB, 6])
        mv = sa("mv", [P, GB, 2])
        rstd = sa("rstd", [P, GB])
        full = sa("full", [P, DC, GT])
        xb = sa("xb", [P, 2, GB, D])
        q_hl = sa("q_hl", [P, 2, DC, GT], F16)
        qd = sa("qd", [P, 2, 2, DC, GT // QB, V4, QB], F16)
        kT = sa("kT", [P, 2, 2, DC, GB, KS], F16)
        vw = sa("vw", [P, 2, 2, 2, GB, D], F16)

        mx = sa("mx", [P, 16])
        es = sa("es", [P, 2, 16, SLOT])
        esum = sa("esum", [P, 16])
        rinv = sa("rinv", [P, 2, 4, 2])
        pT = sa("pT", [P, 2, 8, P], F16)
        osb = sa("osb", [P, 16, HD])
        oT = sa("oT", [P, 2, 4, QB])
        x1 = sa("x1", [P, 2, D])
        stat2 = sa("stat2", [P, 6])
        mv2 = sa("mv2", [P, 2])
        rstd2 = sa("rstd2", [P, 1])
        xn2 = sa("xn2", [P, 2, D])
        x2T = sa("x2T", [P, DC, P])
        var_e = sa("var_e", [P, GB])
        var_e2 = sa("var_e2", [P, 1])
        mhalf = sa("mhalf", [P, GB])
        eps_t = sa("eps_t", [P, GB])
        zrow = sa("zrow", [P, D])
        mr, shift = sa("mr", [P, GB]), sa("shift", [P, GB])
        mr2, shift2 = sa("mr2", [P, 1]), sa("shift2", [P, 1])

        const_in, weights_in, bias_in = sem("const_in"), sem("weights_in"), sem("bias_in")
        bv_in, wo_in = sem("bv_in"), sem("wo_in")
        init_dve, init_pool, init_act = sem("init_dve"), sem("init_pool"), sem("init_act")
        x_in = [sem(f"x_in{i}") for i in range(2)]
        c_in = [sem(f"c_in{i}") for i in range(2)]
        dve_ln = sem("dve_ln")
        xn_done, xT_ps, xT_hi, xT_lo = sem("xn_done"), sem("xT_ps"), sem("xT_hi"), sem("xT_lo")
        c_hi, c_lo, xb_done = sem("c_hi"), sem("c_lo"), sem("xb_done")
        q_ps, q_hi, q_lo, qd_done = sem("q_ps"), sem("q_hi"), sem("q_lo"), sem("qd_done")
        k_ps, k_hi, k_lo = sem("k_ps"), sem("k_hi"), sem("k_lo")
        v_ps, v_hi, v_lo = sem("v_ps"), sem("v_hi"), sem("v_lo")
        v_shift = [sem(f"v_shift{i}") for i in range(2)]
        s_ps, mx_done, s_sub, e_done = sem("s_ps"), sem("mx_done"), sem("s_sub"), sem("e_done")
        sum_done, bv_zero, qd3_done = sem("sum_done"), sem("bv_zero"), sem("qd3_done")
        pT_ps, pT_hi, pT_lo, rinv_done = sem("pT_ps"), sem("pT_hi"), sem("pT_lo"), sem("rinv_done")
        o_ps, o_done, oT_ps, oT_done = sem("o_ps"), sem("o_done"), sem("oT_ps"), sem("oT_done")
        y_ps, x1_done, st2_done, xn2_done = sem("y_ps"), sem("x1_done"), sem("st2_done"), sem("xn2_done")
        x2T_ps, x2T_done, lg_ps, lg_done = sem("x2T_ps"), sem("x2T_done"), sem("lg_ps"), sem("lg_done")
        x1_out = [sem(f"x1_out{i}") for i in range(2)]
        xn2_out = [sem(f"xn2_out{i}") for i in range(2)]
        zero_out = sem("zero_out")
        full_done = sem("full_done")
        var_done, var2_done = sem("var_done"), sem("var2_done")
        rstd_done, rstd2_done = sem("rstd_done"), sem("rstd2_done")
        mr_done, mr2_done = sem("mr_done"), sem("mr2_done")
        shift_done, shift2_done = sem("shift_done"), sem("shift2_done")

        x_g = x.rearrange("(g b s) d -> g s b d", b=GB, s=S)
        c_g = ctxT.rearrange("(c p) (g t) -> g p c t", p=P, t=GT)

        def isint(k):
            return isinstance(k, int)

        def valid(k, r, lag):
            return not isint(k) or (8 * k + r - lag >= 0 and 8 * k + r - lag < B)

        LAGS = 3

        def schedule(eng, step):
            for r in range(4):
                step(0, r)
            with eng.Fori(0, (NGROUP - 2) // 2) as k:
                for r in range(4, 12):
                    step(k, r)
            for r in range(4, 8 + LAGS):
                step((NGROUP - 2) // 2, r)

        def has_next(k, r):
            return not isint(k) or 8 * k + r < B - 4

        def ahead(k, r):
            return not isint(k) or 8 * k + r < B - 8

        block = att.enter_context(nc.Block())

        @block.sync
        def _(sp):
            sp.dma_start(xg[:, 0], x_g[0]).then_inc(x_in[0], 16)
            sp.dma_start(cst[:, :], consts).then_inc(const_in, 16)
            sp.dma_start(bv_raw[0:1, :], bv.rearrange("(a n) -> a n", a=1)).then_inc(bv_in, 16)
            sp.dma_start(bv_raw[32:33, :], bv.rearrange("(a n) -> a n", a=1)).then_inc(bv_in, 16)
            for n, w in enumerate((wqT, wkT, wvT)):
                sp.dma_start(w_raw[:, n], w.rearrange("(c p) n -> p c n", p=P)).then_inc(weights_in, 16)
            sp.dma_start(cg[:, 0], c_g[0]).then_inc(c_in[0], 16)
            sp.dma_start(bqk[:, 0, :], bq).then_inc(bias_in, 16)
            sp.dma_start(bqk[:, 1, :], bk).then_inc(bias_in, 16)
            sp.dma_start(gates[:, 0:1], gx.rearrange("(a n) -> a n", a=1).broadcast_to([P, 1])).then_inc(bias_in, 16)
            sp.dma_start(gates[:, 1:2], gf.rearrange("(a n) -> a n", a=1).broadcast_to([P, 1])).then_inc(bias_in, 16)
            sp.dma_start(gbo[:, :], bo.rearrange("(a n) -> a n", a=1).broadcast_to([P, D])).then_inc(bias_in, 16)
            sp.dma_start(wo_sb[:, :, :], woP).then_inc(wo_in, 16)
            sp.dma_start(wg_sb[:, :, :], wgT.rearrange("(c p) e -> p c e", p=P)).then_inc(wo_in, 16)
            sp.dma_start(xg[:, 1], x_g[1]).then_inc(x_in[1], 16)
            sp.dma_start(cg[:, 1], c_g[1]).then_inc(c_in[1], 16)
            sp.wait_ge(init_pool, 1)
            for rows in (xn_rows, out):
                sp.dma_start(rows[N:N + TRASH, :].rearrange("(t p) d -> p t d", p=P),
                             zrow[:, :].unsqueeze(1).to_broadcast([P, STE, D])).then_inc(zero_out, 16)

            def shift_v(k, r):
                g = (r // 4) % 2
                for part, done in enumerate((v_hi, v_lo)):
                    sp.wait_ge(done, gcnt(k, r))
                    sp.dma_start(vw[QB:P, g, 0, part], vw[0:P - QB, g, 1, part]).then_inc(v_shift[g], 16)

            def load_ahead(k, r):
                g = (r // 4) % 2
                nxt = (2 * k + r // 4 + 2) % NGROUP
                sp.wait_ge(xn_done, gcnt(k, r))
                sp.wait_ge(xb_done, gcnt(k, r))
                sp.dma_start(xg[:, g], x_g[nxt]).then_inc(x_in[g], 16)
                sp.wait_ge(c_hi, gcnt(k, r))
                sp.wait_ge(c_lo, gcnt(k, r))
                sp.dma_start(cg[:, g], c_g[nxt]).then_inc(c_in[g], 16)

            sp.wait_ge(init_dve, 3)
            shift_v(0, 0)
            load_ahead(0, 0)

            def step(k, r):
                if r % 4 == 3 and has_next(k, r) and ahead(k, r + 1):
                    load_ahead(k, r + 1)
                if valid(k, r, 2):
                    b = r % 2
                    row = (8 * k + r - 2) * S
                    sp.wait_ge(x1_done, cnt(k, r - 2))
                    sp.dma_start(out[bass.ds(row, S), :], x1[:, b]).then_inc(x1_out[b], 16)
                    sp.wait_ge(xn2_done, cnt(k, r - 2))
                    sp.dma_start(xn_rows[bass.ds(row, S), :], xn2[:, b]).then_inc(xn2_out[b], 16)
                if r % 4 == 3 and has_next(k, r):
                    shift_v(k, r + 4)

            schedule(sp, step)
            for b in range(2):
                sp.wait_ge(x1_out[b], 16 * (B // 2))
                sp.wait_ge(xn2_out[b], 16 * (B // 2))
            sp.wait_ge(zero_out, 32)
            for g in range(2):
                sp.wait_ge(x_in[g], 16 * 9)
                sp.wait_ge(c_in[g], 16 * 9)

        @block.gpsimd
        def _(pool):
            pool.memset(zrow[:, :], 0.0).then_inc(init_pool, 1)
            pool.memset(mhalf[:, :], -0.5)
            pool.memset(eps_t[:, :], EPS)
            pool.memset(es[:, :, :, :], 0.0).then_inc(init_pool, 1)
            pool.wait_ge(init_pool, 2)

            def split_c(k, r):
                g = (r // 4) % 2
                pool.wait_ge(c_hi, gcnt(k, r))
                pool.tensor_tensor(c_hl[:, 1], cg[:, g], c_hl[:, 0].bitcast(F32), ALU.subtract).then_inc(c_lo, 1)

            def add_xb(k, r):
                g = (r // 4) % 2
                pool.wait_ge(x_in[g], 16 * (k + r // 8 + 1))
                pool.tensor_tensor(xb[:, g], xg[:, g], gbo[:, :].unsqueeze(1).to_broadcast([P, GB, D]), ALU.add).then_inc(xb_done, 1)

            def low_part(k, r, part):
                g = (r // 4) % 2
                pool.wait_ge(full_done, gcnt(k, r, 3) - 2 + (0, 1, None, 2)[part])
                if part == 0:
                    pool.tensor_tensor(xT_hl[:, 1], full[:, :, :], xT_hl[:, 0].bitcast(F32), ALU.subtract).then_inc(xT_lo, 1)
                if part == 1:
                    pool.tensor_tensor(q_hl[:, 1], full[:, :, :], q_hl[:, 0], ALU.subtract).then_inc(q_lo, 1)
                if part == 3:
                    pool.tensor_tensor(vw[:, g, 1, 1], full[:, :, :].rearrange("p a (b d) -> p (a b) d", d=D), vw[:, g, 1, 0],
                                       ALU.subtract).then_inc(v_lo, 1)

            def rstd_in(k, r):
                pool.wait_ge(dve_ln, gcnt(k, r, 2))
                pool.tensor_tensor(var_e[:, :], mv[:, :, 1], eps_t[:, :], ALU.add).then_inc(var_done, 1)
                pool.wait_ge(var_done, gcnt(k, r))
                if not isint(k) or r >= 4:
                    pool.wait_ge(xn_done, gcnt(k, r - 4))
                pool.tensor_tensor(rstd[:, :], var_e[:, :], mhalf[:, 0:GB], ALU.pow).then_inc(rstd_done, 1)
                pool.wait_ge(rstd_done, gcnt(k, r))
                pool.tensor_tensor(mr[:, :], mv[:, :, 0], rstd[:, :], ALU.mult).then_inc(mr_done, 1)
                pool.wait_ge(mr_done, gcnt(k, r))
                pool.tensor_tensor(shift[:, :], zrow[:, 0:GB], mr[:, :], ALU.subtract).then_inc(shift_done, 1)

            rstd_in(0, 0)
            low_part(0, 0, 0)
            rstd_in(0, 4)
            split_c(0, 0)
            low_part(0, 0, 1)
            pool.wait_ge(init_act, 4)
            pool.tensor_scalar(gbo[:, :], gbo[:, :], gtanh[:, 0:1], None, ALU.mult).then_inc(init_pool, 1)
            pool.wait_ge(init_pool, 3)
            add_xb(0, 0)
            low_part(0, 0, 3)

            def step(k, r):
                if valid(k, r, 2):
                    pool.wait_ge(st2_done, cnt(k, r - 2, 2))
                    pool.tensor_tensor(var_e2[:, :], mv2[:, 1:2], eps_t[:, 0:1], ALU.add).then_inc(var2_done, 1)
                    pool.wait_ge(var2_done, cnt(k, r - 2))
                    if valid(k, r, 3):
                        pool.wait_ge(xn2_done, cnt(k, r - 3))
                    pool.tensor_tensor(rstd2[:, :], var_e2[:, :], mhalf[:, 0:1], ALU.pow).then_inc(rstd2_done, 1)
                    pool.wait_ge(rstd2_done, cnt(k, r - 2))
                    pool.tensor_tensor(mr2[:, :], mv2[:, 0:1], rstd2[:, :], ALU.mult).then_inc(mr2_done, 1)
                    pool.wait_ge(mr2_done, cnt(k, r - 2))
                    pool.tensor_tensor(shift2[:, :], zrow[:, 0:1], mr2[:, :], ALU.subtract).then_inc(shift2_done, 1)
                if has_next(k, r):
                    if r % 4 == 0:
                        split_c(k, r + 4)
                    if r % 4 == 2:
                        if not isint(k) or r >= 4:
                            pool.wait_ge(x1_done, cnt(k, r - 3))
                        add_xb(k, r + 4)
                if r % 4 != 2 and has_next(k, r):
                    low_part(k, r + 4, r % 4)
                if r % 4 == 1 and ahead(k, r):
                    rstd_in(k, r + 7)

            schedule(pool, step)

        @block.scalar
        def _(act):
            def ctx_hi(k, r):
                g = (r // 4) % 2
                act.wait_ge(c_in[g], 16 * (k + r // 8 + 1))
                if not isint(k) or r >= 4:
                    act.wait_ge(v_ps, gcnt(k, r - 4))
                act.activation(c_hl[:, 0], cg[:, g], ACT.Copy).then_inc(c_hi, 1)

            def keep_full(k, r, part):
                if part > 0:
                    act.wait_ge(xT_lo if part == 1 else q_lo, gcnt(k, r))
                elif not isint(k) or r >= 4:
                    act.wait_ge(v_lo, gcnt(k, r - 4))
                if part != 1:
                    i = act.activation(full[:, :, :], ps_g[:, :, :], ACT.Copy)
                else:
                    for c in range(DC):
                        i = act.activation(full[:, c], ps_g[:, c], ACT.Identity, bias=bqk[:, 0, c:c + 1])
                i.then_inc(full_done, 1)

            def prep(k, r, part):
                g = (r // 4) % 2
                if part == 0:
                    act.wait_ge(xT_ps, gcnt(k, r))
                    act.activation(xT_hl[:, 0], ps_g[:, :, :], ACT.Copy).then_inc(xT_hi, 1)
                    keep_full(k, r, 0)
                if part == 1:
                    act.wait_ge(q_ps, gcnt(k, r))
                    if not isint(k) or r >= 4:
                        act.wait_ge(qd_done, gcnt(k, r - 4))
                        act.wait_ge(qd3_done, gcnt(k, r - 4))
                    for c in range(DC):
                        i = act.activation(q_hl[:, 0, c], ps_g[:, c], ACT.Identity, bias=bqk[:, 0, c:c + 1])
                    i.then_inc(q_hi, 1)
                    keep_full(k, r, 1)
                if part == 2:
                    act.wait_ge(k_ps, gcnt(k, r))
                    if k_first(k, r):
                        act.wait_ge(init_dve, 3)
                    for c in range(DC):
                        i = act.activation(kT[:, g, 0, c, :, KPAD:KS], ps_g[:, c].rearrange("p (b s) -> p b s", b=GB),
                                           ACT.Identity, bias=bqk[:, 1, c:c + 1])
                    i.then_inc(k_hi, 1)
                if part == 3:
                    act.wait_ge(v_ps, gcnt(k, r))
                    act.activation(vw[:, g, 1, 0], ps_g[:, :, :].rearrange("p a (b d) -> p (a b) d", d=D), ACT.Copy).then_inc(v_hi, 1)
                    keep_full(k, r, 3)

            def k_first(k, r):
                return isint(k) and k == 0 and r < 8

            def norm_out(k, r):
                g = (r // 4) % 2
                act.wait_ge(shift_done, gcnt(k, r))
                if not isint(k) or r >= 4:
                    act.wait_ge(xT_ps, gcnt(k, r - 4))
                for b in range(GB):
                    i = act.activation(xn[:, b], xg[:, g, b], ACT.Identity, bias=shift[:, b:b + 1], scale=rstd[:, b:b + 1])
                i.then_inc(xn_done, 1)

            def weights(k, r):
                act.wait_ge(s_sub, cnt(k, r))
                win = es[:, r % 2, :, SLOT - KW:SLOT]
                act.activation(win, win, ACT.Exp, scale=HD ** -0.5).then_inc(e_done, 1)

            def norm2(k, r):
                b = r % 2
                act.wait_ge(shift2_done, cnt(k, r))
                if not isint(k) or r >= 2:
                    act.wait_ge(xn2_out[b], 16 * (4 * k + r // 2))
                    act.wait_ge(x2T_ps, cnt(k, r - 2))
                act.activation(xn2[:, b], x1[:, b], ACT.Identity, bias=shift2[:, 0:1], scale=rstd2[:, 0:1]).then_inc(xn2_done, 1)

            def heads_of_q(k, r, heads):
                g = (r // 4) % 2
                act.wait_ge(q_lo, gcnt(k, r))
                for v in heads:
                    i = act.activation(qd[:, g, :, :, :, v].rearrange("p a c n s -> p (a c n) s"), q_hl[:, :, :, :].rearrange("p a c (n s) -> p (a c n) s", s=QB),
                                       ACT.Copy, scale=vmask[:, v:v + 1])
                if 1 in heads:
                    i.then_inc(qd_done, 1)

            norm_out(0, 0)
            act.wait_ge(bv_zero, 1)
            act.wait_ge(bv_in, 32)
            act.activation(bv_hl[0:1, :], bv_raw[0:1, :], ACT.Copy).then_inc(init_act, 1)
            act.activation(bv_hl[32:33, :], bv_raw[32:33, :], ACT.Copy).then_inc(init_act, 1)
            act.wait_ge(weights_in, 16 * 3)
            act.activation(w_hl[:, :, 0], w_raw[:, :], ACT.Copy).then_inc(init_act, 1)
            prep(0, 0, 0)
            ctx_hi(0, 0)
            act.wait_ge(bias_in, 16 * 5)
            act.activation(gtanh[:, :], gates[:, :], ACT.Tanh).then_inc(init_act, 1)
            prep(0, 0, 1)
            prep(0, 0, 2)
            heads_of_q(0, 0, (0, 1))
            prep(0, 0, 3)
            norm_out(0, 4)

            def step(k, r):
                if valid(k, r, 0):
                    for h in range(2):
                        act.wait_ge(pT_ps, cnt(k, r, 2) - 1 + h)
                        act.activation(pT[:, 0, 4 * h:4 * h + 4], ps_p[:, h].rearrange("p (b n) -> p b n", n=P), ACT.Copy).then_inc(pT_hi, 1)
                if valid(k, r, 1):
                    act.wait_ge(oT_ps, cnt(k, r - 1))
                    for half in range(2):
                        i = act.activation(oT[64 * half:64 * half + 64], ps_o[0:64, :].rearrange("p (q v s) -> p v q s", q=4, v=V4)[:, 2 * half:2 * half + 2],
                                           ACT.Copy)
                    i.then_inc(oT_done, 1)
                if valid(k, r, 3):
                    act.wait_ge(x2T_ps, cnt(k, r - 3))
                    act.activation(x2T[:, :, :], ps_m[:, D:2 * D].rearrange("p (c n) -> p c n", c=DC), ACT.Copy).then_inc(x2T_done, 1)
                if r % 4 == 2 and has_next(k, r):
                    heads_of_q(k, r + 4, (0,))
                if valid(k, r, 2):
                    norm2(k, r - 2)
                if r % 4 == 0 and has_next(k, r):
                    ctx_hi(k, r + 4)
                if valid(k, r, -1):
                    weights(k, r + 1)
                if has_next(k, r):
                    prep(k, r + 4, r % 4)
                    if r % 4 == 2:
                        heads_of_q(k, r + 4, (1,))
                    if r % 4 == 3 and ahead(k, r):
                        norm_out(k, r + 5)

            weights(0, 0)
            schedule(act, step)

        @block.tensor
        def _(pe):
            def prep(k, r, part):
                g = (r // 4) % 2
                if part == 0:
                    pe.wait_ge(xn_done, gcnt(k, r))
                    if not isint(k) or r >= 4:
                        pe.wait_ge(v_hi, gcnt(k, r - 4))
                        pe.wait_ge(v_lo, gcnt(k, r - 4))
                    for c in range(DC):
                        for b in range(GB):
                            i = pe.transpose(ps_g[:, c, b * P:(b + 1) * P], xn[:, b, c * P:(c + 1) * P], ident)
                    i.then_inc(xT_ps, 1)
                if part in (1, 2):
                    src = xT_hl if part == 1 else c_hl
                    if part == 1:
                        pe.wait_ge(xT_hi, gcnt(k, r))
                        pe.wait_ge(xT_lo, gcnt(k, r))
                    else:
                        pe.wait_ge(c_hi, gcnt(k, r))
                        pe.wait_ge(c_lo, gcnt(k, r))
                        pe.wait_ge(q_hi, gcnt(k, r))
                        pe.wait_ge(q_lo, gcnt(k, r))
                    for co in range(DC):
                        n = 0
                        for ci in range(DC):
                            for a, b in ((0, 0), (0, 1), (1, 0)):
                                i = pe.matmul(ps_g[:, co], w_hl[:, part - 1, a, ci, co * P:(co + 1) * P], src[:, b, ci],
                                              start=(n == 0), stop=(n == 3 * DC - 1))
                                n += 1
                    i.then_inc(q_ps if part == 1 else k_ps, 1)
                if part == 3:
                    pe.wait_ge(k_hi, gcnt(k, r))
                    pe.wait_ge(k_lo, gcnt(k, r))
                    for b in range(GB):
                        dst = ps_g[:, b // 2, (b % 2) * D:(b % 2 + 1) * D]
                        n = 0
                        pe.matmul(dst, one_r[:, :], bv_hl[:, :], start=True, stop=False)
                        for ci in range(DC):
                            for a, w in ((0, 0), (0, 1), (1, 0)):
                                i = pe.matmul(dst, c_hl[:, a, ci, b * P:(b + 1) * P], w_hl[:, 2, w, ci],
                                              start=False, stop=(n == 3 * DC - 1))
                                n += 1
                    i.then_inc(v_ps, 1)

            pe.wait_ge(const_in, 16)
            prep(0, 0, 0)
            pe.wait_ge(init_act, 3)
            pe.wait_ge(init_dve, 3)
            for part in range(1, 4):
                prep(0, 0, part)
            pe.wait_ge(wo_in, 32)

            def mask_scores(k, r):
                if not isint(k) or r >= 1:
                    pe.wait_ge(s_sub, cnt(k, r - 1))
                for half in range(2):
                    bank = ps_s[:, half].rearrange("p (n s) -> p n s", s=SLOT)
                    pe.matmul(bank[:, :, 0:KW], identb[:, :], bandb[:, :].rearrange("p (n s) -> p n s", s=SLOT)[:, :, 0:KW],
                              start=True, stop=False)

            def scores(k, r):
                g, b = (r // 4) % 2, r % 4
                if b == 0:
                    pe.wait_ge(qd_done, gcnt(k, r))
                    pe.wait_ge(qd3_done, gcnt(k, r))
                    pe.wait_ge(k_hi, gcnt(k, r))
                    pe.wait_ge(k_lo, gcnt(k, r))
                for half in range(2):
                    rows = slice(64 * half, 64 * half + 64)
                    bank = ps_s[:, half].rearrange("p (n s) -> p n s", s=SLOT)
                    for par in range(2):
                        for c in range(DC):
                            for j in range(2):
                                qb = 2 * j + par
                                for a, w in ((0, 0), (0, 1), (1, 0)):
                                    blk = b * 4 + qb
                                    i = pe.matmul(bank[:, par * 4 + c * 2 + j, 0:KW], qd[rows, g, a, c, blk].rearrange("p v s -> p (v s)"),
                                                  kT[rows, g, w, c, b, qb * QB:qb * QB + KW],
                                                  start=False, stop=(par == 1 and c == 1 and j == 1 and a == 1))
                i.then_inc(s_ps, 1)

            def turn_p(k, r):
                pe.wait_ge(e_done, cnt(k, r))
                if not isint(k) or r >= 1:
                    pe.wait_ge(o_done, cnt(k, r - 1))
                for n in range(8):
                    i = pe.transpose(ps_p[:, n // 4, (n % 4) * P:(n % 4 + 1) * P],
                                     es[:, r % 2, 2 * n:2 * n + 2].rearrange("p a s -> p (a s)"), ident)
                    if n % 4 == 3:
                        i.then_inc(pT_ps, 1)

            def turn_o(k, r):
                o = osb[:, :, :].rearrange("p (j a c h) d -> p j a (c h d)", j=2, h=2, a=2)
                for qb in range(4):
                    i = pe.transpose(ps_o[0:64, qb * P:(qb + 1) * P], o[:, qb // 2, qb % 2], ident)
                i.then_inc(oT_ps, 1)

            def heads_out(k, r):
                g, b = (r // 4) % 2, r % 4
                if b == 0:
                    pe.wait_ge(v_hi, gcnt(k, r))
                    pe.wait_ge(v_lo, gcnt(k, r))
                pe.wait_ge(pT_hi, cnt(k, r, 2))
                pe.wait_ge(pT_lo, cnt(k, r, 2))
                for par in (1, 0):
                    if par == 0 and b == 0:
                        pe.wait_ge(v_shift[g], 32 * (k + r // 8 + 1))
                    for half in range(2):
                        for c in range(DC):
                            n = half * 4 + par * 2 + c
                            d0 = c * P + half * 64
                            m = par * 4 + c * 2 + half
                            for a, w in ((0, 0), (0, 1), (1, 0)):
                                for j in range(2):
                                    rows = slice(64 * j, 64 * j + 64)
                                    i = pe.matmul(ps_p[:, j, m * 64:(m + 1) * 64], pT[rows, a, n], vw[rows, g, par, w, b, d0:d0 + 64],
                                                  start=(a == 0 and w == 0), stop=(a == 1))
                i.then_inc(o_ps, 1)

            def project_o(k, r):
                pe.wait_ge(oT_done, cnt(k, r))
                if not isint(k) or r >= 2:
                    pe.wait_ge(x2T_done, cnt(k, r - 2))
                if not isint(k) or r >= 1:
                    pe.wait_ge(x1_done, cnt(k, r - 1))
                if not isint(k) or r >= 3:
                    pe.wait_ge(lg_done, cnt(k, r - 3))
                for v in range(2):
                    i = pe.matmul(ps_m[:, 0:D], oT[:, v].rearrange("p q s -> p (q s)"), wo_sb[:, v], start=(v == 0), stop=(v == 1))
                i.then_inc(y_ps, 1)

            def turn_x2(k, r):
                for c in range(DC):
                    i = pe.transpose(ps_m[:, D + c * P:D + (c + 1) * P], xn2[:, r % 2, c * P:(c + 1) * P], ident)
                i.then_inc(x2T_ps, 1)

            def route(k, r):
                pe.wait_ge(x2T_done, cnt(k, r))
                if not isint(k) or r >= 1:
                    pe.wait_ge(lg_done, cnt(k, r - 1))
                for c in range(DC):
                    i = pe.matmul(ps_m[:, D:D + E], x2T[:, c], wg_sb[:, c], start=(c == 0), stop=(c == DC - 1))
                i.then_inc(lg_ps, 1)

            def step(k, r):
                if valid(k, r, 1):
                    pe.wait_ge(o_done, cnt(k, r - 1))
                    if valid(k, r, 2):
                        pe.wait_ge(oT_done, cnt(k, r - 2))
                if valid(k, r, 0):
                    turn_p(k, r)
                if valid(k, r, 1):
                    turn_o(k, r - 1)
                if valid(k, r, 3):
                    pe.wait_ge(xn2_done, cnt(k, r - 3))
                    if valid(k, r, 2):
                        pe.wait_ge(x1_done, cnt(k, r - 2))
                    if not isint(k) or r >= 4:
                        pe.wait_ge(lg_done, cnt(k, r - 4))
                    turn_x2(k, r - 3)
                if valid(k, r, -1):
                    scores(k, r + 1)
                if has_next(k, r):
                    prep(k, r + 4, r % 4)
                if valid(k, r, 0):
                    heads_out(k, r)
                if valid(k, r, 1):
                    project_o(k, r - 1)
                if valid(k, r, 3):
                    route(k, r - 3)
                if valid(k, r, -2):
                    mask_scores(k, r + 2)

            mask_scores(0, 0)
            scores(0, 0)
            mask_scores(0, 1)
            schedule(pe, step)

        @block.vector
        def _(dve):
            dve.memset(one_r[:, :].bitcast(F32), 1.0)
            dve.memset(bv_hl[:, :].bitcast(F32), 0.0).then_inc(bv_zero, 1)
            def norm_in(k, r, batches):
                g = (r // 4) % 2
                dve.wait_ge(x_in[g], 16 * (k + r // 8 + 1))
                for b in batches:
                    i = dve.bn_stats(stat[:, b], xg[:, g, b])
                if GB - 1 in batches:
                    i.then_inc(dve_ln, 1)

            def aggregate_in(k, r):
                for b in range(GB):
                    i = dve.bn_aggr(mv[:, b], stat[:, b])
                i.then_inc(dve_ln, 1)

            def last_heads_of_q(k, r):
                g = (r // 4) % 2
                dve.wait_ge(q_lo, gcnt(k, r))
                for v in (2, 3):
                    i = dve.tensor_scalar(qd[:, g, :, :, :, v].rearrange("p a c n s -> p (a c n) s"), q_hl[:, :, :, :].rearrange("p a c (n s) -> p (a c n) s", s=QB),
                                          vmask[:, v:v + 1], None, ALU.mult)
                i.then_inc(qd3_done, 1)

            norm_in(0, 0, range(GB))
            dve.wait_ge(dve_ln, 1)
            aggregate_in(0, 0)
            for g in range(2):
                dve.memset(kT[:, g, :, :, :, 0:KPAD].rearrange("p a c b s -> p (a c b) s"), 0.0)
                dve.memset(vw[0:QB, g, 0].rearrange("p a b d -> p (a b d)"), 0.0)
            dve.wait_ge(const_in, 16)
            dve.tensor_copy(identb[:, :], ident)
            dve.tensor_copy(bandb[:, :], cst[:, C_BAND:C_BAND + 512]).then_inc(init_dve, 1)
            dve.wait_ge(init_act, 3)
            dve.tensor_tensor(w_hl[:, :, 1], w_raw[:, :], w_hl[:, :, 0].bitcast(F32), ALU.subtract).then_inc(init_dve, 1)
            dve.tensor_tensor(bv_hl[32:33, :], bv_raw[32:33, :], bv_hl[32:33, :].bitcast(F32), ALU.subtract).then_inc(init_dve, 1)

            def low_k(k, r):
                g = (r // 4) % 2
                dve.wait_ge(k_hi, gcnt(k, r))
                for c in range(DC):
                    i = dve.scalar_tensor_tensor(out=kT[:, g, 1, c, :, KPAD:KS], in0=ps_g[:, c].rearrange("p (b s) -> p b s", b=GB),
                                                 scalar=bqk[:, 1, c:c + 1], in1=kT[:, g, 0, c, :, KPAD:KS],
                                                 op0=ALU.add, op1=ALU.subtract)
                i.then_inc(k_lo, 1)

            dve.wait_ge(dve_ln, 2)
            norm_in(0, 4, range(GB))
            dve.wait_ge(dve_ln, 3)
            dve.wait_ge(shift_done, 1)
            aggregate_in(0, 4)
            last_heads_of_q(0, 0)
            low_k(0, 0)

            def soft(k, r):
                sc = ps_s[:, :, :].rearrange("p a (n s) -> p (a n) s", s=SLOT)[:, :, 0:KW]
                dve.wait_ge(s_ps, cnt(k, r))
                dve.tensor_reduce(mx[:, :], sc, AX, ALU.max).then_inc(mx_done, 1)
                dve.wait_ge(mx_done, cnt(k, r))
                if r >= 2 or not isint(k):
                    dve.wait_ge(pT_ps, cnt(k, r - 2, 2))
                else:
                    dve.wait_ge(init_pool, 2)
                dve.tensor_tensor(es[:, r % 2, :, SLOT - KW:SLOT], sc, mx[:, :].unsqueeze(2).to_broadcast([P, 16, KW]),
                                  ALU.subtract).then_inc(s_sub, 1)

            def low_p(k, r):
                for h in range(2):
                    dve.wait_ge(pT_hi, cnt(k, r, 2) - 1 + h)
                    dve.tensor_tensor(pT[:, 1, 4 * h:4 * h + 4], ps_p[:, h].rearrange("p (b n) -> p b n", n=P), pT[:, 0, 4 * h:4 * h + 4],
                                      ALU.subtract).then_inc(pT_lo, 1)

            def sum_weights(k, r):
                dve.wait_ge(e_done, cnt(k, r))
                dve.tensor_reduce(esum[:, :], es[:, r % 2, :, SLOT - KW:SLOT], AX, ALU.add).then_inc(sum_done, 1)

            def invert_sums(k, r):
                dve.wait_ge(sum_done, cnt(k, r))
                if not isint(k) or r >= 1:
                    dve.wait_ge(o_done, cnt(k, r - 1))
                dve.reciprocal(rinv[:, :, :, :].rearrange("p j x h -> p h x j"), esum[:, :].rearrange("p (h x j) -> p h x j", h=2, j=2)).then_inc(rinv_done, 1)

            def take_o(k, r):
                dve.wait_ge(rinv_done, cnt(k, r))
                dve.wait_ge(o_ps, cnt(k, r))
                if not isint(k) or r >= 1:
                    dve.wait_ge(oT_ps, cnt(k, r - 1))
                o = ps_p[:, :, :].rearrange("p a (n d) -> p (a n) d", d=64)
                for v in range(V4):
                    rows = slice(32 * v, 32 * v + 32)
                    i = dve.tensor_tensor(osb[rows], o[rows, :, v * HD:(v + 1) * HD],
                                          rinv[rows].rearrange("p j x h -> p (j x h)").unsqueeze(2).to_broadcast([32, 16, HD]), ALU.mult)
                i.then_inc(o_done, 1)

            def residual(k, r):
                b, g = r % 2, (r // 4) % 2
                if isint(k) and k == 0 and r == 0:
                    dve.wait_ge(init_act, 4)
                dve.wait_ge(y_ps, cnt(k, r))
                if not isint(k) or r >= 2:
                    dve.wait_ge(lg_ps, cnt(k, r - 2))
                dve.wait_ge(xb_done, gcnt(k, r))
                if not isint(k) or r >= 2:
                    dve.wait_ge(x1_out[b], 16 * (4 * k + r // 2))
                    dve.wait_ge(xn2_done, cnt(k, r - 2))
                dve.scalar_tensor_tensor(out=x1[:, b], in0=ps_m[:, 0:D], scalar=gtanh[:, 0:1], in1=xb[:, g, r % 4],
                                         op0=ALU.mult, op1=ALU.add).then_inc(x1_done, 1)

            def stats2(k, r):
                b = r % 2
                dve.wait_ge(x1_done, cnt(k, r))
                dve.bn_stats(stat2[:, :], x1[:, b]).then_inc(st2_done, 1)

            def aggregate2(k, r):
                dve.bn_aggr(mv2[:, :], stat2[:, :]).then_inc(st2_done, 1)

            def keep_logits(k, r):
                dve.wait_ge(lg_ps, cnt(k, r))
                dve.tensor_copy(logits[:, bass.ds(8 * k + r, 1)].rearrange("p a e -> p (a e)"), ps_m[:, D:D + E]).then_inc(lg_done, 1)

            def step(k, r):
                if valid(k, r, 2):
                    dve.wait_ge(st2_done, cnt(k, r - 2, 2) - 1)
                    if valid(k, r, 3):
                        dve.wait_ge(shift2_done, cnt(k, r - 3))
                if valid(k, r, 0):
                    sum_weights(k, r)
                if valid(k, r, 2):
                    aggregate2(k, r - 2)
                if valid(k, r, 0):
                    low_p(k, r)
                    invert_sums(k, r)
                if valid(k, r, -1):
                    soft(k, r + 1)
                if r % 4 == 1 and ahead(k, r):
                    norm_in(k, r + 7, (2, 3))
                    dve.wait_ge(dve_ln, gcnt(k, r + 7, 2) - 1)
                    dve.wait_ge(shift_done, gcnt(k, r + 3))
                if r % 4 == 2 and has_next(k, r):
                    last_heads_of_q(k, r + 4)
                if valid(k, r, 0):
                    take_o(k, r)
                if r % 4 == 1 and ahead(k, r):
                    aggregate_in(k, r + 7)
                if r % 4 == 2 and has_next(k, r):
                    low_k(k, r + 4)
                if valid(k, r, 1):
                    residual(k, r - 1)
                if valid(k, r, 3):
                    keep_logits(k, r - 3)
                if valid(k, r, 1):
                    stats2(k, r - 1)
                if r % 4 == 0 and ahead(k, r):
                    norm_in(k, r + 8, (0, 1))

            soft(0, 0)
            schedule(dve, step)
            dve.wait_ge(lg_done, B)

        att.close()
        route_and_experts(nc, ctx, cst, gtanh, logits, xn_rows, w1, w2, out)


def route_and_experts(nc, ctx, cst, gtanh, logits, xn_rows, w1, w2, out):
    def sb(name, shape, dt=F32):
        return ctx.enter_context(nc.sbuf_tensor(name, shape, dt))

    def sem(name):
        return ctx.enter_context(nc.semaphore(name))

    ident = cst[:, C_ID:C_ID + P]
    KT = TOPK * B

    idx_all = sb("idx_all", [P, ST + SPARE], I32)
    p_all = sb("p_all", [P, ST + SPARE])
    w_raw = sb("we_raw", [P, 2, DC * F])
    w_hl = sb("we_hl", [P, 2, 2, 2, DC * F], F32R)
    NPIECE = 8
    PIECE = 2 * DC * F // NPIECE

    raw_in, w_hi, w_lo = sem("raw_in"), sem("w_hi"), sem("w_lo")

    w1_e = w1.rearrange("e (c p) f -> e p c f", p=P)
    w2_e = w2.rearrange("e (c p) d -> e p c d", p=P)

    def load_weights(sp, e):
        sp.dma_start(w_raw[:, 0].rearrange("p (c f) -> p c f", c=DC), w1_e[e]).then_inc(raw_in, 16)
        sp.dma_start(w_raw[:, 1].rearrange("p (c d) -> p c d", c=FC), w2_e[e]).then_inc(raw_in, 16)

    def piece(t, n):
        return t.rearrange("p l n -> p (l n)")[:, n * PIECE:(n + 1) * PIECE]

    def split_hi(act, buf, n):
        return act.activation(piece(w_hl[:, buf, 0], n), piece(w_raw[:, :], n), ACT.Copy)

    def split_lo(eng, buf, n):
        return eng.tensor_tensor(piece(w_hl[:, buf, 1], n), piece(w_raw[:, :], n), piece(w_hl[:, buf, 0], n).bitcast(F32), ALU.subtract)

    with ExitStack() as rt:
        def sr(name, shape, dt=F32):
            return rt.enter_context(nc.sbuf_tensor(name, shape, dt))

        oh = sr("oh", [P, TOPK, B, E])
        lg2 = sr("lg2", [P, B, E])
        tmp = sr("tmp", [P, B, E])
        top = sr("top", [P, TOPK, B])
        eid = sr("eid", [P, TOPK, B])
        io8 = sr("io8", [P, E])
        dlt, ex, den, inv = sr("dlt", [P, B]), sr("ex", [P, B]), sr("den", [P, B]), sr("inv", [P, B])
        prob = sr("prob", [P, TOPK, B])
        tot = sr("tot", [P, E])
        tot_rows = sr("tot_rows", [P, E, P])
        own = sr("own", [P, KT, E])
        rank = sr("rank", [P, KT])
        valid_t = sr("valid_t", [P, KT])
        slot_f = sr("slot_f", [P, KT])
        slot_i, hi_i, lo_i = sr("slot_i", [P, KT], I32), sr("hi_i", [P, KT], I32), sr("lo_i", [P, KT], I32)
        hi_f, lo_f = sr("hi_f", [P, KT]), sr("lo_f", [P, KT])
        tokv, pval = sr("tokv", [P, KT]), sr("pval", [P, KT])
        NB = 8
        at_row = sr("at_row", [P, NB, P])
        tok_row, prob_row = sr("tok_row", [P, NB, P]), sr("prob_row", [P, NB, P])
        at_col = sr("at_col", [P, NB, ST])
        ps_pre = rt.enter_context(nc.psum_tensor("ps_pre", [P, 2, 512], F32))
        ps_tot = rt.enter_context(nc.psum_tensor("ps_tot", [P, 512], F32))
        ps_tab = rt.enter_context(nc.psum_tensor("ps_tab", [P, 2, 512], F32))
        seq, exp_done, sums_ps = sem("seq"), sem("exp_done"), sem("sums_ps")
        hot_done, hot_used, table_ps = sem("hot_done"), sem("hot_used"), sem("table_ps")
        dlt_done, tok_done, prob_done = sem("dlt_done"), sem("tok_done"), sem("prob_done")

        rows_ready = []
        tot_ps, tot_done = sem("tot_ps"), sem("tot_done")

        def bc(ap):
            return ap.unsqueeze(2).to_broadcast([P, B, E])

        block = rt.enter_context(nc.Block())

        @block.sync
        def _(sp):
            load_weights(sp, 0)

        @block.gpsimd
        def _(pool):
            for n in range(NPIECE):
                pool.wait_ge(w_hi, n + 1)
                split_lo(pool, 0, n).then_inc(w_lo, 1)

            def token_row(t, j):
                pool.tensor_tensor(tok_row[:, j], at_row[:, j], tokv[:, bass.ds(t, 1)].to_broadcast([P, P]), ALU.mult).then_inc(tok_done, 1)

            for j in range(NB):
                pool.wait_ge(hot_done, j + 1)
                token_row(j, j)
            with pool.Fori(1, KT // NB) as q:
                for j in range(NB):
                    pool.wait_ge(hot_used, NB * q - NB + j + 1)
                    pool.wait_ge(hot_done, NB * q + j + 1)
                    token_row(NB * q + j, j)

        @block.scalar
        def _(act):
            act.wait_ge(dlt_done, 1)
            act.activation(ex[:, :], dlt[:, :], ACT.Exp).then_inc(exp_done, 1)
            act.wait_ge(raw_in, 32)
            for n in range(NPIECE):
                split_hi(act, 0, n).then_inc(w_hi, 1)

            def weight_row(t, j):
                act.activation(prob_row[:, j], at_row[:, j], ACT.Copy, scale=pval[:, bass.ds(t, 1)]).then_inc(prob_done, 1)

            for j in range(NB):
                act.wait_ge(hot_done, j + 1)
                weight_row(j, j)
            with act.Fori(1, KT // NB) as q:
                for j in range(NB):
                    act.wait_ge(hot_used, NB * q - NB + j + 1)
                    act.wait_ge(hot_done, NB * q + j + 1)
                    weight_row(NB * q + j, j)

        @block.vector
        def _(dve):
            count = [0]

            def then(ins):
                count[0] += 1
                ins.then_inc(seq, 1)
                dve.wait_ge(seq, count[0])

            iota = cst[:, C_E8:C_E8 + E].unsqueeze(1).to_broadcast([P, B, E])
            then(dve.tensor_scalar(io8[:, :], cst[:, C_E8:C_E8 + E], float(E), None, ALU.add))
            src = logits[:, :, :]
            for k in range(TOPK):
                then(dve.tensor_reduce(top[:, k], src, AX, ALU.max))
                then(dve.tensor_tensor(tmp[:, :, :], src, bc(top[:, k]), ALU.is_equal))
                then(dve.scalar_tensor_tensor(out=tmp[:, :, :], in0=tmp[:, :, :], scalar=-float(E),
                                              in1=io8[:, :].unsqueeze(1).to_broadcast([P, B, E]), op0=ALU.mult, op1=ALU.add))
                then(dve.tensor_reduce(eid[:, k], tmp[:, :, :], AX, ALU.min))
                then(dve.tensor_tensor(oh[:, k], iota, bc(eid[:, k]), ALU.is_equal))
                rows_ready.append(count[0])
                if k == 0:
                    then(dve.scalar_tensor_tensor(out=lg2[:, :, :], in0=oh[:, 0], scalar=-3.0e38, in1=src, op0=ALU.mult, op1=ALU.add))
                    src = lg2[:, :, :]
            dve.tensor_tensor(dlt[:, :], top[:, 1], top[:, 0], ALU.subtract).then_inc(dlt_done, 1)
            dve.wait_ge(exp_done, 1)
            then(dve.tensor_scalar(den[:, :], ex[:, :], 1.0, None, ALU.add))
            then(dve.reciprocal(inv[:, :], den[:, :]))
            then(dve.tensor_scalar(prob[:, 0], inv[:, :], gtanh[:, 1:2], None, ALU.mult))
            then(dve.tensor_tensor(prob[:, 1], prob[:, 0], ex[:, :], ALU.mult))

            dve.wait_ge(tot_ps, 1)
            then(dve.tensor_copy(tot[:, :], ps_tot[:, 0:E]))
            dve.tensor_copy(tot_rows[:, :, :], tot[:, :].unsqueeze(2).to_broadcast([P, E, P])).then_inc(tot_done, 1)
            dve.wait_ge(sums_ps, 1)
            then(dve.tensor_tensor(own[:, :, :].rearrange("p t e -> p (t e)"), ps_pre[:, :, :].rearrange("p a b -> p (a b)"),
                                   oh[:, :, :, :].rearrange("p k t e -> p (k t e)"), ALU.mult))
            then(dve.tensor_reduce(rank[:, :], own[:, :, :], AX, ALU.add))
            then(dve.tensor_scalar(valid_t[:, :], rank[:, :], float(CAP), None, ALU.is_lt))
            then(dve.scalar_tensor_tensor(out=slot_f[:, :], in0=eid[:, :, :].rearrange("p k t -> p (k t)"), scalar=float(CAP), in1=rank[:, :],
                                          op0=ALU.mult, op1=ALU.add))
            then(dve.tensor_copy(slot_i[:, :], slot_f[:, :]))
            dve.tensor_scalar(hi_i[:, :], slot_i[:, :], 7, None, ALU.arith_shift_right)
            then(dve.tensor_scalar(lo_i[:, :], slot_i[:, :], P - 1, None, ALU.bitwise_and))
            then(dve.tensor_copy(hi_f[:, :], hi_i[:, :]))
            dve.tensor_copy(lo_f[:, :], lo_i[:, :])
            then(dve.scalar_tensor_tensor(out=hi_f[:, :], in0=hi_f[:, :], scalar=1.0, in1=valid_t[:, :], op0=ALU.add, op1=ALU.mult))
            dve.tensor_scalar(hi_f[:, :], hi_f[:, :], -1.0, None, ALU.add)
            dve.tensor_tensor(tokv[:, :], cst[:, C_TOK:C_TOK + KT], rank[:, :], ALU.subtract)
            then(dve.tensor_tensor(pval[:, :], prob[:, :, :].rearrange("p k t -> p (k t)"), valid_t[:, :], ALU.mult))

            def hot(t, j):
                dve.tensor_scalar(at_row[:, j], cst[:, C_I128:C_I128 + P], lo_f[:, bass.ds(t, 1)], None, ALU.is_equal)
                dve.tensor_scalar(at_col[:, j], cst[:, C_I160:C_I160 + ST], hi_f[:, bass.ds(t, 1)], None, ALU.is_equal).then_inc(hot_done, 1)

            for j in range(NB):
                hot(j, j)
            with dve.Fori(1, KT // NB) as q:
                for j in range(NB):
                    dve.wait_ge(hot_used, NB * q - NB + j + 1)
                    hot(NB * q + j, j)
            dve.wait_ge(table_ps, 1)
            dve.tensor_copy(p_all[:, 0:ST], ps_tab[:, 1, 0:ST])
            dve.memset(p_all[:, ST:ST + SPARE], 0.0)
            dve.tensor_tensor(idx_all[:, 0:ST], ps_tab[:, 0, 0:ST], cst[:, C_PB:C_PB + ST], ALU.add)
            dve.tensor_copy(idx_all[:, ST:ST + SPARE], cst[:, C_PB + ST:C_PB + ST + SPARE])

        @block.tensor
        def _(pe):
            for k in range(TOPK):
                pe.wait_ge(seq, rows_ready[k])
                pe.matmul(ps_pre[:, k], cst[:, C_TRI:C_TRI + P], oh[:, k].rearrange("p t e -> p (t e)"), start=True, stop=False)
            for e in range(E):
                i = pe.matmul(ps_tot[:, e:e + 1], oh[:, :, :, e].rearrange("p k t -> p (k t)"), cst[:, C_ONE:C_ONE + 1], start=True, stop=True)
            i.then_inc(tot_ps, 1)
            pe.wait_ge(tot_done, 1)
            for k in range(TOPK):
                for e in range(E):
                    i = pe.matmul(ps_pre[:, k].rearrange("p (t e) -> p t e", e=E)[:, :, e], tot_rows[:, e],
                                  cst[:, C_TRI + k * B:C_TRI + (k + 1) * B], start=False, stop=(e == E - 1))
            i.then_inc(sums_ps, 1)

            def place(n, j, first, last):
                pe.wait_ge(tok_done, n)
                pe.matmul(ps_tab[:, 0, 0:ST], tok_row[:, j], at_col[:, j], start=first, stop=last)
                pe.wait_ge(prob_done, n)
                return pe.matmul(ps_tab[:, 1, 0:ST], prob_row[:, j], at_col[:, j], start=first, stop=last)

            for j in range(NB):
                place(j + 1, j, j == 0, False).then_inc(hot_used, 1)
            with pe.Fori(1, KT // NB - 1) as q:
                for j in range(NB):
                    place(NB * q + j + 1, j, False, False).then_inc(hot_used, 1)
            for j in range(NB):
                i = place(KT - NB + j + 1, j, False, j == NB - 1)
            i.then_inc(table_ps, 1)

    RM = 2 * MTE
    idx_st = sb("idx_st", [P, RM, SUB], I32)
    p_st = sb("p_st", [P, RM, SUB])
    rows_in = sb("rows_in", [P, 2, SUB, D])
    xT = sb("xe_T", [P, 2, 2, DC, MT], F32R)
    r_sb = sb("r_sb", [P, 2, MT])
    sq_sb = sb("sq_sb", [P, 2, MT])
    HR = 4
    h_hl = sb("h_hl", [P, HR, 2, MT], F32R)
    y_sb = sb("y_sb", [P, 2, SUB, D])
    ps_x = ctx.enter_context(nc.psum_tensor("pe_x", [P, DC, 512], F32))
    ps_h = ctx.enter_context(nc.psum_tensor("pe_h", [P, 2, 512], F32))
    ps_y = ctx.enter_context(nc.psum_tensor("pe_y", [P, SUB, 512], F32))

    gate_t = sb("gate_t", [P, 3])
    staged, gate_done = sem("staged"), sem("gate_done")
    g_in = [sem(f"g_in{i}") for i in range(2)]
    xe_ps, xe_hi, xe_lo = sem("xe_ps"), sem("xe_hi"), sem("xe_lo")
    h_ps, relu_done, sq_done, h_hi, h_lo, g2_done = sem("h_ps"), sem("relu_done"), sem("sq_done"), sem("h_hi"), sem("h_lo"), sem("g2_done")
    ye_ps, ye_sb, y_out = sem("ye_ps"), sem("ye_sb"), sem("y_out")

    X0 = 1
    GATES = 5 * RM + 1

    def mc(k, r):
        return k * RM + (r + 1)

    def nch(k, r, f):
        return k * (RM * FC) + (r * FC + f + 1)

    block = ctx.enter_context(nc.Block())

    @block.sync
    def _(sp):
        with sp.Fori(0, E // 2) as k:
            for h in range(2):
                sp.wait_ge(w_hi, (2 * k + h + 1) * NPIECE)
                sp.wait_ge(w_lo, (2 * k + h + 1) * NPIECE)
                load_weights(sp, (2 * k + h + 1) % E)
        sp.wait_ge(raw_in, 32 * (E + 1))

    @block.gpsimd
    def _(pool):
        def gate(k, r, n):
            pool.wait_ge(gate_done, k * GATES + (5 * r + n + 1))
            pool.tensor_tensor(gate_t[:, 0:1], ident[:, 0:1], ident[:, 0:1], ALU.add).then_inc(gate_done, 1)

        def gather(k, r, first=False):
            b = r % 2
            pool.wait_ge(staged, mc(k, r))
            if not first:
                pool.wait_ge(xe_ps, X0 + mc(k, r) - 2)
                gate(k, r - 2, 0)
            for s in range(SUB):
                pool.indirect_dma_start(rows_in[:, b, s], None, xn_rows,
                                        bass.IndirectOffsetOnAxis(ap=idx_st[:, r % RM, s:s + 1], axis=0)).then_inc(g_in[b], 16)

        def scatter(k, r):
            for s in range(SUB):
                pool.wait_ge(ye_sb, X0 + 4 * mc(k, r) - 3 + s)
                if r % MTE == 0 and r > 0 and s == 0:
                    pool.wait_ge(y_out, 64 * mc(k, r - 1))
                gate(k, r, s + 1)
                pool.indirect_dma_start(out, bass.IndirectOffsetOnAxis(ap=idx_st[:, r % RM, s:s + 1], axis=0),
                                        y_sb[:, r % 2, s], None, compute_op=ALU.add).then_inc(y_out, 16)

        pool.tensor_tensor(gate_t[:, 0:1], ident[:, 0:1], ident[:, 0:1], ALU.add).then_inc(gate_done, 1)
        gather(0, 0, True)
        gather(0, 1, True)
        with pool.Fori(0, E // 2) as k:
            for r in range(RM):
                gather(k, r + 2)
                if r % MTE in (1, 2):
                    for n in range(4):
                        m = (r % MTE - 1) * 4 + n
                        pool.wait_ge(w_hi, (2 * k + r // MTE + 1) * NPIECE + m + 1)
                        split_lo(pool, 1 - r // MTE, m).then_inc(w_lo, 1)
                scatter(k, r)
            pool.wait_ge(y_out, 64 * mc(k, RM - 1))
            gate(k, RM, 0)
        pool.wait_ge(y_out, 16 * ST)
        pool.wait_ge(g_in[0], 64 * (NSLOT // MT // 2 + 1))
        pool.wait_ge(g_in[1], 64 * (NSLOT // MT // 2 + 1))

    @block.scalar
    def _(act):
        def x_hi(k, r):
            act.wait_ge(xe_ps, X0 + mc(k, r))
            act.activation(xT[:, r % 2, 0], ps_x[:, :, :], ACT.Copy).then_inc(xe_hi, 1)

        def evac(k, r):
            for s in range(SUB):
                if s < SUB - 1:
                    act.wait_ge(ye_ps, (SUB - 1) * (mc(k, r) - 1) + s + 1)
                else:
                    act.wait_ge(g2_done, nch(k, r, FC - 1))
                act.activation(y_sb[:, r % 2, s], ps_y[:, s, 0:D], ACT.Copy, scale=p_st[:, r, s:s + 1]).then_inc(ye_sb, 1)

        act.activation(gate_t[:, 2:3], ident[:, 0:1], ACT.Copy).then_inc(ye_sb, X0)
        x_hi(0, 0)
        with act.Fori(0, E // 2) as k:
            for r in range(RM):
                for f in range(FC):
                    n = r * FC + f
                    if f == 2 and r > 0:
                        if r > 1:
                            act.wait_ge(y_out, 64 * mc(k, r - 3))
                        else:
                            act.wait_ge(gate_done, X0 + k * GATES)
                        evac(k, r - 1)
                    act.wait_ge(h_ps, nch(k, r, f))
                    if n >= 2:
                        act.wait_ge(sq_done, nch(k, r, f) - 2)
                    act.activation(r_sb[:, f % 2], ps_h[:, f % 2], ACT.Relu).then_inc(relu_done, 1)
                    act.wait_ge(relu_done, nch(k, r, f))
                    if n >= HR:
                        act.wait_ge(g2_done, nch(k, r, f) - HR)
                    act.activation(h_hl[:, f % HR, 0], r_sb[:, f % 2], ACT.Square).then_inc(h_hi, 1)
                    if f == 5:
                        x_hi(k, r + 1)
                    if r % MTE == 1:
                        if f == 0:
                            act.wait_ge(raw_in, 32 * (2 * k + r // MTE + 2))
                        split_hi(act, 1 - r // MTE, f).then_inc(w_hi, 1)
            act.wait_ge(y_out, 64 * mc(k, RM - 3))
            evac(k, RM - 1)

    @block.tensor
    def _(pe):
        def turn(k, r):
            b = r % 2
            pe.wait_ge(g_in[b], 64 * (MTE * k + r // 2 + 1))
            if not (isinstance(k, int) and r == 0):
                pe.wait_ge(xe_lo, mc(k, r) - 1)
            for c in range(DC):
                for s in range(SUB):
                    i = pe.transpose(ps_x[:, c, s * P:(s + 1) * P], rows_in[:, b, s, c * P:(c + 1) * P], ident)
            i.then_inc(xe_ps, 1)

        def first_layer(k, r, f):
            e = r // MTE
            if f == 0:
                pe.wait_ge(xe_hi, mc(k, r))
                pe.wait_ge(xe_lo, mc(k, r))
                if r % MTE == 0:
                    pe.wait_ge(w_hi, (2 * k + e + 1) * NPIECE)
                    pe.wait_ge(w_lo, (2 * k + e + 1) * NPIECE)
            if r * FC + f >= 2:
                pe.wait_ge(relu_done, nch(k, r, f) - 2)
            n = 0
            for c in range(DC):
                for w, a in ((0, 0), (0, 1), (1, 0)):
                    i = pe.matmul(ps_h[:, f % 2], w_hl[:, e, w, 0, c * F + f * P:c * F + (f + 1) * P], xT[:, r % 2, a, c],
                                  start=(n == 0), stop=(n == 3 * DC - 1))
                    n += 1
            i.then_inc(h_ps, 1)

        def second_layer(k, r, f):
            e = r // MTE
            pe.wait_ge(h_hi, nch(k, r, f))
            pe.wait_ge(h_lo, nch(k, r, f))
            for s in range(SUB):
                if f == 0 and r > 0:
                    pe.wait_ge(ye_sb, X0 + 4 * mc(k, r - 1) - 3 + s)
                if f == 0 and r == 0 and s == 0:
                    pe.wait_ge(ye_sb, X0 + k * (4 * RM))
                for a, w in ((0, 0), (0, 1), (1, 0)):
                    i = pe.matmul(ps_y[:, s, 0:D], h_hl[:, f % HR, a, s * P:(s + 1) * P], w_hl[:, e, w, 1, f * D:(f + 1) * D],
                                  start=(f == 0 and a == 0 and w == 0), stop=(f == FC - 1 and a == 1))
                if f == FC - 1 and s < SUB - 1:
                    i.then_inc(ye_ps, 1)
            i.then_inc(g2_done, 1)

        LAG = 2
        pe.transpose(ps_h[:, 0, 0:P], ident, ident).then_inc(xe_ps, X0)
        turn(0, 0)
        with pe.Fori(0, E // 2) as k:
            for r in range(RM):
                for f in range(FC):
                    first_layer(k, r, f)
                    if f == 4:
                        turn(k, r + 1)
                    n = r * FC + f - LAG
                    if n >= 0:
                        second_layer(k, n // FC, n % FC)
            for n in range(RM * FC - LAG, RM * FC):
                second_layer(k, n // FC, n % FC)

    @block.vector
    def _(dve):
        def stage(k, r):
            dve.tensor_copy(p_st[:, r % RM], p_all[:, bass.ds((k * RM + r) * SUB, SUB)])
            dve.tensor_copy(idx_st[:, r % RM], idx_all[:, bass.ds((k * RM + r) * SUB, SUB)]).then_inc(staged, 1)

        def x_lo(k, r):
            dve.wait_ge(xe_hi, mc(k, r))
            dve.tensor_tensor(xT[:, r % 2, 1], ps_x[:, :, :], xT[:, r % 2, 0].bitcast(F32), ALU.subtract).then_inc(xe_lo, 1)

        stage(0, 0)
        stage(0, 1)
        x_lo(0, 0)
        with dve.Fori(0, E // 2) as k:
            for r in range(RM):
                for f in range(FC):
                    n = r * FC + f
                    dve.wait_ge(relu_done, nch(k, r, f))
                    dve.tensor_tensor(sq_sb[:, f % 2], r_sb[:, f % 2], r_sb[:, f % 2], ALU.mult).then_inc(sq_done, 1)
                    dve.wait_ge(sq_done, nch(k, r, f))
                    dve.wait_ge(h_hi, nch(k, r, f))
                    dve.tensor_tensor(h_hl[:, f % HR, 1], sq_sb[:, f % 2], h_hl[:, f % HR, 0].bitcast(F32), ALU.subtract).then_inc(h_lo, 1)
                    if f == 3:
                        stage(k, r + 2)
                    if f == 5:
                        x_lo(k, r + 1)


def pack_constants():
    import numpy as np

    c = np.zeros((P, C_END), np.float32)
    p = np.arange(P)
    c[:, C_ID:C_ID + P] = np.eye(P)
    q = p % QB
    for half_block in range(8):
        par, j = half_block // 4, half_block % 2
        qb = 2 * j + par
        k = np.arange(KW)
        ok = (k[None] >= q[:, None] + 1) & (k[None] <= q[:, None] + W)
        if qb == 0:
            ok &= (k[None] - q[:, None] - 1) <= q[:, None]
        c[:, C_BAND + half_block * SLOT:C_BAND + half_block * SLOT + KW] = np.where(ok, 0.0, NEG)
    c[:, C_VM:C_VM + V4] = ((p[:, None] % 64) // 16) == np.arange(V4)[None]
    c[:, C_TRI:C_TRI + P] = p[:, None] < p[None]
    c[:, C_ONE:C_ONE + P] = 1.0
    c[:, C_I128:C_I128 + P] = p[None]
    c[:, C_I160:C_I160 + ST] = np.arange(ST)[None]
    c[:, C_TOK:C_TOK + TOPK * B] = (np.arange(TOPK * B)[None] % B) * S + p[:, None] - N
    c[:, C_E8:C_E8 + E] = np.arange(E)[None]
    c[:, C_PB:C_END] = N + (np.arange(ST + SPARE)[None] % STE) * P + p[:, None]
    return c


def kernel(x, ctx_1024, g_xattn, g_ffn, L0_xattn_Wq, L0_xattn_bq, L0_xattn_Wk, L0_xattn_bk, L0_xattn_Wv, L0_xattn_bv,
           L0_xattn_Wo, L0_xattn_bo, L0_ffn_w_g, L0_ffn_c_fc, L0_ffn_c_proj):
    import numpy as np
    import concourse.bacc as bacc
    from concourse.bass_utils import run_bass_kernel_spmd

    def lay(a, *steps):
        a = np.asarray(a)
        for kind, how in steps:
            a = a.reshape(how) if kind == "reshape" else a.transpose(how)
        return np.ascontiguousarray(a)

    arrays = {
        "x": lay(x, ("reshape", (N, D))),
        "ctxT": lay(ctx_1024, ("reshape", (N, D)), ("turn", (1, 0))),
        "gx": lay(g_xattn),
        "gf": lay(g_ffn),
        "wqT": lay(L0_xattn_Wq, ("turn", (1, 0))),
        "bq": lay(L0_xattn_bq, ("reshape", (DC, P)), ("turn", (1, 0))),
        "wkT": lay(L0_xattn_Wk, ("turn", (1, 0))),
        "bk": lay(L0_xattn_bk, ("reshape", (DC, P)), ("turn", (1, 0))),
        "wvT": lay(L0_xattn_Wv, ("turn", (1, 0))),
        "bv": lay(L0_xattn_bv),
        "woP": lay(L0_xattn_Wo, ("turn", (1, 0)), ("reshape", (DC, 2, 2, 2, HD, D)), ("turn", (2, 0, 1, 4, 3, 5)), ("reshape", (P, 2, D))),
        "bo": lay(L0_xattn_bo),
        "wgT": lay(L0_ffn_w_g, ("turn", (1, 0))),
        "w1": lay(L0_ffn_c_fc),
        "w2": lay(L0_ffn_c_proj),
        "consts": pack_constants(),
    }
    nc = bacc.Bacc("TRN2", target_bir_lowering=False, num_devices=1)
    args = [nc.dram_tensor(f"in_{n}", a.shape, mybir.dt.from_np(a.dtype), kind="ExternalInput").ap() for n, a in arrays.items()]
    args.append(nc.dram_tensor("out_rows", (N + TRASH, D), F32, kind="ExternalOutput").ap())
    build_kernel(nc, *args)
    r = run_bass_kernel_spmd(nc, [{f"in_{n}": a for n, a in arrays.items()}], core_ids=[0])
    return r.results[0]["out_rows"][:N].reshape(B, S, D)
```
